# Optimizing a Trainium2 kernel written in Bass

```python
import numpy as np
import jax
import jax.numpy as jnp

def _softmax(x, axis=-1):
    return jax.nn.softmax(x, axis=axis)

def _gelu(x):
    return jax.nn.gelu(x, approximate=True)

def _silu(x):
    return jax.nn.silu(x)

def _sigmoid(x):
    return jax.nn.sigmoid(x)

def _layernorm(x, axis=-1, eps=1e-05):
    m = jnp.mean(x, axis=axis, keepdims=True)
    v = jnp.var(x, axis=axis, keepdims=True)
    return (x - m) / jnp.sqrt(v + eps)

def _scatter_add(tgt, idx, src, axis=0):
    return tgt.at[idx].add(src)

def _segment_sum(src, seg, n):
    return jax.ops.segment_sum(src, seg, n)
kernel_name = 'mk_pixart_seq_d4_seqx_r8_1f26ae'

def setup_inputs(seed: int=0):
    np.random.seed(seed)
    _w = jnp.asarray

    def _rec_inputs():
        import jax
        import jax.numpy as jnp
        _rk = jax.random.key(seed)
        x = -0.0003929 + 0.9999 * jax.random.normal(jax.random.fold_in(_rk, 1), (4, 256, 128), jnp.float32)
        _lenS = 256 - jax.random.randint(jax.random.fold_in(_rk, 7), (4,), 0, max(1, 256 // 4) + 1, jnp.int32)
        _lenS2 = 1601 - jax.random.randint(jax.random.fold_in(_rk, 8), (4,), 0, max(1, 1601 // 4) + 1, jnp.int32)
        cond_1024 = 0.00782532 + 1.00527 * jax.random.normal(jax.random.fold_in(_rk, 11), (4, 128), jnp.float32)
        _ctx_1024P = jax.random.normal(jax.random.fold_in(_rk, 12), (4, 16, 128), jnp.float32)
        _ctx_1024c = jax.random.dirichlet(jax.random.fold_in(_rk, 512), 0.3 * jnp.ones((16,), jnp.float32), (4, 1601))
        _ctx_1024t = jnp.einsum('bsk,bkd->bsd', _ctx_1024c, _ctx_1024P)
        _ctx_1024t = _ctx_1024t * jax.lax.rsqrt(jnp.mean(jnp.square(_ctx_1024t)) + 1e-12) * 0.953939
        ctx_1024 = -0.000761806 + 0.999296 * (_ctx_1024t + 0.3 * jax.random.normal(jax.random.fold_in(_rk, 612), (4, 1601, 128), jnp.float32))
        return (x, cond_1024, ctx_1024)
    x, cond_1024, ctx_1024 = _rec_inputs()

    def _L0_xcond_setup():
        import jax, jax.numpy as jnp
        import numpy as np
        H = 128
        RH = 2 * H
        E = 3
        B, T, P = (8, 256, 64)
        LN_EPS = 1e-05

        def _layer_norm(x, gamma, beta):
            mu = jnp.mean(x, axis=-1, keepdims=True)
            var = jnp.mean(jnp.square(x - mu), axis=-1, keepdims=True)
            return (x - mu) * jax.lax.rsqrt(var + LN_EPS) * gamma + beta
        key = jax.random.key(seed)
        ks = jax.random.split(key, 24)
        s = lambda fan_in: 1.0 / np.sqrt(fan_in)
        inp = {'mix_hidden_states': jax.random.normal(ks[0], (B, T, H), jnp.float32), 'global_anchor': jax.random.normal(ks[1], (B, H), jnp.float32), 'prototype_bank': jax.random.normal(ks[2], (B, P, H), jnp.float32), 'ln_gamma': jnp.ones((H,), jnp.float32), 'ln_beta': jnp.zeros((H,), jnp.float32), 'Wq': jax.random.normal(ks[3], (H, H), jnp.float32) * s(H), 'Wk': jax.random.normal(ks[4], (H, H), jnp.float32) * s(H), 'Wv': jax.random.normal(ks[5], (H, H), jnp.float32) * s(H), 'router_W': jax.random.normal(ks[6], (3 * H, E), jnp.float32) * s(3 * H), 'router_b': jnp.zeros((E,), jnp.float32), 'e_w1': jax.random.normal(ks[7], (E, 3 * H, RH), jnp.float32) * s(3 * H), 'e_b1': jnp.zeros((E, RH), jnp.float32), 'e_w2': jax.random.normal(ks[8], (E, RH, H), jnp.float32) * s(RH), 'e_b2': jnp.zeros((E, H), jnp.float32), 'gate_w1': jax.random.normal(ks[9], (3 * H, H), jnp.float32) * s(3 * H), 'gate_b1': jnp.zeros((H,), jnp.float32), 'gate_w2': jax.random.normal(ks[10], (H, H), jnp.float32) * s(H), 'gate_b2': jnp.zeros((H,), jnp.float32), 'out_w': jax.random.normal(ks[11], (H, H), jnp.float32) * s(H), 'out_b': jnp.zeros((H,), jnp.float32)}
        return inp
    _L0_xcond_all = _L0_xcond_setup()
    _L0_xcond_in = {k: v for k, v in _L0_xcond_all.items() if k in ('ln_gamma', 'ln_beta', 'Wq', 'Wk', 'Wv', 'router_W', 'router_b', 'e_w1', 'e_b1', 'e_w2', 'e_b2', 'gate_w1', 'gate_b1', 'gate_w2', 'gate_b2', 'out_w', 'out_b')}
    del _L0_xcond_all

    def _L1_xcond_setup():
        import jax, jax.numpy as jnp
        import numpy as np
        D = 128
        H = 16
        DH = D // H
        DFF = 512
        B = 2
        L = 256
        EPS = 1e-05

        def layer_norm(x, g, b):
            mu = jnp.mean(x, axis=-1, keepdims=True)
            var = jnp.mean(jnp.square(x - mu), axis=-1, keepdims=True)
            return (x - mu) * jax.lax.rsqrt(var + EPS) * g + b

        def ada_ln(x, t_emb, ln_g, ln_b, aff_w, aff_b):
            normed = layer_norm(x, ln_g, ln_b)
            affine = t_emb @ aff_w + aff_b
            gamma, beta = jnp.split(affine, 2, axis=-1)
            return gamma[:, None, :] * normed + beta[:, None, :]

        def mha(q_in, k_in, v_in, qw, qb, kw, kb, vw, vb, ow, ob):
            Bq, Lq, _ = q_in.shape
            Lk = k_in.shape[1]
            Q = (q_in @ qw + qb).reshape(Bq, Lq, H, DH)
            K = (k_in @ kw + kb).reshape(Bq, Lk, H, DH)
            V = (v_in @ vw + vb).reshape(Bq, Lk, H, DH)
            scores = jnp.einsum('bqhd,bkhd->bhqk', Q, K) / np.sqrt(DH).astype(np.float32)
            attn = jax.nn.softmax(scores, axis=-1)
            out = jnp.einsum('bhqk,bkhd->bqhd', attn, V).reshape(Bq, Lq, D)
            return out @ ow + ob
        key = jax.random.key(seed)
        ks = jax.random.split(key, 32)
        s = lambda k, shape, scale=0.02: jax.random.normal(k, shape, dtype=jnp.float32) * scale
        inp = {'x': jax.random.normal(ks[0], (B, L, D), dtype=jnp.float32), 'u': jax.random.normal(ks[1], (B, L, D), dtype=jnp.float32), 't_emb': jax.random.normal(ks[2], (B, D), dtype=jnp.float32), 'ln1_g': jnp.ones((D,), jnp.float32), 'ln1_b': jnp.zeros((D,), jnp.float32), 'aff1_w': s(ks[3], (D, 2 * D)), 'aff1_b': jnp.zeros((2 * D,), jnp.float32), 'ln2_g': jnp.ones((D,), jnp.float32), 'ln2_b': jnp.zeros((D,), jnp.float32), 'aff2_w': s(ks[4], (D, 2 * D)), 'aff2_b': jnp.zeros((2 * D,), jnp.float32), 'sa_qw': s(ks[5], (D, D)), 'sa_qb': jnp.zeros((D,), jnp.float32), 'sa_kw': s(ks[6], (D, D)), 'sa_kb': jnp.zeros((D,), jnp.float32), 'sa_vw': s(ks[7], (D, D)), 'sa_vb': jnp.zeros((D,), jnp.float32), 'sa_ow': s(ks[8], (D, D)), 'sa_ob': jnp.zeros((D,), jnp.float32), 'ca_qw': s(ks[9], (D, D)), 'ca_qb': jnp.zeros((D,), jnp.float32), 'ca_kw': s(ks[10], (D, D)), 'ca_kb': jnp.zeros((D,), jnp.float32), 'ca_vw': s(ks[11], (D, D)), 'ca_vb': jnp.zeros((D,), jnp.float32), 'ca_ow': s(ks[12], (D, D)), 'ca_ob': jnp.zeros((D,), jnp.float32), 'ffn_w1': s(ks[13], (D, DFF)), 'ffn_b1': jnp.zeros((DFF,), jnp.float32), 'ffn_w2': s(ks[14], (DFF, D)), 'ffn_b2': jnp.zeros((D,), jnp.float32)}
        return inp
    _L1_xcond_all = _L1_xcond_setup()
    _L1_xcond_in = {k: v for k, v in _L1_xcond_all.items() if k in ('ln1_g', 'ln1_b', 'aff1_w', 'aff1_b', 'ln2_g', 'ln2_b', 'aff2_w', 'aff2_b', 'sa_qw', 'sa_qb', 'sa_kw', 'sa_kb', 'sa_vw', 'sa_vb', 'sa_ow', 'sa_ob', 'ca_qw', 'ca_qb', 'ca_kw', 'ca_kb', 'ca_vw', 'ca_vb', 'ca_ow', 'ca_ob', 'ffn_w1', 'ffn_b1', 'ffn_w2', 'ffn_b2')}
    del _L1_xcond_all

    def _L2_xcond_setup():
        import jax, jax.numpy as jnp
        import numpy as np
        import math
        D_MODEL = 128
        N_HEADS = 16
        HEAD_DIM = D_MODEL // N_HEADS
        D_FF = 512
        EPS = 1e-05
        ROPE_BASE = 10000.0

        def _rope(t):
            L, Dh = (t.shape[1], t.shape[-1])
            half = Dh // 2
            inv_freq = 1.0 / ROPE_BASE ** (jnp.arange(half, dtype=t.dtype) / half)
            ang = jnp.arange(L, dtype=t.dtype)[:, None] * inv_freq[None, :]
            cos = jnp.cos(ang)[None, :, None, :]
            sin = jnp.sin(ang)[None, :, None, :]
            t1, t2 = (t[..., :half], t[..., half:])
            return jnp.concatenate([t1 * cos - t2 * sin, t2 * cos + t1 * sin], axis=-1)

        def _adaln(x, emb, w, b):
            e = emb[:, 0, :]
            gb = e @ w.T + b
            gamma, beta = jnp.split(gb, 2, axis=-1)
            mu = x.mean(-1, keepdims=True)
            var = x.var(-1, keepdims=True)
            xn = (x - mu) * jax.lax.rsqrt(var + EPS)
            return xn * (1.0 + gamma[:, None, :]) + beta[:, None, :]

        def _attn(q, k, v):
            scale = 1.0 / math.sqrt(HEAD_DIM)
            scores = jnp.einsum('bqhd,bkhd->bhqk', q, k) * scale
            w = jax.nn.softmax(scores, axis=-1)
            out = jnp.einsum('bhqk,bkhd->bqhd', w, v)
            B, Lq = (out.shape[0], out.shape[1])
            return out.reshape(B, Lq, D_MODEL)
        key = jax.random.key(seed)
        ks = jax.random.split(key, 24)
        s = 0.02
        inp = {'x': jax.random.normal(ks[0], (2, 256, D_MODEL), jnp.float32), 'noise_emb': jax.random.normal(ks[1], (2, 1, D_MODEL), jnp.float32), 'context': jax.random.normal(ks[2], (2, 128, D_MODEL), jnp.float32), 'ln1_w': jax.random.normal(ks[3], (2 * D_MODEL, D_MODEL), jnp.float32) * s, 'ln1_b': jax.random.normal(ks[4], (2 * D_MODEL,), jnp.float32) * s, 'ln2_w': jax.random.normal(ks[5], (2 * D_MODEL, D_MODEL), jnp.float32) * s, 'ln2_b': jax.random.normal(ks[6], (2 * D_MODEL,), jnp.float32) * s, 'ln3_w': jax.random.normal(ks[7], (2 * D_MODEL, D_MODEL), jnp.float32) * s, 'ln3_b': jax.random.normal(ks[8], (2 * D_MODEL,), jnp.float32) * s, 'qkv_w': jax.random.normal(ks[9], (3 * D_MODEL, D_MODEL), jnp.float32) * s, 'sa_out_w': jax.random.normal(ks[10], (D_MODEL, D_MODEL), jnp.float32) * s, 'q_w': jax.random.normal(ks[11], (D_MODEL, D_MODEL), jnp.float32) * s, 'k_w': jax.random.normal(ks[12], (D_MODEL, D_MODEL), jnp.float32) * s, 'v_w': jax.random.normal(ks[13], (D_MODEL, D_MODEL), jnp.float32) * s, 'ca_out_w': jax.random.normal(ks[14], (D_MODEL, D_MODEL), jnp.float32) * s, 'ffn_w1': jax.random.normal(ks[15], (D_FF, D_MODEL), jnp.float32) * s, 'ffn_b1': jax.random.normal(ks[16], (D_FF,), jnp.float32) * s, 'ffn_w2': jax.random.normal(ks[17], (D_MODEL, D_FF), jnp.float32) * s, 'ffn_b2': jax.random.normal(ks[18], (D_MODEL,), jnp.float32) * s}
        return inp
    _L2_xcond_all = _L2_xcond_setup()
    _L2_xcond_in = {k: v for k, v in _L2_xcond_all.items() if k in ('ln1_w', 'ln1_b', 'ln2_w', 'ln2_b', 'ln3_w', 'ln3_b', 'qkv_w', 'sa_out_w', 'q_w', 'k_w', 'v_w', 'ca_out_w', 'ffn_w1', 'ffn_b1', 'ffn_w2', 'ffn_b2')}
    del _L2_xcond_all

    def _L3_xcond_setup():
        import jax, jax.numpy as jnp
        import numpy as np
        C = 128
        H = 16
        D = C // H
        WIN = 64
        SHIFT = 32
        TOPK = 16
        HID = 512
        EPS = 1e-06

        def _ln(x):
            x32 = x.astype(jnp.float32)
            m = x32.mean(-1, keepdims=True)
            v = jnp.mean((x32 - m) ** 2, axis=-1, keepdims=True)
            return ((x32 - m) * jax.lax.rsqrt(v + EPS)).astype(x.dtype)

        def _self_attn(h, w_qkv, b_qkv, w_so, b_so):
            B, L, _ = h.shape
            qkv = h @ w_qkv + b_qkv
            qkv = jnp.roll(qkv, -SHIFT, axis=1)
            nw = L // WIN
            qkv = qkv.reshape(B, nw, WIN, 3, H, D)
            q, k, v = (qkv[:, :, :, 0], qkv[:, :, :, 1], qkv[:, :, :, 2])
            scores = jnp.einsum('bnqhd,bnkhd->bnhqk', q, k) / jnp.sqrt(jnp.float32(D)).astype(h.dtype)
            attn = jax.nn.softmax(scores, axis=-1)
            o = jnp.einsum('bnhqk,bnkhd->bnqhd', attn, v).reshape(B, L, C)
            o = jnp.roll(o, SHIFT, axis=1)
            return o @ w_so + b_so

        def _topk_cross_attn(h, ctx, w_q, b_q, w_kv, b_kv, w_co, b_co):
            B, L, _ = h.shape
            Lc = ctx.shape[1]
            q = (h @ w_q + b_q).reshape(B, L, H, D)
            kv = (ctx @ w_kv + b_kv).reshape(B, Lc, 2, H, D)
            k, v = (kv[:, :, 0], kv[:, :, 1])
            scores = jnp.einsum('bqhd,bkhd->bhqk', q, k) / jnp.sqrt(jnp.float32(D)).astype(h.dtype)
            top_s, top_i = jax.lax.top_k(scores, TOPK)
            attn = jax.nn.softmax(top_s, axis=-1)
            v_bh = jnp.transpose(v, (0, 2, 1, 3))
            vg = jnp.take_along_axis(v_bh[:, :, None, :, :], top_i[..., None], axis=3)
            o = jnp.einsum('bhqk,bhqkd->bqhd', attn, vg).reshape(B, L, C)
            return o @ w_co + b_co

        def _swiglu(h, w_m1, b_m1, w_m2, b_m2):
            u = h @ w_m1 + b_m1
            a, b = (u[..., :HID], u[..., HID:])
            return jax.nn.silu(a) * b @ w_m2 + b_m2
        key = jax.random.key(seed)
        ks = jax.random.split(key, 24)
        s = 0.02
        inp = {'x': jax.random.normal(ks[0], (2, 512, C), jnp.float32), 'mod': jax.random.normal(ks[1], (2, C), jnp.float32), 'context': jax.random.normal(ks[2], (2, 128, C), jnp.float32), 'w_ada': jax.random.normal(ks[3], (C, 9 * C), jnp.float32) * s, 'b_ada': jnp.zeros((9 * C,), jnp.float32), 'w_qkv': jax.random.normal(ks[4], (C, 3 * C), jnp.float32) * s, 'b_qkv': jnp.zeros((3 * C,), jnp.float32), 'w_so': jax.random.normal(ks[5], (C, C), jnp.float32) * s, 'b_so': jnp.zeros((C,), jnp.float32), 'w_q': jax.random.normal(ks[6], (C, C), jnp.float32) * s, 'b_q': jnp.zeros((C,), jnp.float32), 'w_kv': jax.random.normal(ks[7], (C, 2 * C), jnp.float32) * s, 'b_kv': jnp.zeros((2 * C,), jnp.float32), 'w_co': jax.random.normal(ks[8], (C, C), jnp.float32) * s, 'b_co': jnp.zeros((C,), jnp.float32), 'w_m1': jax.random.normal(ks[9], (C, 2 * HID), jnp.float32) * s, 'b_m1': jnp.zeros((2 * HID,), jnp.float32), 'w_m2': jax.random.normal(ks[10], (HID, C), jnp.float32) * s, 'b_m2': jnp.zeros((C,), jnp.float32)}
        return inp
    _L3_xcond_all = _L3_xcond_setup()
    _L3_xcond_in = {k: v for k, v in _L3_xcond_all.items() if k in ('w_ada', 'b_ada', 'w_qkv', 'b_qkv', 'w_so', 'b_so', 'w_q', 'b_q', 'w_kv', 'b_kv', 'w_co', 'b_co', 'w_m1', 'b_m1', 'w_m2', 'b_m2')}
    del _L3_xcond_all
    return {'x': x, 'cond_1024': cond_1024, 'ctx_1024': ctx_1024, 'L0_xcond_ln_gamma': _L0_xcond_in['ln_gamma'], 'L0_xcond_ln_beta': _L0_xcond_in['ln_beta'], 'L0_xcond_Wq': _L0_xcond_in['Wq'], 'L0_xcond_Wk': _L0_xcond_in['Wk'], 'L0_xcond_Wv': _L0_xcond_in['Wv'], 'L0_xcond_router_W': _L0_xcond_in['router_W'], 'L0_xcond_router_b': _L0_xcond_in['router_b'], 'L0_xcond_e_w1': _L0_xcond_in['e_w1'], 'L0_xcond_e_b1': _L0_xcond_in['e_b1'], 'L0_xcond_e_w2': _L0_xcond_in['e_w2'], 'L0_xcond_e_b2': _L0_xcond_in['e_b2'], 'L0_xcond_gate_w1': _L0_xcond_in['gate_w1'], 'L0_xcond_gate_b1': _L0_xcond_in['gate_b1'], 'L0_xcond_gate_w2': _L0_xcond_in['gate_w2'], 'L0_xcond_gate_b2': _L0_xcond_in['gate_b2'], 'L0_xcond_out_w': _L0_xcond_in['out_w'], 'L0_xcond_out_b': _L0_xcond_in['out_b'], 'L1_xcond_ln1_g': _L1_xcond_in['ln1_g'], 'L1_xcond_ln1_b': _L1_xcond_in['ln1_b'], 'L1_xcond_aff1_w': _L1_xcond_in['aff1_w'], 'L1_xcond_aff1_b': _L1_xcond_in['aff1_b'], 'L1_xcond_ln2_g': _L1_xcond_in['ln2_g'], 'L1_xcond_ln2_b': _L1_xcond_in['ln2_b'], 'L1_xcond_aff2_w': _L1_xcond_in['aff2_w'], 'L1_xcond_aff2_b': _L1_xcond_in['aff2_b'], 'L1_xcond_sa_qw': _L1_xcond_in['sa_qw'], 'L1_xcond_sa_qb': _L1_xcond_in['sa_qb'], 'L1_xcond_sa_kw': _L1_xcond_in['sa_kw'], 'L1_xcond_sa_kb': _L1_xcond_in['sa_kb'], 'L1_xcond_sa_vw': _L1_xcond_in['sa_vw'], 'L1_xcond_sa_vb': _L1_xcond_in['sa_vb'], 'L1_xcond_sa_ow': _L1_xcond_in['sa_ow'], 'L1_xcond_sa_ob': _L1_xcond_in['sa_ob'], 'L1_xcond_ca_qw': _L1_xcond_in['ca_qw'], 'L1_xcond_ca_qb': _L1_xcond_in['ca_qb'], 'L1_xcond_ca_kw': _L1_xcond_in['ca_kw'], 'L1_xcond_ca_kb': _L1_xcond_in['ca_kb'], 'L1_xcond_ca_vw': _L1_xcond_in['ca_vw'], 'L1_xcond_ca_vb': _L1_xcond_in['ca_vb'], 'L1_xcond_ca_ow': _L1_xcond_in['ca_ow'], 'L1_xcond_ca_ob': _L1_xcond_in['ca_ob'], 'L1_xcond_ffn_w1': _L1_xcond_in['ffn_w1'], 'L1_xcond_ffn_b1': _L1_xcond_in['ffn_b1'], 'L1_xcond_ffn_w2': _L1_xcond_in['ffn_w2'], 'L1_xcond_ffn_b2': _L1_xcond_in['ffn_b2'], 'L2_xcond_ln1_w': _L2_xcond_in['ln1_w'], 'L2_xcond_ln1_b': _L2_xcond_in['ln1_b'], 'L2_xcond_ln2_w': _L2_xcond_in['ln2_w'], 'L2_xcond_ln2_b': _L2_xcond_in['ln2_b'], 'L2_xcond_ln3_w': _L2_xcond_in['ln3_w'], 'L2_xcond_ln3_b': _L2_xcond_in['ln3_b'], 'L2_xcond_qkv_w': _L2_xcond_in['qkv_w'], 'L2_xcond_sa_out_w': _L2_xcond_in['sa_out_w'], 'L2_xcond_q_w': _L2_xcond_in['q_w'], 'L2_xcond_k_w': _L2_xcond_in['k_w'], 'L2_xcond_v_w': _L2_xcond_in['v_w'], 'L2_xcond_ca_out_w': _L2_xcond_in['ca_out_w'], 'L2_xcond_ffn_w1': _L2_xcond_in['ffn_w1'], 'L2_xcond_ffn_b1': _L2_xcond_in['ffn_b1'], 'L2_xcond_ffn_w2': _L2_xcond_in['ffn_w2'], 'L2_xcond_ffn_b2': _L2_xcond_in['ffn_b2'], 'L3_xcond_w_ada': _L3_xcond_in['w_ada'], 'L3_xcond_b_ada': _L3_xcond_in['b_ada'], 'L3_xcond_w_qkv': _L3_xcond_in['w_qkv'], 'L3_xcond_b_qkv': _L3_xcond_in['b_qkv'], 'L3_xcond_w_so': _L3_xcond_in['w_so'], 'L3_xcond_b_so': _L3_xcond_in['b_so'], 'L3_xcond_w_q': _L3_xcond_in['w_q'], 'L3_xcond_b_q': _L3_xcond_in['b_q'], 'L3_xcond_w_kv': _L3_xcond_in['w_kv'], 'L3_xcond_b_kv': _L3_xcond_in['b_kv'], 'L3_xcond_w_co': _L3_xcond_in['w_co'], 'L3_xcond_b_co': _L3_xcond_in['b_co'], 'L3_xcond_w_m1': _L3_xcond_in['w_m1'], 'L3_xcond_b_m1': _L3_xcond_in['b_m1'], 'L3_xcond_w_m2': _L3_xcond_in['w_m2'], 'L3_xcond_b_m2': _L3_xcond_in['b_m2']}

def reference(x, cond_1024, ctx_1024, L0_xcond_ln_gamma, L0_xcond_ln_beta, L0_xcond_Wq, L0_xcond_Wk, L0_xcond_Wv, L0_xcond_router_W, L0_xcond_router_b, L0_xcond_e_w1, L0_xcond_e_b1, L0_xcond_e_w2, L0_xcond_e_b2, L0_xcond_gate_w1, L0_xcond_gate_b1, L0_xcond_gate_w2, L0_xcond_gate_b2, L0_xcond_out_w, L0_xcond_out_b, L1_xcond_ln1_g, L1_xcond_ln1_b, L1_xcond_aff1_w, L1_xcond_aff1_b, L1_xcond_ln2_g, L1_xcond_ln2_b, L1_xcond_aff2_w, L1_xcond_aff2_b, L1_xcond_sa_qw, L1_xcond_sa_qb, L1_xcond_sa_kw, L1_xcond_sa_kb, L1_xcond_sa_vw, L1_xcond_sa_vb, L1_xcond_sa_ow, L1_xcond_sa_ob, L1_xcond_ca_qw, L1_xcond_ca_qb, L1_xcond_ca_kw, L1_xcond_ca_kb, L1_xcond_ca_vw, L1_xcond_ca_vb, L1_xcond_ca_ow, L1_xcond_ca_ob, L1_xcond_ffn_w1, L1_xcond_ffn_b1, L1_xcond_ffn_w2, L1_xcond_ffn_b2, L2_xcond_ln1_w, L2_xcond_ln1_b, L2_xcond_ln2_w, L2_xcond_ln2_b, L2_xcond_ln3_w, L2_xcond_ln3_b, L2_xcond_qkv_w, L2_xcond_sa_out_w, L2_xcond_q_w, L2_xcond_k_w, L2_xcond_v_w, L2_xcond_ca_out_w, L2_xcond_ffn_w1, L2_xcond_ffn_b1, L2_xcond_ffn_w2, L2_xcond_ffn_b2, L3_xcond_w_ada, L3_xcond_b_ada, L3_xcond_w_qkv, L3_xcond_b_qkv, L3_xcond_w_so, L3_xcond_b_so, L3_xcond_w_q, L3_xcond_b_q, L3_xcond_w_kv, L3_xcond_b_kv, L3_xcond_w_co, L3_xcond_b_co, L3_xcond_w_m1, L3_xcond_b_m1, L3_xcond_w_m2, L3_xcond_b_m2):
    import jax
    import jax.numpy as jnp

    def _L0_xcond_ref(mix_hidden_states, global_anchor, prototype_bank, ln_gamma, ln_beta, Wq, Wk, Wv, router_W, router_b, e_w1, e_b1, e_w2, e_b2, gate_w1, gate_b1, gate_w2, gate_b2, out_w, out_b):
        import jax, jax.numpy as jnp
        import numpy as np
        H = 128
        RH = 2 * H
        E = 3
        B, T, P = (8, 256, 64)
        LN_EPS = 1e-05

        def _layer_norm(x, gamma, beta):
            mu = jnp.mean(x, axis=-1, keepdims=True)
            var = jnp.mean(jnp.square(x - mu), axis=-1, keepdims=True)
            return (x - mu) * jax.lax.rsqrt(var + LN_EPS) * gamma + beta
        x = mix_hidden_states
        nx = _layer_norm(x, ln_gamma, ln_beta)
        q = nx @ Wq
        k = prototype_bank @ Wk
        v = prototype_bank @ Wv
        scores = jnp.einsum('bth,bph->btp', q, k) * H ** (-0.5)
        weights = jax.nn.softmax(scores, axis=-1)
        evidence = jnp.einsum('btp,bph->bth', weights, v)
        anchor = jnp.broadcast_to(global_anchor[:, None, :], nx.shape)
        combined = jnp.concatenate([nx, evidence, anchor], axis=-1)
        router_logits = combined @ router_W + router_b
        router_probs = jax.nn.softmax(router_logits, axis=-1)
        h = jax.nn.silu(jnp.einsum('btc,ecr->bter', combined, e_w1) + e_b1)
        expert_out = jnp.einsum('bter,erh->bteh', h, e_w2) + e_b2
        routed = jnp.sum(expert_out * router_probs[..., None], axis=-2)
        g = jax.nn.sigmoid(jax.nn.silu(combined @ gate_w1 + gate_b1) @ gate_w2 + gate_b2)
        refined_delta = g * (routed @ out_w + out_b)
        return x + refined_delta

    def _L1_xcond_ref(x, u, t_emb, ln1_g, ln1_b, aff1_w, aff1_b, ln2_g, ln2_b, aff2_w, aff2_b, sa_qw, sa_qb, sa_kw, sa_kb, sa_vw, sa_vb, sa_ow, sa_ob, ca_qw, ca_qb, ca_kw, ca_kb, ca_vw, ca_vb, ca_ow, ca_ob, ffn_w1, ffn_b1, ffn_w2, ffn_b2):
        import jax, jax.numpy as jnp
        import numpy as np
        D = 128
        H = 16
        DH = D // H
        DFF = 512
        B = 2
        L = 256
        EPS = 1e-05

        def layer_norm(x, g, b):
            mu = jnp.mean(x, axis=-1, keepdims=True)
            var = jnp.mean(jnp.square(x - mu), axis=-1, keepdims=True)
            return (x - mu) * jax.lax.rsqrt(var + EPS) * g + b

        def ada_ln(x, t_emb, ln_g, ln_b, aff_w, aff_b):
            normed = layer_norm(x, ln_g, ln_b)
            affine = t_emb @ aff_w + aff_b
            gamma, beta = jnp.split(affine, 2, axis=-1)
            return gamma[:, None, :] * normed + beta[:, None, :]

        def mha(q_in, k_in, v_in, qw, qb, kw, kb, vw, vb, ow, ob):
            Bq, Lq, _ = q_in.shape
            Lk = k_in.shape[1]
            Q = (q_in @ qw + qb).reshape(Bq, Lq, H, DH)
            K = (k_in @ kw + kb).reshape(Bq, Lk, H, DH)
            V = (v_in @ vw + vb).reshape(Bq, Lk, H, DH)
            scores = jnp.einsum('bqhd,bkhd->bhqk', Q, K) / np.sqrt(DH).astype(np.float32)
            attn = jax.nn.softmax(scores, axis=-1)
            out = jnp.einsum('bhqk,bkhd->bqhd', attn, V).reshape(Bq, Lq, D)
            return out @ ow + ob
        xn = ada_ln(x, t_emb, ln1_g, ln1_b, aff1_w, aff1_b)
        x = x + mha(xn, xn, xn, sa_qw, sa_qb, sa_kw, sa_kb, sa_vw, sa_vb, sa_ow, sa_ob)
        x = x + mha(x, u, u, ca_qw, ca_qb, ca_kw, ca_kb, ca_vw, ca_vb, ca_ow, ca_ob)
        xn = ada_ln(x, t_emb, ln2_g, ln2_b, aff2_w, aff2_b)
        h = jax.nn.gelu(xn @ ffn_w1 + ffn_b1, approximate=False)
        x = x + (h @ ffn_w2 + ffn_b2)
        return x

    def _L2_xcond_ref(x, noise_emb, context, ln1_w, ln1_b, ln2_w, ln2_b, ln3_w, ln3_b, qkv_w, sa_out_w, q_w, k_w, v_w, ca_out_w, ffn_w1, ffn_b1, ffn_w2, ffn_b2):
        import jax, jax.numpy as jnp
        import numpy as np
        import math
        D_MODEL = 128
        N_HEADS = 16
        HEAD_DIM = D_MODEL // N_HEADS
        D_FF = 512
        EPS = 1e-05
        ROPE_BASE = 10000.0

        def _rope(t):
            L, Dh = (t.shape[1], t.shape[-1])
            half = Dh // 2
            inv_freq = 1.0 / ROPE_BASE ** (jnp.arange(half, dtype=t.dtype) / half)
            ang = jnp.arange(L, dtype=t.dtype)[:, None] * inv_freq[None, :]
            cos = jnp.cos(ang)[None, :, None, :]
            sin = jnp.sin(ang)[None, :, None, :]
            t1, t2 = (t[..., :half], t[..., half:])
            return jnp.concatenate([t1 * cos - t2 * sin, t2 * cos + t1 * sin], axis=-1)

        def _adaln(x, emb, w, b):
            e = emb[:, 0, :]
            gb = e @ w.T + b
            gamma, beta = jnp.split(gb, 2, axis=-1)
            mu = x.mean(-1, keepdims=True)
            var = x.var(-1, keepdims=True)
            xn = (x - mu) * jax.lax.rsqrt(var + EPS)
            return xn * (1.0 + gamma[:, None, :]) + beta[:, None, :]

        def _attn(q, k, v):
            scale = 1.0 / math.sqrt(HEAD_DIM)
            scores = jnp.einsum('bqhd,bkhd->bhqk', q, k) * scale
            w = jax.nn.softmax(scores, axis=-1)
            out = jnp.einsum('bhqk,bkhd->bqhd', w, v)
            B, Lq = (out.shape[0], out.shape[1])
            return out.reshape(B, Lq, D_MODEL)
        B, L, D = x.shape
        L_ctx = context.shape[1]
        res = x
        xn = _adaln(x, noise_emb, ln1_w, ln1_b)
        qkv = xn @ qkv_w.T
        q, k, v = jnp.split(qkv, 3, axis=-1)
        q = _rope(q.reshape(B, L, N_HEADS, HEAD_DIM))
        k = _rope(k.reshape(B, L, N_HEADS, HEAD_DIM))
        v = v.reshape(B, L, N_HEADS, HEAD_DIM)
        sa = _attn(q, k, v) @ sa_out_w.T
        x = res + sa
        res = x
        xn = _adaln(x, noise_emb, ln2_w, ln2_b)
        q = _rope((xn @ q_w.T).reshape(B, L, N_HEADS, HEAD_DIM))
        k = _rope((context @ k_w.T).reshape(B, L_ctx, N_HEADS, HEAD_DIM))
        v = (context @ v_w.T).reshape(B, L_ctx, N_HEADS, HEAD_DIM)
        ca = _attn(q, k, v) @ ca_out_w.T
        x = res + ca
        res = x
        xn = _adaln(x, noise_emb, ln3_w, ln3_b)
        h = jax.nn.gelu(xn @ ffn_w1.T + ffn_b1, approximate=False)
        x = res + (h @ ffn_w2.T + ffn_b2)
        return x

    def _L3_xcond_ref(x, mod, context, w_ada, b_ada, w_qkv, b_qkv, w_so, b_so, w_q, b_q, w_kv, b_kv, w_co, b_co, w_m1, b_m1, w_m2, b_m2):
        import jax, jax.numpy as jnp
        import numpy as np
        C = 128
        H = 16
        D = C // H
        WIN = 64
        SHIFT = 32
        TOPK = 16
        HID = 512
        EPS = 1e-06

        def _ln(x):
            x32 = x.astype(jnp.float32)
            m = x32.mean(-1, keepdims=True)
            v = jnp.mean((x32 - m) ** 2, axis=-1, keepdims=True)
            return ((x32 - m) * jax.lax.rsqrt(v + EPS)).astype(x.dtype)

        def _self_attn(h, w_qkv, b_qkv, w_so, b_so):
            B, L, _ = h.shape
            qkv = h @ w_qkv + b_qkv
            qkv = jnp.roll(qkv, -SHIFT, axis=1)
            nw = L // WIN
            qkv = qkv.reshape(B, nw, WIN, 3, H, D)
            q, k, v = (qkv[:, :, :, 0], qkv[:, :, :, 1], qkv[:, :, :, 2])
            scores = jnp.einsum('bnqhd,bnkhd->bnhqk', q, k) / jnp.sqrt(jnp.float32(D)).astype(h.dtype)
            attn = jax.nn.softmax(scores, axis=-1)
            o = jnp.einsum('bnhqk,bnkhd->bnqhd', attn, v).reshape(B, L, C)
            o = jnp.roll(o, SHIFT, axis=1)
            return o @ w_so + b_so

        def _topk_cross_attn(h, ctx, w_q, b_q, w_kv, b_kv, w_co, b_co):
            B, L, _ = h.shape
            Lc = ctx.shape[1]
            q = (h @ w_q + b_q).reshape(B, L, H, D)
            kv = (ctx @ w_kv + b_kv).reshape(B, Lc, 2, H, D)
            k, v = (kv[:, :, 0], kv[:, :, 1])
            scores = jnp.einsum('bqhd,bkhd->bhqk', q, k) / jnp.sqrt(jnp.float32(D)).astype(h.dtype)
            top_s, top_i = jax.lax.top_k(scores, TOPK)
            attn = jax.nn.softmax(top_s, axis=-1)
            v_bh = jnp.transpose(v, (0, 2, 1, 3))
            vg = jnp.take_along_axis(v_bh[:, :, None, :, :], top_i[..., None], axis=3)
            o = jnp.einsum('bhqk,bhqkd->bqhd', attn, vg).reshape(B, L, C)
            return o @ w_co + b_co

        def _swiglu(h, w_m1, b_m1, w_m2, b_m2):
            u = h @ w_m1 + b_m1
            a, b = (u[..., :HID], u[..., HID:])
            return jax.nn.silu(a) * b @ w_m2 + b_m2
        m = jax.nn.silu(mod) @ w_ada + b_ada
        sh_msa, sc_msa, g_msa, sh_mca, sc_mca, g_mca, sh_mlp, sc_mlp, g_mlp = [m[:, i * C:(i + 1) * C][:, None, :] for i in range(9)]
        h = _ln(x) * (1 + sc_msa) + sh_msa
        h = _self_attn(h, w_qkv, b_qkv, w_so, b_so)
        x = x + h * g_msa
        h = _ln(x) * (1 + sc_mca) + sh_mca
        h = _topk_cross_attn(h, context, w_q, b_q, w_kv, b_kv, w_co, b_co)
        x = x + h * g_mca
        h = _ln(x) * (1 + sc_mlp) + sh_mlp
        h = _swiglu(h, w_m1, b_m1, w_m2, b_m2)
        x = x + h * g_mlp
        return x
    x = _L0_xcond_ref(x, cond_1024, ctx_1024, L0_xcond_ln_gamma, L0_xcond_ln_beta, L0_xcond_Wq, L0_xcond_Wk, L0_xcond_Wv, L0_xcond_router_W, L0_xcond_router_b, L0_xcond_e_w1, L0_xcond_e_b1, L0_xcond_e_w2, L0_xcond_e_b2, L0_xcond_gate_w1, L0_xcond_gate_b1, L0_xcond_gate_w2, L0_xcond_gate_b2, L0_xcond_out_w, L0_xcond_out_b)
    x = _L1_xcond_ref(x, ctx_1024, cond_1024, L1_xcond_ln1_g, L1_xcond_ln1_b, L1_xcond_aff1_w, L1_xcond_aff1_b, L1_xcond_ln2_g, L1_xcond_ln2_b, L1_xcond_aff2_w, L1_xcond_aff2_b, L1_xcond_sa_qw, L1_xcond_sa_qb, L1_xcond_sa_kw, L1_xcond_sa_kb, L1_xcond_sa_vw, L1_xcond_sa_vb, L1_xcond_sa_ow, L1_xcond_sa_ob, L1_xcond_ca_qw, L1_xcond_ca_qb, L1_xcond_ca_kw, L1_xcond_ca_kb, L1_xcond_ca_vw, L1_xcond_ca_vb, L1_xcond_ca_ow, L1_xcond_ca_ob, L1_xcond_ffn_w1, L1_xcond_ffn_b1, L1_xcond_ffn_w2, L1_xcond_ffn_b2)
    x = _L2_xcond_ref(x, cond_1024[:, None, :], ctx_1024, L2_xcond_ln1_w, L2_xcond_ln1_b, L2_xcond_ln2_w, L2_xcond_ln2_b, L2_xcond_ln3_w, L2_xcond_ln3_b, L2_xcond_qkv_w, L2_xcond_sa_out_w, L2_xcond_q_w, L2_xcond_k_w, L2_xcond_v_w, L2_xcond_ca_out_w, L2_xcond_ffn_w1, L2_xcond_ffn_b1, L2_xcond_ffn_w2, L2_xcond_ffn_b2)
    x = _L3_xcond_ref(x, cond_1024, ctx_1024, L3_xcond_w_ada, L3_xcond_b_ada, L3_xcond_w_qkv, L3_xcond_b_qkv, L3_xcond_w_so, L3_xcond_b_so, L3_xcond_w_q, L3_xcond_b_q, L3_xcond_w_kv, L3_xcond_b_kv, L3_xcond_w_co, L3_xcond_b_co, L3_xcond_w_m1, L3_xcond_b_m1, L3_xcond_w_m2, L3_xcond_b_m2)
    return x

_drawn_inputs = setup_inputs


def setup_inputs(seed=0):
    import zlib

    import numpy as np

    out = dict(_drawn_inputs(seed))
    spreads = {'L0_xcond_ln_gamma': (1.0, 0.2),
     'L0_xcond_ln_beta': (0.0, 0.627),
     'L0_xcond_router_b': (0.0, 0.8),
     'L0_xcond_e_b1': (0.0, 0.366),
     'L0_xcond_e_b2': (0.0, 0.1),
     'L0_xcond_gate_b1': (0.0, 0.8),
     'L0_xcond_gate_b2': (0.0, 0.8),
     'L0_xcond_out_b': (0.0, 0.1),
     'L1_xcond_ln1_g': (1.0, 0.6),
     'L1_xcond_ln1_b': (0.0, 0.8),
     'L1_xcond_aff1_b': (0.0, 0.8),
     'L1_xcond_ln2_g': (1.0, 0.6),
     'L1_xcond_ln2_b': (0.0, 0.8),
     'L1_xcond_aff2_b': (0.0, 0.8),
     'L1_xcond_sa_qb': (0.0, 0.8),
     'L1_xcond_sa_kb': (0.0, 2.0),
     'L1_xcond_sa_vb': (0.0, 0.391),
     'L1_xcond_sa_ob': (0.0, 0.1),
     'L1_xcond_ca_qb': (0.0, 2.0),
     'L1_xcond_ca_kb': (0.0, 2.0),
     'L1_xcond_ca_vb': (0.0, 0.387),
     'L1_xcond_ca_ob': (0.0, 0.1),
     'L1_xcond_ffn_b1': (0.0, 0.354),
     'L1_xcond_ffn_b2': (0.0, 0.1),
     'L3_xcond_b_ada': (0.0, 0.447),
     'L3_xcond_b_qkv': (0.0, 0.8),
     'L3_xcond_b_so': (0.0, 0.397),
     'L3_xcond_b_q': (0.0, 0.8),
     'L3_xcond_b_kv': (0.0, 0.8),
     'L3_xcond_b_co': (0.0, 0.442),
     'L3_xcond_b_m1': (0.0, 0.8),
     'L3_xcond_b_m2': (0.0, 0.449)}
    factors = {'L1_xcond_aff1_w': 5.284,
     'L1_xcond_aff2_w': 3.313,
     'L1_xcond_sa_qw': 8.0,
     'L1_xcond_sa_kw': 8.0,
     'L1_xcond_sa_vw': 4.618,
     'L1_xcond_ca_qw': 8.0,
     'L1_xcond_ca_kw': 8.0,
     'L1_xcond_ffn_w1': 2.975,
     'L2_xcond_ln1_w': 4.535,
     'L2_xcond_ln1_b': 8.0,
     'L2_xcond_ln2_w': 8.0,
     'L2_xcond_ln2_b': 36.239,
     'L2_xcond_ln3_w': 3.229,
     'L2_xcond_ln3_b': 38.277,
     'L2_xcond_qkv_w': 3.318,
     'L2_xcond_sa_out_w': 3.301,
     'L2_xcond_q_w': 8.0,
     'L2_xcond_k_w': 8.0,
     'L2_xcond_ffn_b1': 8.0,
     'L2_xcond_ffn_b2': 3.095,
     'L3_xcond_w_qkv': 8.0,
     'L3_xcond_w_so': 8.0,
     'L3_xcond_w_q': 8.0,
     'L3_xcond_w_kv': 7.074,
     'L3_xcond_w_co': 6.489,
     'L3_xcond_w_m1': 8.0,
     'L3_xcond_w_m2': 8.0}
    for name, (base, spread) in spreads.items():
        noise = np.random.default_rng([zlib.crc32(name.encode()), seed]).standard_normal(out[name].shape)
        drawn = base * np.exp(spread * noise) if base else spread * noise
        out[name] = jnp.asarray(drawn.astype(out[name].dtype))
    for name, factor in factors.items():
        out[name] = (out[name] * factor).astype(out[name].dtype)
    return out
```

```python
import numpy as np

import concourse.bass as bass
from concourse import mybir

F32 = mybir.dt.float32
BF16 = mybir.dt.bfloat16
ALU = mybir.AluOpType
ACT = mybir.ActivationFunctionType
AX = mybir.AxisListType

P = 128
D = 128
HEADS, HD = 16, 8
GROUP = 4
GROUPS = HEADS // GROUP
BATCHES, TOK, CTX = 4, 256, 1601
PAIR = 2
N = PAIR * TOK
CTX_TILES = -(-CTX // P)
SHIFT, WIN = 32, 64
TOPK = 16
SPLIT_ROWS = 9 * HD
SCORE_ROWS = 96
MAX_ROWS = 99
VH = HD + 1
VROW = HEADS * VH + 24
SCALE = float(np.float32(1.0) / np.sqrt(np.float32(HD)))
LOW = -3.0e38

PERM = np.array([(GROUP * g + j) * HD + d for g in range(GROUPS) for d in range(HD) for j in range(GROUP)])
ROT = np.array([(GROUP * g + j) * HD + (d + HD // 2) % HD
                for g in range(GROUPS) for d in range(HD) for j in range(GROUP)])


class Columns:

    def __init__(self):
        self.at, self.n = {}, 0

    def add(self, name, width):
        self.at[name] = (self.n, width)
        self.n += width


def weight_plan():
    w = Columns()
    for name, width in [
        ("0q", D), ("0k", D), ("0v", D), ("0out", D), ("0gate2", D), ("0gate1", 2 * D), ("0e1", 3 * 2 * 2 * D),
        ("0e2", 3 * 2 * D), ("0router", 2 * 3),
        ("1sq", D), ("1sk", D), ("1sv", D), ("1so", D), ("1cq", D), ("1ck", D), ("1cv", D), ("1co", D),
        ("1f1", 4 * D), ("1f2", 4 * D),
        ("2sq", D), ("2sqr", D), ("2sk", D), ("2skr", D), ("2sv", D), ("2so", D),
        ("2cq", D), ("2cqr", D), ("2ck", D), ("2ckr", D), ("2cv", D), ("2co", D), ("2f1", 4 * D), ("2f2", 4 * D),
        ("3sq", D), ("3sk", D), ("3sv", D), ("3so", D), ("3cq", D), ("3ck", D), ("3cv", D), ("3co", D),
        ("3f1", 8 * D), ("3f2", 4 * D),
    ]:
        w.add(name, width)
    return w


def modulation_plan():
    m = Columns()
    for name, chunks in [("0gate1", 1), ("0e1", 6), ("1aff1", 2), ("1aff2", 2), ("2ln1", 2), ("2ln2", 2),
                         ("2ln3", 2), ("3ada", 9)]:
        m.add(name, chunks)
    m.add("0router", 3)
    return m


def bias_plan():
    b = Columns()
    b.add("mod", modulation_plan().n)
    for name, n in [("0g", 1), ("0b", 1), ("0gate2", 1), ("0out", 1), ("0e2", 3),
                    ("1g1", 1), ("1b1", 1), ("1g2", 1), ("1b2", 1), ("1sq", 1), ("1sk", 1), ("1sv", 1), ("1so", 1),
                    ("1cq", 1), ("1ck", 1), ("1cv", 1), ("1co", 1), ("1f1", 4), ("1f2", 1), ("2f1", 4), ("2f2", 1),
                    ("3sq", 1), ("3sk", 1), ("3sv", 1), ("3so", 1), ("3cq", 1), ("3ck", 1), ("3cv", 1), ("3co", 1),
                    ("3f1", 8), ("3f2", 1)]:
        b.add(name, n)
    return b


class SemaphoreSet:

    def __init__(self, nc, name, n):
        self.sems = [nc.alloc_semaphore(f"{name}{i}") for i in range(n)]
        self.range = range(self.sems[0].num, self.sems[0].num + n)
        self.used = 0

    def take(self, n=1):
        got = self.sems[self.used:self.used + n]
        self.used += n
        return got[0] if n == 1 else got


def build_program(nc, x_in, ctx_in, cond_in, weights_in, modw_in, bias_in, const_in, rope_in, out, last_stage=99):
    W, M, B = weight_plan(), modulation_plan(), bias_plan()

    def sb(name, shape, dt=F32):
        return nc.alloc_sbuf_tensor(name, shape, dt)

    weights = sb("weights", [P, W.n])
    biases = sb("biases", [P, B.n])
    ident = sb("ident", [P, P])
    ident16 = sb("ident16", [P, P], BF16)
    mean_w = sb("mean_w", [P, P])
    ones = sb("ones", [P, P])
    rope_tok = sb("rope_tok", [P, 2, TOK])
    mod_all = sb("mod_all", [P, BATCHES, M.n])
    x = sb("x", [P, N])
    normed = sb("normed", [P, N])
    tmp_a = sb("tmp_a", [P, N])
    tmp_b = sb("tmp_b", [P, N])
    ctx = sb("ctx", [P, PAIR, CTX])
    mod = sb("mod", [P, PAIR, M.n])
    lnw = sb("lnw", [P, 2, PAIR, 2])
    q_parts = sb("q_parts", [P, 3, N], BF16)
    k_parts = sb("k_parts", [P, 3, PAIR * CTX], BF16)
    q_stack = sb("q_stack", [P, HEADS, N], BF16)
    k_stack = [sb(f"k_stack{i}", [P, GROUP, CTX], BF16) for i in range(2)]
    values = sb("values", [P, PAIR * CTX_TILES, VROW])
    attn_tok = sb("attn_tok", [P, PAIR, 2, D])
    attn = sb("attn", [P, N])
    heads_out = sb("heads_out", [P, TOK])
    maxima = sb("maxima", [P, 2, 16])
    max8 = sb("max8", [P, 8])
    neg_f = sb("neg_f", [P, 8])
    neg_parts = sb("neg_parts", [P, 2, 3, GROUP], BF16)
    neg_rows = [sb(f"neg_rows{i}", [24, P], BF16) for i in range(2)]
    sums_inv = sb("sums_inv", [P, 2, GROUP])
    shared = sb("shared", [P, 9920])

    def part(first, shape):
        size = int(np.prod(shape))
        v = shared[:, first:first + size]
        if len(shape) == 2:
            v = v.rearrange("p (a b) -> p a b", a=shape[0])
        if len(shape) == 3:
            v = v.rearrange("p (a b c) -> p a b c", a=shape[0], b=shape[1])
        return v

    modw = shared[:, 0:M.at["0router"][0] * D + 3]
    condT = shared[:, 29 * D:29 * D + BATCHES]
    condS = shared[:, 29 * D + BATCHES:29 * D + 2 * BATCHES]
    split_f = part(0, [2, 512])
    split_t = part(1024, [2, 512])
    split_r = part(2048, [2, 512])
    rope_ctx = part(3072, [2, CTX])
    probs = [part(1024 * i, [GROUP, TOK]) for i in range(3)]
    hidden = part(0, [7, N])
    router_p = part(7 * N, [3, N])
    k0 = part(0, [PAIR, CTX])
    v0 = part(PAIR * CTX, [PAIR * CTX_TILES, D])
    probs0 = [part(PAIR * CTX + PAIR * CTX_TILES * D + TOK * i, [TOK]) for i in range(3)]
    neg_row0 = shared[0:1, 7424:7424 + N]
    untaken = [part(CTX * i, [CTX]) for i in range(2)]
    weight_e = [part(CTX * (2 + i), [CTX]) for i in range(2)]
    probs_t = [part(4 * CTX + CTX_TILES * P * i, [CTX_TILES, P]) for i in range(2)]
    best = sb("best", [P, 2, TOPK + 1])

    ps = nc.alloc_psum_tensor("ps", [P, 8, 512], F32)

    def w(name, i=0, n=1):
        at, width = W.at[name]
        return weights[:, at + i * D:at + (i + n) * D]

    def bias(name, i=0):
        at = B.at[name][0] + i
        return biases[:, at:at + 1]

    def modc(name, b, i=0):
        at = M.at[name][0] + i
        return mod[:, b, at:at + 1]

    sets = [SemaphoreSet(nc, "even", 28), SemaphoreSet(nc, "odd", 28)]
    turn = [0]

    def semaphores():
        s, other = sets[turn[0] % 2], sets[1 - turn[0] % 2]
        turn[0] += 1
        s.used = 0
        return s, other.range

    def tile_rows(t):
        return min(P, CTX - t * P)

    def load_constants():
        s, other = semaphores()
        loaded, cond_loaded, filled, silu_done, mod_ready, biased, step = [s.take() for _ in range(7)]
        with nc.Block() as block:
            @block.sync
            def _(sp):
                sp.sem_clear(other)
                sp.dma_start(modw, modw_in).then_inc(cond_loaded, 16)
                sp.dma_start(condT, cond_in).then_inc(cond_loaded, 16)
                sp.dma_start(biases[:, :], bias_in).then_inc(cond_loaded, 16)
                sp.dma_start(ident[:, :], const_in[:, 0:P]).then_inc(loaded, 16)
                sp.dma_start(rope_tok[:, :, :], const_in[:, P:P + 2 * TOK].rearrange("p (a b) -> p a b", a=2)) \
                    .then_inc(loaded, 16)
                sp.dma_start(weights[:, :], weights_in).then_inc(loaded, 16)
                sp.wait_ge(loaded, 48)

            @block.gpsimd
            def _(pool):
                pool.memset(q_stack[:, :, :], 0.0).then_inc(filled, 1)
                for i in range(2):
                    pool.wait_ge(filled, 2 * i + 1)
                    pool.memset(k_stack[i][0:96, :, :], 0.0).then_inc(filled, 1)
                    pool.wait_ge(filled, 2 * i + 2)
                    pool.memset(k_stack[i][96:128, :, :], 1.0).then_inc(filled, 1)
                pool.wait_ge(filled, 5)
                pool.memset(values[:, :, :], 1.0).then_inc(filled, 1)

            @block.vector
            def _(dve):
                dve.memset(mean_w[:, :], 1.0 / D)
                dve.memset(ones[:, :], 1.0)
                dve.wait_ge(loaded, 48)
                dve.tensor_copy(ident16[:, :], ident[:, :])
                dve.wait_ge(mod_ready, 1)
                dve.wait_ge(cond_loaded, 48)
                m_view = ps[:, 0, 0:M.n * BATCHES].rearrange("p (c b) -> p b c", b=BATCHES)
                b_view = biases[:, 0:M.n].unsqueeze(1).to_broadcast([P, BATCHES, M.n])
                dve.tensor_tensor(mod_all[:, :, :], m_view, b_view, ALU.add).then_inc(biased, 1)

            @block.scalar
            def _(act):
                act.wait_ge(cond_loaded, 48)
                act.activation(condS, condT, ACT.Silu).then_inc(silu_done, 1)

            @block.tensor
            def _(pe):
                pe.wait_ge(cond_loaded, 48)
                pe.wait_ge(silu_done, 1)
                for c in range(M.n):
                    router = c >= M.at["0router"][0]
                    ada = M.at["3ada"][0] <= c < M.at["3ada"][0] + 9
                    if router:
                        e = M.at["0router"][0] * D + c - M.at["0router"][0]
                        lhs = modw[:, e:e + 1].to_broadcast([P, P])
                    else:
                        lhs = modw[:, c * D:(c + 1) * D]
                    mm = pe.matmul(ps[:, 0, c * BATCHES:(c + 1) * BATCHES], lhs, condS if ada else condT,
                                   start=True, stop=True)
                mm.then_inc(mod_ready, 1)

    def load_pair(pair):
        s, other = semaphores()
        loaded, copied, made = s.take(), s.take(), s.take()
        with nc.Block() as block:
            @block.sync
            def _(sp):
                sp.sem_clear(other)
                sp.dma_start(x[:, :], x_in[bass.ds(pair, 1), :, :].rearrange("a p n -> (a p) n")).then_inc(loaded, 16)
                sp.dma_start(ctx[:, :, :].rearrange("p b n -> p (b n)"),
                             ctx_in[bass.ds(pair, 1), :, :].rearrange("a p n -> (a p) n")).then_inc(loaded, 16)
                sp.wait_ge(loaded, 32)

            @block.vector
            def _(dve):
                src = mod_all[:, :, :].rearrange("p b m -> p (b m)")
                dve.tensor_copy(mod[:, :, :].rearrange("p b m -> p (b m)"),
                                src[:, bass.ds(pair * (PAIR * M.n), PAIR * M.n)]).then_inc(copied, 1)
                dve.wait_ge(copied, 1)
                for i, name in enumerate(("1aff1", "1aff2")):
                    for b in range(PAIR):
                        dve.tensor_scalar(lnw[:, i, b, 0:1], modc(name, b, 0), bias(f"1g{i + 1}"), None, ALU.mult)
                        dve.scalar_tensor_tensor(lnw[:, i, b, 1:2], modc(name, b, 0), bias(f"1b{i + 1}"),
                                                 modc(name, b, 1), ALU.mult, ALU.add)
                at2 = M.at["2ln1"][0]
                g2 = mod[:, :, at2:at2 + 6:2]
                dve.tensor_scalar(g2, g2, 1.0, None, ALU.add)
                at3 = M.at["3ada"][0]
                g3 = mod[:, :, at3 + 1:at3 + 9:3]
                dve.tensor_scalar(g3, g3, 1.0, None, ALU.add).then_inc(made, 1)

    def even_out(first_turn):
        if (turn[0] - first_turn) % 2:
            s, other = semaphores()
            with nc.Block() as block:
                @block.sync
                def _(sp):
                    sp.sem_clear(other)

    def store_pair(pair):
        s, other = semaphores()
        stored = s.take()
        with nc.Block() as block:
            @block.sync
            def _(sp):
                sp.sem_clear(other)
                sp.dma_start(out[bass.ds(pair, 1), :, :].rearrange("a p n -> (a p) n"), x[:, :]).then_inc(stored, 16)
                sp.wait_ge(stored, 16)

    def layer_norm(eps, affine):
        s, other = semaphores()
        mean_ready, centred, squared, var_ready, root_done, inverted, scaled, done = [s.take() for _ in range(8)]
        mean, var = ps[:, 0, :], ps[:, 1, :]
        with nc.Block() as block:
            @block.sync
            def _(sp):
                sp.sem_clear(other)

            @block.tensor
            def _(pe):
                pe.matmul(mean, mean_w[:, :], x[:, :], start=True, stop=True).then_inc(mean_ready, 1)
                pe.wait_ge(squared, 1)
                pe.matmul(var, mean_w[:, :], tmp_b[:, :], start=True, stop=True).then_inc(var_ready, 1)

            @block.scalar
            def _(act):
                act.wait_ge(centred, 1)
                act.activation(tmp_b[:, :], tmp_a[:, :], ACT.Square).then_inc(squared, 1)
                act.wait_ge(var_ready, 1)
                act.wait_ge(mean_ready, 1)
                act.activation(tmp_b[:, :], var, ACT.Sqrt, bias=eps_col[eps]).then_inc(root_done, 1)

            @block.vector
            def _(dve):
                dve.wait_ge(mean_ready, 1)
                dve.tensor_tensor(tmp_a[:, :], x[:, :], mean, ALU.subtract).then_inc(centred, 1)
                dve.wait_ge(root_done, 1)
                dve.reciprocal(tmp_b[:, :], tmp_b[:, :]).then_inc(inverted, 1)
                dve.wait_ge(inverted, 1)
                dve.wait_ge(centred, 1)
                dve.tensor_tensor(tmp_a[:, :], tmp_a[:, :], tmp_b[:, :], ALU.mult).then_inc(scaled, 1)
                dve.wait_ge(scaled, 1)
                for b in range(PAIR):
                    scale, shift = affine(b)
                    dve.tensor_scalar(normed[:, b * TOK:(b + 1) * TOK], tmp_a[:, b * TOK:(b + 1) * TOK],
                                      scale, shift, ALU.mult, ALU.add).then_inc(done, 1)

    def dense(jobs):
        s, other = semaphores()
        product_ready, emptied = s.take(), s.take()
        with nc.Block() as block:
            @block.sync
            def _(sp):
                sp.sem_clear(other)

            @block.tensor
            def _(pe):
                for i, (terms, dst, func, b) in enumerate(jobs):
                    if i >= 4:
                        pe.wait_ge(emptied, i - 3)
                    for k, (lhs, rhs) in enumerate(terms):
                        mm = pe.matmul(ps[:, i % 4, 0:dst.shape[1]], lhs, rhs, start=(k == 0), stop=(k == len(terms) - 1))
                    mm.then_inc(product_ready, 1)

            @block.scalar
            def _(act):
                for i, (terms, dst, func, b) in enumerate(jobs):
                    act.wait_ge(product_ready, i + 1)
                    act.activation(dst, ps[:, i % 4, 0:dst.shape[1]], func, bias=b).then_inc(emptied, 1)

    def add_to_x(terms, b_col, gate=None):
        s, other = semaphores()
        product_ready, gated, added = s.take(), s.take(), s.take()
        with nc.Block() as block:
            @block.sync
            def _(sp):
                sp.sem_clear(other)

            @block.tensor
            def _(pe):
                for k, (lhs, rhs) in enumerate(terms):
                    mm = pe.matmul(ps[:, 0, :], lhs, rhs, start=(k == 0), stop=(k == len(terms) - 1))
                mm.then_inc(product_ready, 1)

            @block.vector
            def _(dve):
                dve.wait_ge(product_ready, 1)
                if gate is None:
                    if b_col is None:
                        dve.tensor_tensor(x[:, :], ps[:, 0, :], x[:, :], ALU.add).then_inc(added, 1)
                    else:
                        dve.scalar_tensor_tensor(x[:, :], ps[:, 0, :], b_col, x[:, :], ALU.add, ALU.add) \
                            .then_inc(added, 1)
                    return
                for b in range(PAIR):
                    cols = slice(b * TOK, (b + 1) * TOK)
                    dve.tensor_scalar(tmp_a[:, cols], ps[:, 0, cols], b_col, gate(b), ALU.add, ALU.mult) \
                        .then_inc(gated, 1)
                dve.wait_ge(gated, PAIR)
                dve.tensor_tensor(x[:, :], tmp_a[:, :], x[:, :], ALU.add).then_inc(added, 1)

    def project_heads(split_jobs, value_jobs, w_v, rope=False, load_rope=False):
        s, other = semaphores()
        (proj_ready, exact_done, hi_done, rest_done, mid_done, lo_done, turned, rotated, v_ready, v_done,
         rope_loaded) = [s.take() for _ in range(11)]
        n_split = len(split_jobs)
        with nc.Block() as block:
            @block.sync
            def _(sp):
                sp.sem_clear(other)
                if load_rope:
                    sp.dma_start(rope_ctx, rope_in.rearrange("p (a b) -> p a b", a=2)).then_inc(rope_loaded, 16)
                    sp.wait_ge(rope_loaded, 16)

            @block.tensor
            def _(pe):
                v_next = 0

                def value_group(i):
                    if i >= 2:
                        pe.wait_ge(v_done, i - 1)
                    for k, (src, tile) in enumerate(value_jobs[i]):
                        mm = pe.matmul(ps[0:src.shape[1], 4 + i % 2, k * D:(k + 1) * D], src, w_v, start=True, stop=True)
                    mm.then_inc(v_ready, 1)

                for c, (src, wk, wr, b, cos, sin, dst) in enumerate(split_jobs):
                    n = src.shape[1]
                    if c >= 2:
                        if rope:
                            pe.wait_ge(turned, 2 * (c - 1))
                        else:
                            pe.wait_ge(exact_done, 2 * (c - 1))
                    mm = pe.matmul(ps[:, c % 2, 0:n], wk, src, start=True, stop=True)
                    if rope:
                        mm = pe.matmul(ps[:, 2 + c % 2, 0:n], wr, src, start=True, stop=True)
                    mm.then_inc(proj_ready, 1)
                    if v_next < len(value_jobs):
                        value_group(v_next)
                        v_next += 1
                while v_next < len(value_jobs):
                    value_group(v_next)
                    v_next += 1

            @block.scalar
            def _(act):
                v_next = 0

                def value_group(i):
                    act.wait_ge(v_ready, i + 1)
                    jobs = value_jobs[i]
                    rows, tile = jobs[0][0].shape[1], jobs[0][1]
                    dst = values[0:rows, tile:tile + len(jobs), 0:HEADS * VH] \
                        .rearrange("p t (h c) -> p t h c", c=VH)[:, :, :, 0:HD]
                    src = ps[0:rows, 4 + i % 2, 0:len(jobs) * D].rearrange("p (t h d) -> p t h d", t=len(jobs), d=HD)
                    for k in range(len(jobs)):
                        mm = act.copy(dst[:, k], src[:, k])
                    mm.then_inc(v_done, 1)

                for c, (src, wk, wr, b, cos, sin, dst) in enumerate(split_jobs):
                    n = src.shape[1]
                    if rope:
                        act.wait_ge(rotated, c + 1)
                        act.copy(dst[:, 0, :], split_f[:, c % 2, 0:n]).then_inc(hi_done, 1)
                    else:
                        act.wait_ge(proj_ready, c + 1)
                        if c >= 2:
                            act.wait_ge(rest_done, c - 1)
                        act.activation(split_f[:, c % 2, 0:n], ps[:, c % 2, 0:n], ACT.Identity, bias=b) \
                            .then_inc(exact_done, 1)
                        act.activation(dst[:, 0, :], ps[:, c % 2, 0:n], ACT.Identity, bias=b).then_inc(exact_done, 1)
                    if v_next < len(value_jobs):
                        value_group(v_next)
                        v_next += 1
                while v_next < len(value_jobs):
                    value_group(v_next)
                    v_next += 1

            @block.vector
            def _(dve):
                if load_rope:
                    dve.wait_ge(rope_loaded, 16)
                for c, (src, wk, wr, b, cos, sin, dst) in enumerate(split_jobs):
                    n = src.shape[1]
                    exact, turn_, rest = split_f[:, c % 2, 0:n], split_t[:, c % 2, 0:n], split_r[:, c % 2, 0:n]
                    if rope:
                        dve.wait_ge(proj_ready, c + 1)
                        dve.tensor_tensor(exact, ps[:, c % 2, 0:n], cos, ALU.mult).then_inc(turned, 1)
                        dve.tensor_tensor(turn_, ps[:, 2 + c % 2, 0:n], sin, ALU.mult).then_inc(turned, 1)
                        dve.wait_ge(turned, 2 * (c + 1))
                        dve.tensor_tensor(exact, exact, turn_, ALU.add).then_inc(rotated, 1)
                        dve.wait_ge(hi_done, c + 1)
                    else:
                        dve.wait_ge(exact_done, 2 * (c + 1))
                    dve.tensor_tensor(rest, exact, dst[:, 0, :], ALU.subtract).then_inc(rest_done, 1)
                    dve.wait_ge(rest_done, c + 1)
                    dve.tensor_copy(dst[:, 1, :], rest).then_inc(mid_done, 1)
                    dve.wait_ge(mid_done, c + 1)
                    dve.tensor_tensor(dst[:, 2, :], rest, dst[:, 1, :], ALU.subtract).then_inc(lo_done, 1)

    def stack_loads(sp, other, keys, q_terms, q_copies, k_terms, k_copies, keys_read, per_unit, rows_out):
        sp.sem_clear(other)
        for j in range(3):
            for g in range(GROUPS):
                sp.dma_start(q_stack[24 * j:24 * j + 8, 4 * g:4 * g + 4, :],
                             q_parts[32 * g:32 * g + 32, j, :]).then_inc(q_terms, 16)
        load_keys(sp, 0, keys, k_terms, k_copies)
        sp.wait_ge(q_terms, 16 * 12)
        for j in range(3):
            for i in (1, 2):
                sp.dma_start(q_stack[24 * j + 8 * i:24 * j + 8 * i + 8, :, :],
                             q_stack[24 * j:24 * j + 8, :, :]).then_inc(q_copies, 16)
        for u in range(1, PAIR * GROUPS):
            if u >= 2:
                sp.wait_ge(keys_read, per_unit * (u - 1))
            load_keys(sp, u, keys, k_terms, k_copies)
            if rows_out:
                rows_out(sp, u - 1)
        if rows_out:
            rows_out(sp, PAIR * GROUPS - 1)

    def load_keys(sp, u, keys, k_terms, k_copies):
        b, g, slot = u // GROUPS, u % GROUPS, u % 2
        for i in range(3):
            sp.dma_start(k_stack[slot][8 * i:8 * i + 8, :, 0:keys],
                         k_parts[32 * g:32 * g + 32, i, b * keys:(b + 1) * keys]).then_inc(k_terms[slot], 16)
        sp.wait_ge(k_terms[slot], 48 * (u // 2 + 1))
        for j in (1, 2):
            sp.dma_start(k_stack[slot][24 * j:24 * j + 24, :, 0:keys],
                         k_stack[slot][0:24, :, 0:keys]).then_inc(k_copies[slot], 16)

    HALF = (CTX + 1) // 2

    def attention(kind, v_bias):
        s, other = semaphores()
        keys = CTX if kind == "cross" else TOK
        tiles = CTX_TILES if kind == "cross" else 2
        units = PAIR * GROUPS
        q_terms, q_copies = s.take(), s.take()
        k_terms, k_copies = s.take(2), s.take(2)
        neg_loaded = s.take(2)
        (st_ready, exp_done, pv_done, a_ready, max_done, small, neg_ready, neg_turned, rows_ready,
         o_copied, o_turned, normalised, all_turned, finished, cleared) = [s.take() for _ in range(15)]
        chunks = {"cross": 16, "self": 2, "window": 1}[kind]
        smalls = 4 if kind == "cross" else 3
        keys_of = (lambda t: tile_rows(t)) if kind == "cross" else (lambda t: P)
        a_at = [round(chunks * t / tiles) for t in range(tiles + 1)]

        with nc.Block() as block:
            @block.sync
            def _(sp):
                def rows_out(sp, u):
                    b, g = u // GROUPS, u % GROUPS
                    sp.wait_ge(rows_ready, u + 1)
                    for qt in range(2):
                        sp.dma_start(q_stack[96:99, 4 * g:4 * g + 4, b * TOK + qt * P:b * TOK + (qt + 1) * P],
                                     neg_rows[u % 2][12 * qt:12 * qt + 12, :]).then_inc(neg_loaded[u % 2], 16)
                stack_loads(sp, other, keys, q_terms, q_copies, k_terms, k_copies, st_ready, 2 * tiles, rows_out)

            @block.tensor
            def _(pe):
                def phase_a(u, c):
                    b, g, slot = u // GROUPS, u % GROUPS, u % 2
                    n = u * chunks + c
                    if c == 0:
                        pe.wait_ge(k_copies[slot], 32 * (u // 2 + 1))
                    if n >= 2:
                        pe.wait_ge(max_done, n - 1)
                    bank = 2 * (n % 2)
                    if kind == "cross":
                        r, half = c // 2, c % 2
                        j, qt = r // 2, r % 2
                        first = half * HALF
                        for col in range(0, HALF - half, 512):
                            width = min(512, HALF - half - col)
                            mm = pe.matmul(ps[:, bank + col // 512, 0:width],
                                           q_stack[0:SCORE_ROWS, 4 * g + j, b * TOK + qt * P:b * TOK + (qt + 1) * P],
                                           k_stack[slot][0:SCORE_ROWS, j, first + col:first + col + width],
                                           start=True, stop=True)
                    elif kind == "self":
                        for i in range(4):
                            j, qt = (4 * c + i) // 2, i % 2
                            mm = pe.matmul(ps[:, bank + i // 2, (i % 2) * TOK:(i % 2 + 1) * TOK],
                                           q_stack[0:SCORE_ROWS, 4 * g + j, b * TOK + qt * P:b * TOK + (qt + 1) * P],
                                           k_stack[slot][0:SCORE_ROWS, j, 0:TOK], start=True, stop=True)
                    else:
                        for r in range(8):
                            j, qt = r // 2, r % 2
                            for h in range(2):
                                k0_ = qt * P + h * WIN
                                mm = pe.matmul(ps[h * WIN:(h + 1) * WIN, bank, r * WIN:(r + 1) * WIN],
                                               q_stack[0:SCORE_ROWS, 4 * g + j, b * TOK + k0_:b * TOK + k0_ + WIN],
                                               k_stack[slot][0:SCORE_ROWS, j, k0_:k0_ + WIN], start=True, stop=True)
                    mm.then_inc(a_ready, 1)

                def turn_maxima(u):
                    pe.wait_ge(neg_ready, u + 1)
                    pe.transpose(ps[0:24, 7, 0:P // 2].bitcast(BF16), neg_parts[:, :, :, :].rearrange("p a b c -> p (a b c)"),
                                 ident16[:, :]).then_inc(neg_turned, 1)

                def scores_t(u, t):
                    b, g, slot = u // GROUPS, u % GROUPS, u % 2
                    if t == 0:
                        pe.wait_ge(neg_loaded[u % 2], 32 * (u // 2 + 1))
                    rows = keys_of(t)
                    for hp in range(2):
                        n = (u * tiles + t) * 2 + hp
                        if n >= 2:
                            pe.wait_ge(exp_done, n - 1)
                        for i in range(2):
                            j = 2 * hp + i
                            if kind == "window":
                                for h in range(2):
                                    at = t * P + h * WIN
                                    mm = pe.matmul(ps[h * WIN:(h + 1) * WIN, 4 + hp, i * WIN:(i + 1) * WIN],
                                                   k_stack[slot][0:MAX_ROWS, j, at:at + WIN],
                                                   q_stack[0:MAX_ROWS, 4 * g + j, b * TOK + at:b * TOK + at + WIN],
                                                   start=True, stop=True)
                            else:
                                mm = pe.matmul(ps[0:rows, 4 + hp, i * TOK:(i + 1) * TOK],
                                               k_stack[slot][0:MAX_ROWS, j, t * P:t * P + rows],
                                               q_stack[0:MAX_ROWS, 4 * g + j, b * TOK:(b + 1) * TOK],
                                               start=True, stop=True)
                        mm.then_inc(st_ready, 1)

                def weighted(u, t):
                    b, g = u // GROUPS, u % GROUPS
                    n = u * tiles + t
                    rows = keys_of(t)
                    pe.wait_ge(exp_done, 2 * (n + 1))
                    if t == 0 and u >= 1:
                        pe.wait_ge(normalised, u)
                    for j in range(4):
                        lhs = values[0:rows, b * tiles + t, (4 * g + j) * VH:(4 * g + j) * VH + 32]
                        if kind == "window":
                            mm = pe.matmul(ps[32 * j:32 * j + 32, 6, t * P:(t + 1) * P], lhs,
                                           probs[n % 3][:, j, 0:P], start=True, stop=True)
                        else:
                            mm = pe.matmul(ps[32 * j:32 * j + 32, 6, 0:TOK], lhs, probs[n % 3][0:rows, j, :],
                                           start=(t == 0), stop=(t == tiles - 1))
                    mm.then_inc(pv_done, 1)

                def turn_heads(u):
                    pe.wait_ge(o_copied, u + 1)
                    for qt in range(2):
                        mm = pe.transpose(ps[:, 6, TOK + qt * P:TOK + (qt + 1) * P], heads_out[:, qt * P:(qt + 1) * P],
                                          ident[:, :])
                    mm.then_inc(o_turned, 1)

                pe.wait_ge(q_copies, 16 * 6)
                for c in range(chunks):
                    phase_a(0, c)
                turn_maxima(0)
                for u in range(units):
                    for t in range(tiles):
                        scores_t(u, t)
                        if u >= 1 and t == 0:
                            turn_heads(u - 1)
                        if u + 1 < units:
                            for c in range(a_at[t], a_at[t + 1]):
                                phase_a(u + 1, c)
                        if t >= 1:
                            weighted(u, t - 1)
                    weighted(u, tiles - 1)
                    if u + 1 < units:
                        turn_maxima(u + 1)
                turn_heads(units - 1)
                pe.wait_ge(normalised, units)
                for i in range(2 * PAIR):
                    mm = pe.transpose(ps[:, 0, i * P:(i + 1) * P], attn_tok[:, i // 2, i % 2, :], ident[:, :])
                mm.then_inc(all_turned, 1)

            @block.vector
            def _(dve):
                def maxima_of(u):
                    for c in range(chunks):
                        n = u * chunks + c
                        bank = 2 * (n % 2)
                        dve.wait_ge(a_ready, n + 1)
                        if kind == "cross":
                            width = HALF - c % 2
                            src = ps[:, bank:bank + 2, :].rearrange("p a b -> p (a b)")[:, 0:width]
                            dve.tensor_reduce(maxima[:, u % 2, c:c + 1], src, AX.X, ALU.max).then_inc(max_done, 1)
                        elif kind == "self":
                            src = ps[:, bank:bank + 2, :].rearrange("p a (b k) -> p (a b) k", b=2)
                            dve.tensor_reduce(maxima[:, u % 2, 4 * c:4 * c + 4], src, AX.X, ALU.max).then_inc(max_done, 1)
                        else:
                            src = ps[:, bank, :].rearrange("p (r k) -> p r k", r=8)
                            dve.tensor_reduce(maxima[:, u % 2, 0:8], src, AX.X, ALU.max).then_inc(max_done, 1)
                        if n % chunks == 0 and u >= 1 and chunks > 1:
                            heads_to_tokens(u - 2)
                    dve.wait_ge(max_done, (u + 1) * chunks)
                    m, k = maxima[:, u % 2, 0:8], u * smalls
                    if kind == "cross":
                        m = max8[:, :]
                        dve.tensor_reduce(m, maxima[:, u % 2, :].rearrange("p (r h) -> p r h", h=2), AX.X, ALU.max) \
                            .then_inc(small, 1)
                        k += 1
                        dve.wait_ge(small, k)
                    if u >= 1:
                        dve.wait_ge(neg_turned, u)
                    m = m.rearrange("p (j t) -> p t j", t=2)
                    rest = neg_f[:, :].rearrange("p (t j) -> p t j", t=2)
                    dve.tensor_scalar(neg_parts[:, :, 0, :], m, -1.0, None, ALU.mult).then_inc(small, 1)
                    dve.wait_ge(small, k + 1)
                    dve.scalar_tensor_tensor(rest, m, -1.0, neg_parts[:, :, 0, :], ALU.mult, ALU.subtract) \
                        .then_inc(small, 1)
                    dve.wait_ge(small, k + 2)
                    dve.tensor_copy(neg_parts[:, :, 1, :], rest).then_inc(small, 1)
                    dve.wait_ge(small, k + 3)
                    dve.tensor_tensor(neg_parts[:, :, 2, :], rest, neg_parts[:, :, 1, :], ALU.subtract) \
                        .then_inc(neg_ready, 1)

                def heads_to_tokens(u):
                    if u < 0:
                        return
                    b, g = u // GROUPS, u % GROUPS
                    dve.wait_ge(o_turned, u + 1)
                    got = ps[:, 6, TOK:2 * TOK].rearrange("p (t j c) -> p t j c", t=2, j=GROUP)
                    dve.reciprocal(sums_inv[:, :, :], got[:, :, :, HD]).then_inc(finished, 1)
                    dve.wait_ge(finished, u + 1)
                    dst = attn_tok[:, b, :, 32 * g:32 * g + 32].rearrange("p t (j d) -> p t j d", j=GROUP)
                    inv = sums_inv[:, :, :].unsqueeze(3).to_broadcast([P, 2, GROUP, HD])
                    dve.tensor_tensor(dst, got[:, :, :, 0:HD], inv, ALU.mult).then_inc(normalised, 1)

                if kind == "window":
                    for i in range(3):
                        dve.memset(probs[i][:, :, :], 0.0).then_inc(cleared, 1)
                for u in range(units):
                    maxima_of(u)
                    if chunks == 1:
                        heads_to_tokens(u - 2)
                heads_to_tokens(units - 2)
                heads_to_tokens(units - 1)

            @block.scalar
            def _(act):
                def rows_of_maxima(u):
                    act.wait_ge(neg_turned, u + 1)
                    if u >= 2:
                        act.wait_ge(neg_loaded[u % 2], 32 * (u // 2))
                    act.copy(neg_rows[u % 2][:, :], ps[0:24, 7, 0:P // 2].bitcast(BF16)).then_inc(rows_ready, 1)

                if kind == "window":
                    act.wait_ge(cleared, 3)
                rows_of_maxima(0)
                for u in range(units):
                    for t in range(tiles):
                        rows = keys_of(t)
                        n = u * tiles + t
                        if n >= 3:
                            act.wait_ge(pv_done, n - 2)
                        for hp in range(2):
                            act.wait_ge(st_ready, 2 * n + hp + 1)
                            if kind == "window":
                                for h in range(2):
                                    half = slice(h * WIN, (h + 1) * WIN)
                                    src = ps[half, 4 + hp, 0:2 * WIN].rearrange("p (j q) -> p j q", j=2)
                                    e = act.activation(probs[n % 3][half, 2 * hp:2 * hp + 2, half], src,
                                                       ACT.Exp, scale=SCALE)
                            else:
                                src = ps[0:rows, 4 + hp, :].rearrange("p (j q) -> p j q", j=2)
                                e = act.activation(probs[n % 3][0:rows, 2 * hp:2 * hp + 2, :], src,
                                                   ACT.Exp, scale=SCALE)
                            e.then_inc(exp_done, 1)
                    if u + 1 < units:
                        rows_of_maxima(u + 1)
                    act.wait_ge(pv_done, (u + 1) * tiles)
                    if u >= 1:
                        act.wait_ge(o_turned, u)
                    act.copy(heads_out[:, :], ps[:, 6, 0:TOK]).then_inc(o_copied, 1)
                act.wait_ge(all_turned, 1)
                b_ap = 0.0 if v_bias is None else v_bias
                act.activation(attn[:, :], ps[:, 0, :], ACT.Identity, bias=b_ap).then_inc(o_copied, 1)

    def top_attention(v_bias):
        s, other = semaphores()
        q_terms, q_copies = s.take(), s.take()
        k_terms, k_copies = s.take(2), s.take(2)
        (s_ready, top8, taken8, top16, taken16, e_done, rest_done, weight_done, t_ready, t_copied,
         pv_done, o_copied, o_turned, inv_done, normalised, all_turned) = [s.take() for _ in range(16)]
        units = PAIR * GROUPS
        total = units * 8
        quads = [(q, min(4, CTX_TILES - q)) for q in range(0, CTX_TILES, 4)]
        nq = len(quads)
        scores = ps[:, 0:4, :].rearrange("p a b -> p (a b)")[:, 0:CTX]

        with nc.Block() as block:
            @block.sync
            def _(sp):
                stack_loads(sp, other, CTX, q_terms, q_copies, k_terms, k_copies, s_ready, 8, None)

            @block.tensor
            def _(pe):
                def score_tile(i):
                    u, r = i // 8, i % 8
                    b, g, slot, j, qt = u // GROUPS, u % GROUPS, u % 2, r // 2, r % 2
                    if r == 0:
                        pe.wait_ge(k_copies[slot], 32 * (u // 2 + 1))
                    if i >= 1:
                        pe.wait_ge(e_done, i)
                    for col in range(0, CTX, 512):
                        width = min(512, CTX - col)
                        mm = pe.matmul(ps[:, col // 512, 0:width],
                                       q_stack[0:SCORE_ROWS, 4 * g + j, b * TOK + qt * P:b * TOK + (qt + 1) * P],
                                       k_stack[slot][0:SCORE_ROWS, j, col:col + width], start=True, stop=True)
                    mm.then_inc(s_ready, 1)

                def turn_weights(i):
                    pe.wait_ge(weight_done, i + 1)
                    for q, (first, count) in enumerate(quads):
                        n = i * nq + q
                        if n >= 2:
                            pe.wait_ge(t_copied, n - 1)
                        for k in range(count):
                            t = first + k
                            rows = tile_rows(t)
                            mm = pe.transpose(ps[0:rows, 4 + n % 2, k * P:(k + 1) * P],
                                              weight_e[i % 2][:, t * P:t * P + rows], ident[:, :])
                        mm.then_inc(t_ready, 1)

                def weighted(i):
                    u, r = i // 8, i % 8
                    b, g, j, qt = u // GROUPS, u % GROUPS, r // 2, r % 2
                    pe.wait_ge(t_copied, (i + 1) * nq)
                    if r == 0 and u >= 1:
                        pe.wait_ge(normalised, u)
                    for t in range(CTX_TILES):
                        rows = tile_rows(t)
                        h = 4 * g + j
                        mm = pe.matmul(ps[32 * j:32 * j + 32, 6, qt * P:(qt + 1) * P],
                                       values[0:rows, b * CTX_TILES + t, h * VH:h * VH + 32],
                                       probs_t[i % 2][0:rows, t, :], start=(t == 0), stop=(t == CTX_TILES - 1))
                    mm.then_inc(pv_done, 1)

                def turn_heads(u):
                    pe.wait_ge(o_copied, u + 1)
                    for qt in range(2):
                        mm = pe.transpose(ps[:, 6, TOK + qt * P:TOK + (qt + 1) * P], heads_out[:, qt * P:(qt + 1) * P],
                                          ident[:, :])
                    mm.then_inc(o_turned, 1)

                pe.wait_ge(q_copies, 16 * 6)
                for i in range(total + 2):
                    if i < total:
                        score_tile(i)
                    if 1 <= i <= total:
                        turn_weights(i - 1)
                    if i >= 2:
                        if (i - 2) % 8 == 0 and i > 2:
                            turn_heads((i - 2) // 8 - 1)
                        weighted(i - 2)
                turn_heads(units - 1)
                pe.wait_ge(normalised, units)
                for i in range(2 * PAIR):
                    mm = pe.transpose(ps[:, 7, i * P:(i + 1) * P], attn_tok[:, i // 2, i % 2, :], ident[:, :])
                mm.then_inc(all_turned, 1)

            @block.vector
            def _(dve):
                def heads_to_tokens(u):
                    b, g = u // GROUPS, u % GROUPS
                    dve.wait_ge(o_turned, u + 1)
                    got = ps[:, 6, TOK:2 * TOK].rearrange("p (t j c) -> p t j c", t=2, j=GROUP)
                    dve.reciprocal(sums_inv[:, :, :], got[:, :, :, HD]).then_inc(inv_done, 1)
                    dve.wait_ge(inv_done, u + 1)
                    dst = attn_tok[:, b, :, 32 * g:32 * g + 32].rearrange("p t (j d) -> p t j d", j=GROUP)
                    inv = sums_inv[:, :, :].unsqueeze(3).to_broadcast([P, 2, GROUP, HD])
                    dve.tensor_tensor(dst, got[:, :, :, 0:HD], inv, ALU.mult).then_inc(normalised, 1)

                for i in range(total):
                    top, left = best[:, i % 2, :], untaken[i % 2]
                    dve.wait_ge(s_ready, i + 1)
                    if i >= 2:
                        dve.wait_ge(e_done, i - 1)
                        dve.wait_ge(rest_done, i - 1)
                    dve.max(top[:, 0:8], scores).then_inc(top8, 1)
                    if i >= 2:
                        dve.wait_ge(weight_done, i - 1)
                    dve.wait_ge(top8, i + 1)
                    dve.tensor_scalar(top[:, TOPK:TOPK + 1], top[:, 0:1], -SCALE, None, ALU.mult)
                    dve.match_replace(left, top[:, 0:8], scores, LOW).then_inc(taken8, 1)
                    dve.wait_ge(taken8, i + 1)
                    dve.max(top[:, 8:16], left).then_inc(top16, 1)
                    dve.wait_ge(top16, i + 1)
                    dve.match_replace(left, top[:, 8:16], left, LOW).then_inc(taken16, 1)
                    if i % 8 == 2 and i > 8:
                        heads_to_tokens(i // 8 - 1)
                heads_to_tokens(units - 1)

            @block.scalar
            def _(act):
                def copy_turned(i):
                    for q, (first, count) in enumerate(quads):
                        n = i * nq + q
                        rows = tile_rows(first)
                        act.wait_ge(t_ready, n + 1)
                        if q == 0 and i >= 2:
                            act.wait_ge(pv_done, i - 1)
                        act.copy(probs_t[i % 2][0:rows, first:first + count, :],
                                 ps[0:rows, 4 + n % 2, 0:count * P].rearrange("p (t q) -> p t q", t=count)) \
                            .then_inc(t_copied, 1)

                def copy_heads(u):
                    act.wait_ge(pv_done, 8 * (u + 1))
                    if u >= 1:
                        act.wait_ge(o_turned, u)
                    act.copy(heads_out[:, :], ps[:, 6, 0:TOK]).then_inc(o_copied, 1)

                for i in range(total + 1):
                    if i < total:
                        top, left = best[:, i % 2, :], untaken[i % 2]
                        act.wait_ge(taken8, i + 1)
                        if i >= 2:
                            act.wait_ge(t_ready, (i - 1) * nq)
                        act.activation(weight_e[i % 2], scores, ACT.Exp, bias=top[:, TOPK:TOPK + 1], scale=SCALE) \
                            .then_inc(e_done, 1)
                    if i >= 1:
                        copy_turned(i - 1)
                    if i < total:
                        act.wait_ge(taken16, i + 1)
                        act.activation(left, left, ACT.Exp, bias=top[:, TOPK:TOPK + 1], scale=SCALE) \
                            .then_inc(rest_done, 1)
                    if i >= 9 and i % 8 == 1:
                        copy_heads(i // 8 - 1)
                copy_heads(units - 1)
                act.wait_ge(all_turned, 1)
                act.activation(attn[:, :], ps[:, 7, :], ACT.Identity, bias=v_bias).then_inc(o_copied, 1)

            @block.gpsimd
            def _(pool):
                for i in range(total):
                    pool.wait_ge(rest_done, i + 1)
                    pool.wait_ge(e_done, i + 1)
                    pool.tensor_tensor(weight_e[i % 2], weight_e[i % 2], untaken[i % 2], ALU.subtract) \
                        .then_inc(weight_done, 1)

    def project_prototypes():
        jobs = [([(w("0q"), normed[:, :])], tmp_a[:, :])]
        flat = ctx[:, :, :].rearrange("p b n -> p (b n)")
        k_flat = k0.rearrange("p b n -> p (b n)")
        for c in range(0, PAIR * CTX, 512):
            n = min(512, PAIR * CTX - c)
            jobs.append(([(w("0k"), flat[:, c:c + n])], k_flat[:, c:c + n]))
        for b in range(PAIR):
            for t in range(CTX_TILES):
                rows = tile_rows(t)
                jobs.append(([(ctx[:, b, t * P:t * P + rows], w("0v"))], v0[0:rows, b * CTX_TILES + t, :]))
        s, other = semaphores()
        product_ready, act_emptied, dve_emptied = s.take(), s.take(), s.take()
        with nc.Block() as block:
            @block.sync
            def _(sp):
                sp.sem_clear(other)

            @block.tensor
            def _(pe):
                for i, (terms, dst) in enumerate(jobs):
                    if i >= 4:
                        pe.wait_ge(act_emptied if i % 2 == 0 else dve_emptied, (i - 4) // 2 + 1)
                    lhs, rhs = terms[0]
                    pe.matmul(ps[0:dst.shape[0], i % 4, 0:dst.shape[1]], lhs, rhs, start=True, stop=True) \
                        .then_inc(product_ready, 1)

            @block.scalar
            def _(act):
                for i, (terms, dst) in enumerate(jobs):
                    if i % 2 == 0:
                        act.wait_ge(product_ready, i + 1)
                        act.copy(dst, ps[0:dst.shape[0], i % 4, 0:dst.shape[1]]).then_inc(act_emptied, 1)

            @block.vector
            def _(dve):
                for i, (terms, dst) in enumerate(jobs):
                    if i % 2 == 1:
                        dve.wait_ge(product_ready, i + 1)
                        dve.tensor_copy(dst, ps[0:dst.shape[0], i % 4, 0:dst.shape[1]]).then_inc(dve_emptied, 1)

    def prototype_attention():
        s, other = semaphores()
        (a_ready, max_done, neg_ready, neg_turned, row_ready, st_ready, exp_done, pv_done, batch_done, inverted,
         scaled) = [s.take() for _ in range(11)]
        scale0 = float(D) ** -0.5
        tiles = CTX_TILES
        with nc.Block() as block:
            @block.sync
            def _(sp):
                sp.sem_clear(other)

            @block.tensor
            def _(pe):
                for b in range(PAIR):
                    for r in range(4):
                        n = b * 4 + r
                        qt, half = r // 2, r % 2
                        bank = 2 * (n % 2)
                        if n >= 2:
                            pe.wait_ge(max_done, n - 1)
                        for col in range(0, HALF - half, 512):
                            width = min(512, HALF - half - col)
                            mm = pe.matmul(ps[:, bank + col // 512, 0:width],
                                           tmp_a[:, b * TOK + qt * P:b * TOK + (qt + 1) * P],
                                           k0[:, b, half * HALF + col:half * HALF + col + width], start=True, stop=True)
                        mm.then_inc(a_ready, 1)
                pe.wait_ge(neg_ready, 1)
                for i in range(4):
                    mm = pe.transpose(ps[0:1, 4, i * P:(i + 1) * P], max8[:, i:i + 1], ident[:, :])
                mm.then_inc(neg_turned, 1)
                pe.wait_ge(row_ready, 1)
                for n in range(PAIR * tiles + 1):
                    if n < PAIR * tiles:
                        b, t = n // tiles, n % tiles
                        rows = tile_rows(t)
                        if n >= 2:
                            pe.wait_ge(exp_done, n - 1)
                        st = ps[0:rows, n % 2, 0:TOK]
                        pe.matmul(st, k0[:, b, t * P:t * P + rows], tmp_a[:, b * TOK:(b + 1) * TOK],
                                  start=True, stop=False)
                        pe.matmul(st, ones[0:1, 0:rows], neg_row0[:, b * TOK:(b + 1) * TOK],
                                  start=False, stop=True).then_inc(st_ready, 1)
                    if n >= 1:
                        m = n - 1
                        b, t = m // tiles, m % tiles
                        rows = tile_rows(t)
                        pe.wait_ge(exp_done, n)
                        pe.matmul(ps[:, 4 + 2 * b, 0:TOK], v0[0:rows, m, :], probs0[m % 3][0:rows, :],
                                  start=(t == 0), stop=(t == tiles - 1))
                        pe.matmul(ps[:, 5 + 2 * b, 0:TOK], ones[0:rows, :], probs0[m % 3][0:rows, :],
                                  start=(t == 0), stop=(t == tiles - 1)).then_inc(pv_done, 1)

            @block.vector
            def _(dve):
                for n in range(PAIR * 4):
                    bank = 2 * (n % 2)
                    dve.wait_ge(a_ready, n + 1)
                    src = ps[:, bank:bank + 2, :].rearrange("p a b -> p (a b)")[:, 0:HALF - n % 2]
                    dve.tensor_reduce(maxima[:, 0, n:n + 1], src, AX.X, ALU.max).then_inc(max_done, 1)
                dve.wait_ge(max_done, 8)
                dve.tensor_reduce(neg_f[:, 0:4], maxima[:, 0, 0:8].rearrange("p (r h) -> p r h", h=2), AX.X, ALU.max) \
                    .then_inc(scaled, 1)
                dve.wait_ge(scaled, 1)
                dve.tensor_scalar(max8[:, 0:4], neg_f[:, 0:4], -1.0, None, ALU.mult).then_inc(neg_ready, 1)
                dve.wait_ge(neg_turned, 1)
                dve.tensor_copy(neg_row0, ps[0:1, 4, :]).then_inc(row_ready, 1)
                for b in range(PAIR):
                    cols = slice(b * TOK, (b + 1) * TOK)
                    dve.wait_ge(pv_done, (b + 1) * tiles)
                    dve.reciprocal(tmp_b[:, cols], ps[:, 5 + 2 * b, 0:TOK]).then_inc(inverted, 1)
                    dve.wait_ge(inverted, b + 1)
                    dve.tensor_tensor(attn[:, cols], ps[:, 4 + 2 * b, 0:TOK], tmp_b[:, cols], ALU.mult) \
                        .then_inc(scaled, 1)

            @block.scalar
            def _(act):
                for n in range(PAIR * tiles):
                    rows = tile_rows(n % tiles)
                    act.wait_ge(st_ready, n + 1)
                    if n >= 3:
                        act.wait_ge(pv_done, n - 2)
                    act.activation(probs0[n % 3][0:rows, :], ps[0:rows, n % 2, 0:TOK], ACT.Exp, scale=scale0) \
                        .then_inc(exp_done, 1)

    def route():
        s, other = semaphores()
        logits_ready, biased, step, exp_done = [s.take() for _ in range(4)]
        at = W.at["0router"][0]
        with nc.Block() as block:
            @block.sync
            def _(sp):
                sp.sem_clear(other)

            @block.tensor
            def _(pe):
                for e in range(3):
                    pe.matmul(ps[:, e, :], weights[:, at + e:at + e + 1].to_broadcast([P, P]), normed[:, :],
                              start=True, stop=False)
                    pe.matmul(ps[:, e, :], weights[:, at + 3 + e:at + 4 + e].to_broadcast([P, P]), attn[:, :],
                              start=False, stop=True).then_inc(logits_ready, 1)

            @block.vector
            def _(dve):
                for e in range(3):
                    dve.wait_ge(logits_ready, e + 1)
                    for b in range(PAIR):
                        cols = slice(b * TOK, (b + 1) * TOK)
                        dve.tensor_scalar(router_p[:, e, cols], ps[:, e, cols], modc("0router", b, e), None, ALU.add) \
                            .then_inc(biased, 1)
                dve.wait_ge(biased, 6)
                dve.tensor_tensor(tmp_a[:, :], router_p[:, 0, :], router_p[:, 1, :], ALU.max).then_inc(step, 1)
                dve.wait_ge(step, 1)
                dve.tensor_tensor(tmp_a[:, :], tmp_a[:, :], router_p[:, 2, :], ALU.max).then_inc(step, 1)
                dve.wait_ge(step, 2)
                for e in range(3):
                    dve.tensor_tensor(router_p[:, e, :], router_p[:, e, :], tmp_a[:, :], ALU.subtract).then_inc(step, 1)
                dve.wait_ge(exp_done, 3)
                dve.tensor_tensor(tmp_b[:, :], router_p[:, 0, :], router_p[:, 1, :], ALU.add).then_inc(step, 1)
                dve.wait_ge(step, 6)
                dve.tensor_tensor(tmp_b[:, :], tmp_b[:, :], router_p[:, 2, :], ALU.add).then_inc(step, 1)
                dve.wait_ge(step, 7)
                dve.reciprocal(tmp_a[:, :], tmp_b[:, :]).then_inc(step, 1)
                dve.wait_ge(step, 8)
                for e in range(3):
                    dve.tensor_tensor(router_p[:, e, :], router_p[:, e, :], tmp_a[:, :], ALU.mult).then_inc(step, 1)

            @block.scalar
            def _(act):
                for e in range(3):
                    act.wait_ge(step, 3 + e)
                    act.activation(router_p[:, e, :], router_p[:, e, :], ACT.Exp).then_inc(exp_done, 1)

    def hidden_of_experts():
        s, other = semaphores()
        product_ready, emptied = s.take(), s.take()
        with nc.Block() as block:
            @block.sync
            def _(sp):
                sp.sem_clear(other)

            @block.tensor
            def _(pe):
                for i in range(7):
                    if i >= 4:
                        pe.wait_ge(emptied, 2 * (i - 3))
                    for k, rhs in enumerate((normed[:, :], attn[:, :])):
                        lhs = w("0gate1", k) if i == 6 else w("0e1", (i // 2) * 4 + k * 2 + i % 2)
                        mm = pe.matmul(ps[:, i % 4, :], lhs, rhs, start=(k == 0), stop=(k == 1))
                    mm.then_inc(product_ready, 1)

            @block.scalar
            def _(act):
                for i in range(7):
                    act.wait_ge(product_ready, i + 1)
                    for b in range(PAIR):
                        cols = slice(b * TOK, (b + 1) * TOK)
                        col = modc("0gate1", b) if i == 6 else modc("0e1", b, i)
                        act.activation(hidden[:, i, cols], ps[:, i % 4, cols], ACT.Silu, bias=col).then_inc(emptied, 1)

    def mix_experts():
        s, other = semaphores()
        product_ready, gate_done, weighed, mixed, out_ready, gated, added = [s.take() for _ in range(7)]
        with nc.Block() as block:
            @block.sync
            def _(sp):
                sp.sem_clear(other)

            @block.tensor
            def _(pe):
                for e in range(3):
                    for k in range(2):
                        mm = pe.matmul(ps[:, e, :], w("0e2", 2 * e + k), hidden[:, 2 * e + k, :], start=(k == 0), stop=(k == 1))
                    mm.then_inc(product_ready, 1)
                pe.matmul(ps[:, 3, :], w("0gate2"), hidden[:, 6, :], start=True, stop=True).then_inc(product_ready, 1)
                pe.wait_ge(mixed, 2)
                pe.matmul(ps[:, 4, :], w("0out"), tmp_a[:, :], start=True, stop=True).then_inc(out_ready, 1)

            @block.scalar
            def _(act):
                act.wait_ge(product_ready, 4)
                act.activation(tmp_b[:, :], ps[:, 3, :], ACT.Sigmoid, bias=bias("0gate2")).then_inc(gate_done, 1)

            @block.vector
            def _(dve):
                for e in range(3):
                    dve.wait_ge(product_ready, e + 1)
                    dst = tmp_a[:, :] if e == 0 else router_p[:, e, :]
                    dve.scalar_tensor_tensor(dst, ps[:, e, :], bias("0e2", e), router_p[:, e, :], ALU.add, ALU.mult) \
                        .then_inc(weighed, 1)
                for e in (1, 2):
                    dve.wait_ge(weighed, e + 1)
                    if e == 2:
                        dve.wait_ge(mixed, 1)
                    dve.tensor_tensor(tmp_a[:, :], tmp_a[:, :], router_p[:, e, :], ALU.add).then_inc(mixed, 1)
                dve.wait_ge(out_ready, 1)
                dve.wait_ge(gate_done, 1)
                dve.scalar_tensor_tensor(tmp_b[:, :], ps[:, 4, :], bias("0out"), tmp_b[:, :], ALU.add, ALU.mult) \
                    .then_inc(gated, 1)
                dve.wait_ge(gated, 1)
                dve.tensor_tensor(x[:, :], x[:, :], tmp_b[:, :], ALU.add).then_inc(added, 1)

    def swiglu():
        s, other = semaphores()
        product_ready, silu_done, multiplied = s.take(), s.take(), s.take()
        with nc.Block() as block:
            @block.sync
            def _(sp):
                sp.sem_clear(other)

            @block.tensor
            def _(pe):
                for i in range(8):
                    chunk = i // 2 + 4 * (i % 2)
                    if i >= 4:
                        if i % 2 == 0:
                            pe.wait_ge(silu_done, i // 2 - 1)
                        else:
                            pe.wait_ge(multiplied, i // 2 - 1)
                    pe.matmul(ps[:, i % 4, :], w("3f1", chunk), normed[:, :], start=True, stop=True) \
                        .then_inc(product_ready, 1)

            @block.scalar
            def _(act):
                for c in range(4):
                    act.wait_ge(product_ready, 2 * c + 1)
                    act.activation(hidden[:, c, :], ps[:, (2 * c) % 4, :], ACT.Silu, bias=bias("3f1", c)) \
                        .then_inc(silu_done, 1)

            @block.vector
            def _(dve):
                for c in range(4):
                    dve.wait_ge(product_ready, 2 * c + 2)
                    dve.wait_ge(silu_done, c + 1)
                    dve.scalar_tensor_tensor(hidden[:, c, :], ps[:, (2 * c + 1) % 4, :], bias("3f1", 4 + c),
                                             hidden[:, c, :], ALU.add, ALU.mult).then_inc(multiplied, 1)

    ctx_flat = ctx[:, :, :].rearrange("p b n -> p (b n)")

    def self_jobs(src, layer, rope=False):
        jobs = []
        for n, dst in (("sq", q_parts[:, :, :]), ("sk", k_parts[:, :, 0:N])):
            if rope:
                for b in range(PAIR):
                    cols = slice(b * TOK, (b + 1) * TOK)
                    jobs.append((src[:, cols], w(f"{layer}{n}"), w(f"{layer}{n}r"), None,
                                 rope_tok[:, 0, :], rope_tok[:, 1, :], dst[:, :, cols]))
            else:
                jobs.append((src, w(f"{layer}{n}"), None, bias(f"{layer}{n}"), None, None, dst))
        values_ = [[(src[:, i * P:(i + 1) * P], i) for i in range(4)]]
        return jobs, values_

    def cross_jobs(src, layer, rope=False):
        if rope:
            jobs = [(src[:, b * TOK:(b + 1) * TOK], w(f"{layer}cq"), w(f"{layer}cqr"), None, rope_tok[:, 0, :],
                     rope_tok[:, 1, :], q_parts[:, :, b * TOK:(b + 1) * TOK]) for b in range(PAIR)]
        else:
            jobs = [(src, w(f"{layer}cq"), None, bias(f"{layer}cq"), None, None, q_parts[:, :, :])]
        for b in range(PAIR):
            for c in range(0, CTX, 512):
                n = min(512, CTX - c)
                dst = k_parts[:, :, b * CTX + c:b * CTX + c + n]
                if rope:
                    jobs.append((ctx[:, b, c:c + n], w(f"{layer}ck"), w(f"{layer}ckr"), None,
                                 rope_ctx[:, 0, c:c + n], rope_ctx[:, 1, c:c + n], dst))
                else:
                    jobs.append((ctx[:, b, c:c + n], w(f"{layer}ck"), None, bias(f"{layer}ck"), None, None, dst))
        groups = []
        for b in range(PAIR):
            for first in range(0, CTX_TILES, 4):
                groups.append([(ctx[:, b, t * P:t * P + tile_rows(t)], b * CTX_TILES + t)
                               for t in range(first, min(first + 4, CTX_TILES))])
        return jobs, groups

    eps5, eps6 = sb("eps5", [P, 1]), sb("eps6", [P, 1])
    eps_col = {1e-5: eps5[:, :], 1e-6: eps6[:, :]}

    nc.vector.memset(eps5[:, :], 1e-5)
    nc.vector.memset(eps6[:, :], 1e-6)
    load_constants()
    with nc.Fori(0, BATCHES // PAIR) as pair:
        first_turn = turn[0]
        load_pair(pair)
        layer_norm(1e-5, lambda b: (bias("0g"), bias("0b")))
        project_prototypes()
        prototype_attention()
        route()
        hidden_of_experts()
        mix_experts()
        if last_stage >= 1:
            layer_norm(1e-5, lambda b: (lnw[:, 0, b, 0:1], lnw[:, 0, b, 1:2]))
            project_heads(*self_jobs(normed[:, :], 1), w("1sv"))
            attention("self", bias("1sv"))
            add_to_x([(w("1so"), attn[:, :])], bias("1so"))
        if last_stage >= 2:
            project_heads(*cross_jobs(x[:, :], 1), w("1cv"))
            attention("cross", bias("1cv"))
            add_to_x([(w("1co"), attn[:, :])], bias("1co"))
        if last_stage >= 3:
            layer_norm(1e-5, lambda b: (lnw[:, 1, b, 0:1], lnw[:, 1, b, 1:2]))
            dense([([(w("1f1", i), normed[:, :])], hidden[:, i, :], ACT.Gelu, bias("1f1", i)) for i in range(4)])
            add_to_x([(w("1f2", i), hidden[:, i, :]) for i in range(4)], bias("1f2"))
        if last_stage >= 4:
            layer_norm(1e-5, lambda b: (modc("2ln1", b, 0), modc("2ln1", b, 1)))
            project_heads(*self_jobs(normed[:, :], 2, rope=True), w("2sv"), rope=True)
            attention("self", None)
            add_to_x([(w("2so"), attn[:, :])], None)
        if last_stage >= 5:
            layer_norm(1e-5, lambda b: (modc("2ln2", b, 0), modc("2ln2", b, 1)))
            project_heads(*cross_jobs(normed[:, :], 2, rope=True), w("2cv"), rope=True, load_rope=True)
            attention("cross", None)
            add_to_x([(w("2co"), attn[:, :])], None)
            layer_norm(1e-5, lambda b: (modc("2ln3", b, 0), modc("2ln3", b, 1)))
            dense([([(w("2f1", i), normed[:, :])], hidden[:, i, :], ACT.Gelu, bias("2f1", i)) for i in range(4)])
            add_to_x([(w("2f2", i), hidden[:, i, :]) for i in range(4)], bias("2f2"))
        if last_stage >= 6:
            layer_norm(1e-6, lambda b: (modc("3ada", b, 1), modc("3ada", b, 0)))
            project_heads(*self_jobs(normed[:, :], 3), w("3sv"))
            attention("window", bias("3sv"))
            add_to_x([(w("3so"), attn[:, :])], bias("3so"), lambda b: modc("3ada", b, 2))
        if last_stage >= 7:
            layer_norm(1e-6, lambda b: (modc("3ada", b, 4), modc("3ada", b, 3)))
            project_heads(*cross_jobs(normed[:, :], 3), w("3cv"))
            top_attention(bias("3cv"))
            add_to_x([(w("3co"), attn[:, :])], bias("3co"), lambda b: modc("3ada", b, 5))
        if last_stage >= 8:
            layer_norm(1e-6, lambda b: (modc("3ada", b, 7), modc("3ada", b, 6)))
            swiglu()
            add_to_x([(w("3f2", i), hidden[:, i, :]) for i in range(4)], bias("3f2"), lambda b: modc("3ada", b, 8))
        store_pair(pair)
        even_out(first_turn)


def _rows(a, k):
    a = np.asarray(a)
    return a.reshape(k, D, -1).transpose(1, 0, 2).reshape(D, -1)


def pack(i):
    g = {k: np.asarray(v) for k, v in i.items()}
    L0, L1, L2, L3 = (lambda n, k=k: g[f"L{k}_xcond_{n}"] for k in range(4))
    e1 = L0("e_w1")
    blocks = {
        "0q": L0("Wq"), "0k": L0("Wk"), "0v": L0("Wv"), "0out": L0("out_w"), "0gate2": L0("gate_w2"),
        "0gate1": _rows(L0("gate_w1")[:2 * D], 2),
        "0e1": np.concatenate([_rows(e1[e, :2 * D], 2) for e in range(3)], 1),
        "0e2": np.concatenate([_rows(L0("e_w2")[e], 2) for e in range(3)], 1),
        "0router": _rows(L0("router_W")[:2 * D], 2),
        "1sq": L1("sa_qw")[:, PERM], "1sk": L1("sa_kw")[:, PERM], "1sv": L1("sa_vw"), "1so": L1("sa_ow"),
        "1cq": L1("ca_qw")[:, PERM], "1ck": L1("ca_kw")[:, PERM], "1cv": L1("ca_vw"), "1co": L1("ca_ow"),
        "1f1": L1("ffn_w1"), "1f2": _rows(L1("ffn_w2"), 4),
        "2sq": L2("qkv_w")[:D].T[:, PERM], "2sqr": L2("qkv_w")[:D].T[:, ROT],
        "2sk": L2("qkv_w")[D:2 * D].T[:, PERM], "2skr": L2("qkv_w")[D:2 * D].T[:, ROT],
        "2sv": L2("qkv_w")[2 * D:].T, "2so": L2("sa_out_w").T,
        "2cq": L2("q_w").T[:, PERM], "2cqr": L2("q_w").T[:, ROT],
        "2ck": L2("k_w").T[:, PERM], "2ckr": L2("k_w").T[:, ROT],
        "2cv": L2("v_w").T, "2co": L2("ca_out_w").T, "2f1": L2("ffn_w1").T, "2f2": _rows(L2("ffn_w2").T, 4),
        "3sq": L3("w_qkv")[:, :D][:, PERM], "3sk": L3("w_qkv")[:, D:2 * D][:, PERM], "3sv": L3("w_qkv")[:, 2 * D:],
        "3so": L3("w_so"), "3cq": L3("w_q")[:, PERM], "3ck": L3("w_kv")[:, :D][:, PERM], "3cv": L3("w_kv")[:, D:],
        "3co": L3("w_co"), "3f1": L3("w_m1"), "3f2": _rows(L3("w_m2"), 4),
    }
    W, M, B = weight_plan(), modulation_plan(), bias_plan()
    weights = np.concatenate([blocks[n] for n in W.at], 1)
    cond_blocks = {
        "0gate1": L0("gate_w1")[2 * D:], "0e1": np.concatenate([e1[e, 2 * D:] for e in range(3)], 1),
        "1aff1": L1("aff1_w"), "1aff2": L1("aff2_w"), "2ln1": L2("ln1_w").T, "2ln2": L2("ln2_w").T,
        "2ln3": L2("ln3_w").T, "3ada": L3("w_ada"), "0router": L0("router_W")[2 * D:],
    }
    modw = np.concatenate([cond_blocks[n] for n in M.at], 1)

    def cols(v):
        return np.asarray(v).reshape(-1, D).T

    mod_bias = {
        "0gate1": cols(L0("gate_b1")), "0e1": cols(L0("e_b1")), "1aff1": cols(L1("aff1_b")), "1aff2": cols(L1("aff2_b")),
        "2ln1": cols(L2("ln1_b")), "2ln2": cols(L2("ln2_b")), "2ln3": cols(L2("ln3_b")), "3ada": cols(L3("b_ada")),
        "0router": np.broadcast_to(L0("router_b"), (D, 3)),
    }
    qkv_b, kv_b = L3("b_qkv"), L3("b_kv")
    bias_blocks = {
        "mod": np.concatenate([mod_bias[n] for n in M.at], 1),
        "0g": cols(L0("ln_gamma")), "0b": cols(L0("ln_beta")), "0gate2": cols(L0("gate_b2")), "0out": cols(L0("out_b")),
        "0e2": cols(L0("e_b2")), "1g1": cols(L1("ln1_g")), "1b1": cols(L1("ln1_b")), "1g2": cols(L1("ln2_g")),
        "1b2": cols(L1("ln2_b")), "1sq": cols(L1("sa_qb")[PERM]), "1sk": cols(L1("sa_kb")[PERM]),
        "1sv": cols(L1("sa_vb")), "1so": cols(L1("sa_ob")), "1cq": cols(L1("ca_qb")[PERM]),
        "1ck": cols(L1("ca_kb")[PERM]), "1cv": cols(L1("ca_vb")), "1co": cols(L1("ca_ob")), "1f1": cols(L1("ffn_b1")),
        "1f2": cols(L1("ffn_b2")), "2f1": cols(L2("ffn_b1")), "2f2": cols(L2("ffn_b2")),
        "3sq": cols(qkv_b[:D][PERM]), "3sk": cols(qkv_b[D:2 * D][PERM]), "3sv": cols(qkv_b[2 * D:]),
        "3so": cols(L3("b_so")), "3cq": cols(L3("b_q")[PERM]), "3ck": cols(kv_b[:D][PERM]), "3cv": cols(kv_b[D:]),
        "3co": cols(L3("b_co")), "3f1": cols(L3("b_m1")), "3f2": cols(L3("b_m2")),
    }
    biases = np.concatenate([bias_blocks[n] for n in B.at], 1)

    half = HD // 2
    inv_freq = (np.float32(1.0) / np.float32(10000.0) ** (np.arange(half, dtype=np.float32) / np.float32(half)))
    d_of = np.array([d for _ in range(GROUPS) for d in range(HD) for _ in range(GROUP)])
    ang = (np.arange(CTX, dtype=np.float32)[None, :] * inv_freq.astype(np.float32)[d_of % half][:, None]).astype(np.float32)
    cos = np.cos(ang.astype(np.float64)).astype(np.float32)
    sin = (np.sin(ang.astype(np.float64)) * np.where(d_of < half, -1.0, 1.0)[:, None]).astype(np.float32)
    rope = np.concatenate([cos, sin], 1)
    rolled = np.roll(np.arange(TOK), -SHIFT)
    const = np.concatenate([np.eye(P, dtype=np.float32), cos[:, rolled], sin[:, rolled]], 1)

    pairs = BATCHES // PAIR
    x = np.roll(g["x"], -SHIFT, axis=1).reshape(pairs, N, D).transpose(0, 2, 1)
    ctx = g["ctx_1024"].reshape(pairs, PAIR * CTX, D).transpose(0, 2, 1)
    return {"x": x, "ctx": ctx, "cond": g["cond_1024"].T, "weights": weights, "modw": modw, "biases": biases,
            "const": const, "rope": rope}


def kernel(**inputs):
    import concourse.bacc as bacc
    from concourse.bass_utils import run_bass_kernel_spmd

    nc = bacc.Bacc("TRN2", target_bir_lowering=False, num_devices=1)
    arrays = {f"in_{k}": np.ascontiguousarray(v) for k, v in pack(inputs).items()}
    args = [nc.dram_tensor(k, v.shape, F32, kind="ExternalInput").ap() for k, v in arrays.items()]
    out = nc.dram_tensor("out_0", (BATCHES // PAIR, D, N), F32, kind="ExternalOutput").ap()
    build_program(nc, *args, out)
    r = run_bass_kernel_spmd(nc, [arrays], core_ids=[0])
    got = np.asarray(r.results[0]["out_0"])
    return np.roll(got.transpose(0, 2, 1).reshape(BATCHES, TOK, D), SHIFT, axis=1)
```

```python
import numpy as np

import concourse.bass as bass
from concourse import mybir

F32 = mybir.dt.float32
BF16 = mybir.dt.bfloat16
ALU = mybir.AluOpType
ACT = mybir.ActivationFunctionType
AX = mybir.AxisListType

P = 128
D = 128
HEADS, HD = 16, 8
GROUP = 4
GROUPS = HEADS // GROUP
BATCHES, TOK, CTX = 4, 256, 1601
PAIR = 2
N = PAIR * TOK
CTX_TILES = -(-CTX // P)
SHIFT, WIN = 32, 64
TOPK = 16
SPLIT_ROWS = 9 * HD
SCORE_ROWS = 96
MAX_ROWS = 99
VH = HD + 1
VROW = HEADS * VH + 24
SCALE = float(np.float32(1.0) / np.sqrt(np.float32(HD)))
LOW = -3.0e38

BY_DIM = np.array([(h, d) for d in range(HD) for h in range(HEADS)])
BY_GROUP = np.array([(GROUP * g + j, d) for g in range(GROUPS) for d in range(HD) for j in range(GROUP)])


class Columns:

    def __init__(self):
        self.at, self.n = {}, 0

    def add(self, name, width):
        self.at[name] = (self.n, width)
        self.n += width


def weight_plan():
    w = Columns()
    for name, width in [
        ("0q", D), ("0k", D), ("0v", D), ("0out", D), ("0gate2", D), ("0gate1", 2 * D), ("0e1", 3 * 2 * 2 * D),
        ("0e2", 3 * 2 * D), ("0router", 2 * 3),
        ("1sq", D), ("1sk", D), ("1sv", D), ("1so", D), ("1cq", D), ("1ck", D), ("1cv", D), ("1co", D),
        ("1f1", 4 * D), ("1f2", 4 * D),
        ("2sq", D), ("2sqr", D), ("2sk", D), ("2skr", D), ("2sv", D), ("2so", D),
        ("2cq", D), ("2cqr", D), ("2ck", D), ("2ckr", D), ("2cv", D), ("2co", D), ("2f1", 4 * D), ("2f2", 4 * D),
        ("3sq", D), ("3sk", D), ("3sv", D), ("3so", D), ("3cq", D), ("3ck", D), ("3cv", D), ("3co", D),
        ("3f1", 8 * D), ("3f2", 4 * D),
    ]:
        w.add(name, width)
    return w


def modulation_plan():
    m = Columns()
    for name, chunks in [("0gate1", 1), ("0e1", 6), ("1aff1", 2), ("1aff2", 2), ("2ln1", 2), ("2ln2", 2),
                         ("2ln3", 2), ("3ada", 9)]:
        m.add(name, chunks)
    m.add("0router", 3)
    return m


def bias_plan():
    b = Columns()
    b.add("mod", modulation_plan().n)
    for name, n in [("0g", 1), ("0b", 1), ("0gate2", 1), ("0out", 1), ("0e2", 3),
                    ("1g1", 1), ("1b1", 1), ("1g2", 1), ("1b2", 1), ("1sq", 1), ("1sk", 1), ("1sv", 1), ("1so", 1),
                    ("1cq", 1), ("1ck", 1), ("1cv", 1), ("1co", 1), ("1f1", 4), ("1f2", 1), ("2f1", 4), ("2f2", 1),
                    ("3sq", 1), ("3sk", 1), ("3sv", 1), ("3so", 1), ("3cq", 1), ("3ck", 1), ("3cv", 1), ("3co", 1),
                    ("3f1", 8), ("3f2", 1)]:
        b.add(name, n)
    return b


class SemaphoreSet:

    def __init__(self, nc, name, n):
        self.sems = [nc.alloc_semaphore(f"{name}{i}") for i in range(n)]
        self.range = range(self.sems[0].num, self.sems[0].num + n)
        self.used = 0

    def take(self, n=1):
        got = self.sems[self.used:self.used + n]
        self.used += n
        return got[0] if n == 1 else got


def build_program(nc, x_in, ctx_in, cond_in, weights_in, modw_in, bias_in, const_in, rope_in, out, last_stage=99):
    W, M, B = weight_plan(), modulation_plan(), bias_plan()

    def sb(name, shape, dt=F32):
        return nc.alloc_sbuf_tensor(name, shape, dt)

    weights = sb("weights", [P, W.n])
    biases = sb("biases", [P, B.n])
    ident = sb("ident", [P, P])
    ident16 = sb("ident16", [P, P], BF16)
    mean_w = sb("mean_w", [P, P])
    ones = sb("ones", [P, P])
    rope_tok = sb("rope_tok", [P, 2, TOK])
    mod_all = sb("mod_all", [P, BATCHES, M.n])
    x = sb("x", [P, N])
    normed = sb("normed", [P, N])
    tmp_a = sb("tmp_a", [P, N])
    tmp_b = sb("tmp_b", [P, N])
    ctx = sb("ctx", [P, PAIR, CTX])
    mod = sb("mod", [P, PAIR, M.n])
    lnw = sb("lnw", [P, 2, PAIR, 2])
    q_parts = sb("q_parts", [P, 3, N], BF16)
    k_parts = sb("k_parts", [P, 3, PAIR * CTX], BF16)
    q_stack = sb("q_stack", [P, HEADS, N], BF16)
    k_room = sb("k_room", [P, 3 * GROUP * CTX], BF16)
    values = sb("values", [P, PAIR * CTX_TILES, VROW])
    attn_tok = sb("attn_tok", [P, PAIR, 2, D])
    attn = sb("attn", [P, N])
    heads_out = sb("heads_out", [P, TOK])
    maxima = sb("maxima", [P, 2, 16])
    max8 = sb("max8", [P, 8])
    neg_f = sb("neg_f", [P, 8])
    neg_parts = sb("neg_parts", [P, 2, 2, 3, GROUP], BF16)
    neg_rows = [sb(f"neg_rows{i}", [24, P], BF16) for i in range(2)]
    sums_inv = sb("sums_inv", [P, 2, GROUP])
    deviation = sb("deviation", [P, PAIR, TOK // P])
    shared = sb("shared", [P, 9920])
    slots = [k_room[:, i * GROUP * CTX:(i + 1) * GROUP * CTX] for i in range(3)]
    slots.append(shared[:, 9920 - GROUP * CTX // 2:9920].bitcast(BF16))
    k_stack = [v.rearrange("p (j n) -> p j n", j=GROUP) for v in slots]
    k_tokens = k_room[:, 0:HEADS * N].rearrange("p (h n) -> p h n", h=HEADS)

    def part(first, shape):
        size = int(np.prod(shape))
        v = shared[:, first:first + size]
        if len(shape) == 2:
            v = v.rearrange("p (a b) -> p a b", a=shape[0])
        if len(shape) == 3:
            v = v.rearrange("p (a b c) -> p a b c", a=shape[0], b=shape[1])
        return v

    modw = shared[:, 0:M.at["0router"][0] * D + 3]
    condT = shared[:, 29 * D:29 * D + BATCHES]
    condS = shared[:, 29 * D + BATCHES:29 * D + 2 * BATCHES]
    split_f = part(0, [2, 512])
    split_t = part(1024, [2, 512])
    split_r = part(2048, [2, 512])
    rope_ctx = part(3072, [2, CTX])
    probs = [part(1024 * i, [GROUP, TOK]) for i in range(4)]
    hidden = part(0, [7, N])
    router_p = part(7 * N, [3, N])
    k0 = part(0, [PAIR, CTX])
    v0 = part(PAIR * CTX, [PAIR * CTX_TILES, D])
    probs0 = [part(PAIR * CTX + PAIR * CTX_TILES * D + TOK * i, [TOK]) for i in range(3)]
    neg_row0 = shared[0:1, 7424:7424 + N]
    untaken = [part(CTX * i, [CTX]) for i in range(2)]
    weight_e = [part(CTX * (2 + i), [CTX]) for i in range(2)]
    probs_t = [part(4 * CTX + CTX_TILES * P * i, [CTX_TILES, P]) for i in range(2)]
    best = sb("best", [P, 2, TOPK + 1])

    ps = nc.alloc_psum_tensor("ps", [P, 8, 512], F32)

    def w(name, i=0, n=1):
        at, width = W.at[name]
        return weights[:, at + i * D:at + (i + n) * D]

    def bias(name, i=0):
        at = B.at[name][0] + i
        return biases[:, at:at + 1]

    def modc(name, b, i=0):
        at = M.at[name][0] + i
        return mod[:, b, at:at + 1]

    sets = [SemaphoreSet(nc, "even", 28), SemaphoreSet(nc, "odd", 28)]
    turn = [0]
    carried = SemaphoreSet(nc, "carried", 9)
    q_loaded = carried.take()
    k_terms, k_copies = carried.take(4), carried.take(4)

    def semaphores():
        s, other = sets[turn[0] % 2], sets[1 - turn[0] % 2]
        turn[0] += 1
        s.used = 0
        return s, other.range

    def tile_rows(t):
        return min(P, CTX - t * P)

    def load_constants():
        s, other = semaphores()
        loaded, cond_loaded, filled, silu_done, mod_ready, biased, step = [s.take() for _ in range(7)]
        with nc.Block() as block:
            @block.sync
            def _(sp):
                sp.sem_clear(other)
                sp.dma_start(modw, modw_in).then_inc(cond_loaded, 16)
                sp.dma_start(condT, cond_in).then_inc(cond_loaded, 16)
                sp.dma_start(biases[:, :], bias_in).then_inc(cond_loaded, 16)
                sp.dma_start(ident[:, :], const_in[:, 0:P]).then_inc(loaded, 16)
                sp.dma_start(rope_tok[:, :, :], const_in[:, P:P + 2 * TOK].rearrange("p (a b) -> p a b", a=2)) \
                    .then_inc(loaded, 16)
                sp.dma_start(weights[:, :], weights_in).then_inc(loaded, 16)
                sp.wait_ge(loaded, 48)

            @block.gpsimd
            def _(pool):
                pool.memset(q_stack[:, :, :], 0.0).then_inc(filled, 1)
                pool.wait_ge(filled, 1)
                pool.memset(k_room[0:96, :], 0.0).then_inc(filled, 1)
                pool.wait_ge(filled, 2)
                pool.memset(k_room[96:128, :], 1.0).then_inc(filled, 1)
                pool.wait_ge(filled, 3)
                pool.memset(values[:, :, :], 1.0).then_inc(filled, 1)

            @block.vector
            def _(dve):
                dve.memset(mean_w[:, :], 1.0 / D)
                dve.memset(ones[:, :], 1.0)
                dve.wait_ge(loaded, 48)
                dve.tensor_copy(ident16[:, :], ident[:, :])
                dve.wait_ge(mod_ready, 1)
                dve.wait_ge(cond_loaded, 48)
                m_view = ps[:, 0, 0:M.n * BATCHES].rearrange("p (c b) -> p b c", b=BATCHES)
                b_view = biases[:, 0:M.n].unsqueeze(1).to_broadcast([P, BATCHES, M.n])
                dve.tensor_tensor(mod_all[:, :, :], m_view, b_view, ALU.add).then_inc(biased, 1)

            @block.scalar
            def _(act):
                act.wait_ge(cond_loaded, 48)
                act.activation(condS, condT, ACT.Silu).then_inc(silu_done, 1)

            @block.tensor
            def _(pe):
                pe.wait_ge(cond_loaded, 48)
                pe.wait_ge(silu_done, 1)
                for c in range(M.n):
                    router = c >= M.at["0router"][0]
                    ada = M.at["3ada"][0] <= c < M.at["3ada"][0] + 9
                    if router:
                        e = M.at["0router"][0] * D + c - M.at["0router"][0]
                        lhs = modw[:, e:e + 1].to_broadcast([P, P])
                    else:
                        lhs = modw[:, c * D:(c + 1) * D]
                    mm = pe.matmul(ps[:, 0, c * BATCHES:(c + 1) * BATCHES], lhs, condS if ada else condT,
                                   start=True, stop=True)
                mm.then_inc(mod_ready, 1)

    def load_pair(pair):
        s, other = semaphores()
        loaded, copied, made = s.take(), s.take(), s.take()
        with nc.Block() as block:
            @block.sync
            def _(sp):
                sp.sem_clear(other)
                sp.dma_start(x[:, :], x_in[bass.ds(pair, 1), :, :].rearrange("a p n -> (a p) n")).then_inc(loaded, 16)
                sp.dma_start(ctx[:, :, :].rearrange("p b n -> p (b n)"),
                             ctx_in[bass.ds(pair, 1), :, :].rearrange("a p n -> (a p) n")).then_inc(loaded, 16)
                sp.wait_ge(loaded, 32)

            @block.vector
            def _(dve):
                src = mod_all[:, :, :].rearrange("p b m -> p (b m)")
                dve.tensor_copy(mod[:, :, :].rearrange("p b m -> p (b m)"),
                                src[:, bass.ds(pair * (PAIR * M.n), PAIR * M.n)]).then_inc(copied, 1)
                dve.wait_ge(copied, 1)
                for i, name in enumerate(("1aff1", "1aff2")):
                    for b in range(PAIR):
                        dve.tensor_scalar(lnw[:, i, b, 0:1], modc(name, b, 0), bias(f"1g{i + 1}"), None, ALU.mult)
                        dve.scalar_tensor_tensor(lnw[:, i, b, 1:2], modc(name, b, 0), bias(f"1b{i + 1}"),
                                                 modc(name, b, 1), ALU.mult, ALU.add)
                at2 = M.at["2ln1"][0]
                g2 = mod[:, :, at2:at2 + 6:2]
                dve.tensor_scalar(g2, g2, 1.0, None, ALU.add)
                at3 = M.at["3ada"][0]
                g3 = mod[:, :, at3 + 1:at3 + 9:3]
                dve.tensor_scalar(g3, g3, 1.0, None, ALU.add).then_inc(made, 1)

    def even_out(first_turn):
        if (turn[0] - first_turn) % 2:
            s, other = semaphores()
            with nc.Block() as block:
                @block.sync
                def _(sp):
                    sp.sem_clear(other)

    def store_pair(pair):
        s, other = semaphores()
        stored = s.take()
        with nc.Block() as block:
            @block.sync
            def _(sp):
                sp.sem_clear(other)
                sp.dma_start(out[bass.ds(pair, 1), :, :].rearrange("a p n -> (a p) n"), x[:, :]).then_inc(stored, 16)
                sp.wait_ge(stored, 16)

    def layer_norm(eps, affine):
        s, other = semaphores()
        (mean_ready, centred, squared, var_ready, root_done, inverted, spread, scaled, done,
         table_loaded) = [s.take() for _ in range(10)]
        mean = [ps[:, b, 0:TOK] for b in range(PAIR)]
        factor = [ps[:, 4 + b, 0:TOK] for b in range(PAIR)]
        cols = [slice(b * TOK, (b + 1) * TOK) for b in range(PAIR)]
        tiles = TOK // P
        with nc.Block() as block:
            @block.sync
            def _(sp):
                sp.sem_clear(other)

            @block.tensor
            def _(pe):
                for b in range(PAIR):
                    pe.matmul(mean[b], mean_w[:, :], x[:, cols[b]], start=True, stop=True).then_inc(mean_ready, 1)
                for b in range(PAIR):
                    pe.wait_ge(squared, b + 1)
                    for i in range(tiles):
                        at = b * TOK + i * P
                        mm = pe.matmul(ps[:, 2 + b, i:i + 1], tmp_b[:, at:at + P], mean_w[:, 0:1], start=True, stop=True)
                    mm.then_inc(var_ready, 1)
                for b in range(PAIR):
                    pe.wait_ge(inverted, b + 1)
                    for i in range(tiles):
                        mm = pe.matmul(factor[b][:, i * P:(i + 1) * P],
                                       deviation[:, b, i:i + 1].to_broadcast([P, P]), ident[:, :], start=True, stop=True)
                    mm.then_inc(spread, 1)

            @block.scalar
            def _(act):
                act.activation(max8[:, 0:1], eps_col[eps], ACT.Sqrt).then_inc(table_loaded, 1)
                for b in range(PAIR):
                    act.wait_ge(centred, b + 1)
                    act.activation(tmp_b[:, cols[b]], tmp_a[:, cols[b]], ACT.Square).then_inc(squared, 1)
                for b in range(PAIR):
                    act.wait_ge(var_ready, b + 1)
                    act.activation(deviation[:, b, :], ps[:, 2 + b, 0:tiles], ACT.Sqrt, bias=eps_col[eps]) \
                        .then_inc(root_done, 1)

            @block.vector
            def _(dve):
                for b in range(PAIR):
                    dve.wait_ge(mean_ready, b + 1)
                    dve.tensor_tensor(tmp_a[:, cols[b]], x[:, cols[b]], mean[b], ALU.subtract).then_inc(centred, 1)
                for b in range(PAIR):
                    dve.wait_ge(root_done, b + 1)
                    dve.reciprocal(deviation[:, b, :], deviation[:, b, :]).then_inc(inverted, 1)
                dve.wait_ge(centred, PAIR)
                for b in range(PAIR):
                    scale, shift = affine(b)
                    dve.wait_ge(spread, b + 1)
                    dve.scalar_tensor_tensor(tmp_a[:, cols[b]], tmp_a[:, cols[b]], scale, factor[b], ALU.mult, ALU.mult) \
                        .then_inc(scaled, 1)
                for b in range(PAIR):
                    scale, shift = affine(b)
                    dve.wait_ge(scaled, b + 1)
                    dve.tensor_scalar(normed[:, cols[b]], tmp_a[:, cols[b]], shift, None, ALU.add).then_inc(done, 1)

    def dense(jobs):
        s, other = semaphores()
        product_ready, emptied = s.take(), s.take()
        with nc.Block() as block:
            @block.sync
            def _(sp):
                sp.sem_clear(other)

            @block.tensor
            def _(pe):
                for i, (terms, dst, func, b) in enumerate(jobs):
                    if i >= 4:
                        pe.wait_ge(emptied, i - 3)
                    for k, (lhs, rhs) in enumerate(terms):
                        mm = pe.matmul(ps[:, i % 4, 0:dst.shape[1]], lhs, rhs, start=(k == 0), stop=(k == len(terms) - 1))
                    mm.then_inc(product_ready, 1)

            @block.scalar
            def _(act):
                for i, (terms, dst, func, b) in enumerate(jobs):
                    act.wait_ge(product_ready, i + 1)
                    act.activation(dst, ps[:, i % 4, 0:dst.shape[1]], func, bias=b).then_inc(emptied, 1)

    def add_to_x(terms, b_col, gate=None, after_attention=False):
        s, other = semaphores()
        product_ready, gated, added = s.take(), s.take(), s.take()
        with nc.Block() as block:
            @block.sync
            def _(sp):
                sp.sem_clear(other)
                if after_attention:
                    sp.sem_clear(carried.range)

            @block.tensor
            def _(pe):
                for k, (lhs, rhs) in enumerate(terms):
                    mm = pe.matmul(ps[:, 0, :], lhs, rhs, start=(k == 0), stop=(k == len(terms) - 1))
                mm.then_inc(product_ready, 1)

            @block.vector
            def _(dve):
                dve.wait_ge(product_ready, 1)
                if gate is None:
                    if b_col is None:
                        dve.tensor_tensor(x[:, :], ps[:, 0, :], x[:, :], ALU.add).then_inc(added, 1)
                    else:
                        dve.scalar_tensor_tensor(x[:, :], ps[:, 0, :], b_col, x[:, :], ALU.add, ALU.add) \
                            .then_inc(added, 1)
                    return
                for b in range(PAIR):
                    cols = slice(b * TOK, (b + 1) * TOK)
                    dve.tensor_scalar(tmp_a[:, cols], ps[:, 0, cols], b_col, gate(b), ALU.add, ALU.mult) \
                        .then_inc(gated, 1)
                dve.wait_ge(gated, PAIR)
                dve.tensor_tensor(x[:, :], tmp_a[:, :], x[:, :], ALU.add).then_inc(added, 1)

    def load_queries(sp):
        for j in range(3):
            for i in range(3):
                sp.dma_start(q_stack[24 * j + 8 * i:24 * j + 8 * i + 8, :, :], q_parts[:, j, :]).then_inc(q_loaded, 16)

    def load_key_parts(sp, u, ring):
        b, g, slot = u // GROUPS, u % GROUPS, u % ring
        for i in range(3):
            sp.dma_start(k_stack[slot][8 * i:8 * i + 8, :, :],
                         k_parts[32 * g:32 * g + 32, i, b * CTX:(b + 1) * CTX]).then_inc(k_terms[slot], 16)

    def copy_key_parts(sp, u, ring):
        copy_rows(sp, u % ring, k_stack[u % ring], u // ring + 1)

    def copy_rows(sp, slot, stack, times):
        sp.wait_ge(k_terms[slot], 48 * times)
        for j in (1, 2):
            sp.dma_start(stack[24 * j:24 * j + 24, :, :], stack[0:24, :, :]).then_inc(k_copies[slot], 16)

    def project_heads(split_jobs, value_jobs, w_v, slots_filled, rope=False, load_rope=False):
        s, other = semaphores()
        (proj_ready, exact_done, hi_done, rest_done, mid_done, lo_done, turned, rotated, v_ready, v_done,
         rope_loaded, filled) = [s.take() for _ in range(12)]
        q_jobs = PAIR if rope else 1
        with nc.Block() as block:
            @block.sync
            def _(sp):
                sp.sem_clear(other)
                if load_rope:
                    sp.dma_start(rope_ctx, rope_in.rearrange("p (a b) -> p a b", a=2)).then_inc(rope_loaded, 16)
                sp.wait_ge(lo_done, q_jobs)
                load_queries(sp)
                if slots_filled is None:
                    sp.wait_ge(lo_done, 2 * q_jobs)
                    for i in range(3):
                        sp.dma_start(k_tokens[8 * i:8 * i + 8, :, :], k_parts[:, i, 0:N]).then_inc(k_terms[0], 16)
                else:
                    sp.wait_ge(lo_done, q_jobs + 4)
                    for u in range(slots_filled):
                        load_key_parts(sp, u, slots_filled)
                if load_rope:
                    sp.wait_ge(rope_loaded, 16)

            @block.gpsimd
            def _(pool):
                if slots_filled == 4:
                    pool.memset(k_stack[3][64:96, :, :], 0.0).then_inc(filled, 1)
                    pool.memset(k_stack[3][96:128, :, :], 1.0).then_inc(filled, 1)

            @block.tensor
            def _(pe):
                v_next = 0

                def value_group(i):
                    if i >= 2:
                        pe.wait_ge(v_done, i - 1)
                    for k, (src, tile) in enumerate(value_jobs[i]):
                        mm = pe.matmul(ps[0:src.shape[1], 4 + i % 2, k * D:(k + 1) * D], src, w_v, start=True, stop=True)
                    mm.then_inc(v_ready, 1)

                for c, (src, wk, wr, b, cos, sin, dst) in enumerate(split_jobs):
                    n = src.shape[1]
                    if c >= 2:
                        if rope:
                            pe.wait_ge(turned, 2 * (c - 1))
                        else:
                            pe.wait_ge(exact_done, 2 * (c - 1))
                    mm = pe.matmul(ps[:, c % 2, 0:n], wk, src, start=True, stop=True)
                    if rope:
                        mm = pe.matmul(ps[:, 2 + c % 2, 0:n], wr, src, start=True, stop=True)
                    mm.then_inc(proj_ready, 1)
                    if v_next < len(value_jobs):
                        value_group(v_next)
                        v_next += 1
                while v_next < len(value_jobs):
                    value_group(v_next)
                    v_next += 1

            @block.scalar
            def _(act):
                v_next = 0

                def value_group(i):
                    act.wait_ge(v_ready, i + 1)
                    jobs = value_jobs[i]
                    rows, tile = jobs[0][0].shape[1], jobs[0][1]
                    dst = values[0:rows, tile:tile + len(jobs), 0:HEADS * VH] \
                        .rearrange("p t (h c) -> p t h c", c=VH)[:, :, :, 0:HD]
                    src = ps[0:rows, 4 + i % 2, 0:len(jobs) * D].rearrange("p (t h d) -> p t h d", t=len(jobs), d=HD)
                    for k in range(len(jobs)):
                        mm = act.copy(dst[:, k], src[:, k])
                    mm.then_inc(v_done, 1)

                for c, (src, wk, wr, b, cos, sin, dst) in enumerate(split_jobs):
                    n = src.shape[1]
                    if rope:
                        act.wait_ge(rotated, c + 1)
                        act.copy(dst[:, 0, :], split_f[:, c % 2, 0:n]).then_inc(hi_done, 1)
                    else:
                        act.wait_ge(proj_ready, c + 1)
                        if c >= 2:
                            act.wait_ge(rest_done, c - 1)
                        act.activation(split_f[:, c % 2, 0:n], ps[:, c % 2, 0:n], ACT.Identity, bias=b) \
                            .then_inc(exact_done, 1)
                        act.activation(dst[:, 0, :], ps[:, c % 2, 0:n], ACT.Identity, bias=b).then_inc(exact_done, 1)
                    if v_next < len(value_jobs):
                        value_group(v_next)
                        v_next += 1
                while v_next < len(value_jobs):
                    value_group(v_next)
                    v_next += 1

            @block.vector
            def _(dve):
                if load_rope:
                    dve.wait_ge(rope_loaded, 16)
                for c, (src, wk, wr, b, cos, sin, dst) in enumerate(split_jobs):
                    n = src.shape[1]
                    exact, turn_, rest = split_f[:, c % 2, 0:n], split_t[:, c % 2, 0:n], split_r[:, c % 2, 0:n]
                    if rope:
                        dve.wait_ge(proj_ready, c + 1)
                        dve.tensor_tensor(exact, ps[:, c % 2, 0:n], cos, ALU.mult).then_inc(turned, 1)
                        dve.tensor_tensor(turn_, ps[:, 2 + c % 2, 0:n], sin, ALU.mult).then_inc(turned, 1)
                        dve.wait_ge(turned, 2 * (c + 1))
                        dve.tensor_tensor(exact, exact, turn_, ALU.add).then_inc(rotated, 1)
                        dve.wait_ge(hi_done, c + 1)
                    else:
                        dve.wait_ge(exact_done, 2 * (c + 1))
                    dve.tensor_tensor(rest, exact, dst[:, 0, :], ALU.subtract).then_inc(rest_done, 1)
                    dve.wait_ge(rest_done, c + 1)
                    dve.tensor_copy(dst[:, 1, :], rest).then_inc(mid_done, 1)
                    dve.wait_ge(mid_done, c + 1)
                    dve.tensor_tensor(dst[:, 2, :], rest, dst[:, 1, :], ALU.subtract).then_inc(lo_done, 1)

    HALF = (CTX + 1) // 2

    def attention(kind, v_bias):
        s, other = semaphores()
        cross = kind == "cross"
        tiles = CTX_TILES if cross else 2
        units = PAIR * GROUPS
        steps = units * tiles
        neg_loaded = s.take(2)
        (st_ready, exp_done, pv_done, a_ready, max_done, small, neg_ready, neg_turned, rows_ready,
         o_copied, o_turned, normalised, all_turned, inverted, cleared) = [s.take() for _ in range(15)]
        chunks = {"cross": 16, "self": 2, "window": 1}[kind]
        smalls = 4 if cross else 3
        keys_of = tile_rows if cross else (lambda t: P)
        lead = {"cross": 21, "self": 6, "window": 4}[kind]
        all_chunks = units * chunks
        first_chunk = [min(all_chunks, lead + round(chunks * n / tiles)) for n in range(steps + 1)]

        def maxima_turned(n):
            first, last = (0, lead) if n < 0 else (first_chunk[n], first_chunk[n + 1])
            got = [c // chunks - 1 for c in range(first, last) if c % chunks == min(1, chunks - 1) and c >= chunks]
            if n >= 1 and last == all_chunks and first < all_chunks:
                got.append(units - 1)
            return got

        def key(rows, u, j, at, n):
            b, g = u // GROUPS, u % GROUPS
            if cross:
                return k_stack[u % 4][0:rows, j, at:at + n]
            return k_tokens[0:rows, 4 * g + j, b * TOK + at:b * TOK + at + n]

        def query(rows, u, j, at, n):
            b, g = u // GROUPS, u % GROUPS
            return q_stack[0:rows, 4 * g + j, b * TOK + at:b * TOK + at + n]

        with nc.Block() as block:
            @block.sync
            def _(sp):
                sp.sem_clear(other)

                def rows_out(u):
                    b, g = u // GROUPS, u % GROUPS
                    sp.wait_ge(rows_ready, u + 1)
                    for qt in range(2):
                        sp.dma_start(q_stack[96:99, 4 * g:4 * g + 4, b * TOK + qt * P:b * TOK + (qt + 1) * P],
                                     neg_rows[u % 2][12 * qt:12 * qt + 12, :]).then_inc(neg_loaded[u % 2], 16)

                if cross:
                    for u in range(4):
                        copy_key_parts(sp, u, 4)
                else:
                    copy_rows(sp, 0, k_tokens, 1)
                for u in range(units):
                    rows_out(u)
                    if cross and 1 <= u < units - 3:
                        sp.wait_ge(st_ready, 2 * tiles * u)
                        load_key_parts(sp, u + 3, 4)
                        copy_key_parts(sp, u + 3, 4)

            @block.tensor
            def _(pe):
                turned_so_far, heads_turned = [0], [0]

                def phase_a(n):
                    u, c = n // chunks, n % chunks
                    if cross and c == 0:
                        pe.wait_ge(k_copies[u % 4], 32 * (u // 4 + 1))
                    if n >= 2:
                        pe.wait_ge(max_done, n - 1)
                    bank = 2 * (n % 2)
                    if cross:
                        r, half = c // 2, c % 2
                        j, qt = r // 2, r % 2
                        for col in range(0, HALF - half, 512):
                            width = min(512, HALF - half - col)
                            mm = pe.matmul(ps[:, bank + col // 512, 0:width], query(SCORE_ROWS, u, j, qt * P, P),
                                           key(SCORE_ROWS, u, j, half * HALF + col, width), start=True, stop=True)
                    elif kind == "self":
                        for i in range(4):
                            j, qt = (4 * c + i) // 2, i % 2
                            mm = pe.matmul(ps[:, bank + i // 2, (i % 2) * TOK:(i % 2 + 1) * TOK],
                                           query(SCORE_ROWS, u, j, qt * P, P), key(SCORE_ROWS, u, j, 0, TOK),
                                           start=True, stop=True)
                    else:
                        for r in range(8):
                            j, qt = r // 2, r % 2
                            for h in range(2):
                                at = qt * P + h * WIN
                                mm = pe.matmul(ps[h * WIN:(h + 1) * WIN, bank, r * WIN:(r + 1) * WIN],
                                               query(SCORE_ROWS, u, j, at, WIN), key(SCORE_ROWS, u, j, at, WIN),
                                               start=True, stop=True)
                    mm.then_inc(a_ready, 1)

                def turn_maxima(u):
                    pe.wait_ge(neg_ready, u + 1)
                    if u >= 1:
                        pe.wait_ge(rows_ready, u)
                    if heads_turned[0]:
                        pe.wait_ge(normalised, heads_turned[0])
                    turned_so_far[0] = u + 1
                    pe.transpose(ps[0:24, 7, 0:P // 2].bitcast(BF16),
                                 neg_parts[:, u % 2, :, :, :].rearrange("p a b c -> p (a b c)"),
                                 ident16[:, :]).then_inc(neg_turned, 1)

                def scores_t(n):
                    u, t = n // tiles, n % tiles
                    if t == 0:
                        pe.wait_ge(neg_loaded[u % 2], 32 * (u // 2 + 1))
                    rows = keys_of(t)
                    for hp in range(2):
                        if n >= 1:
                            pe.wait_ge(exp_done, 2 * n - 1 + hp)
                        for i in range(2):
                            j = 2 * hp + i
                            if kind == "window":
                                for h in range(2):
                                    at = t * P + h * WIN
                                    mm = pe.matmul(ps[h * WIN:(h + 1) * WIN, 4 + hp, i * WIN:(i + 1) * WIN],
                                                   key(MAX_ROWS, u, j, at, WIN), query(MAX_ROWS, u, j, at, WIN),
                                                   start=True, stop=True)
                            else:
                                mm = pe.matmul(ps[0:rows, 4 + hp, i * TOK:(i + 1) * TOK],
                                               key(MAX_ROWS, u, j, t * P, rows), query(MAX_ROWS, u, j, 0, TOK),
                                               start=True, stop=True)
                        mm.then_inc(st_ready, 1)

                def weighted(n):
                    u, t = n // tiles, n % tiles
                    b, g = u // GROUPS, u % GROUPS
                    rows = keys_of(t)
                    pe.wait_ge(exp_done, 2 * (n + 1))
                    if t == 0 and u >= 1:
                        pe.wait_ge(o_copied, u)
                    for j in range(4):
                        lhs = values[0:rows, b * tiles + t, (4 * g + j) * VH:(4 * g + j) * VH + 32]
                        if kind == "window":
                            mm = pe.matmul(ps[32 * j:32 * j + 32, 6, t * P:(t + 1) * P], lhs,
                                           probs[n % 4][:, j, 0:P], start=True, stop=True)
                        else:
                            mm = pe.matmul(ps[32 * j:32 * j + 32, 6, 0:TOK], lhs, probs[n % 4][0:rows, j, :],
                                           start=(t == 0), stop=(t == tiles - 1))
                    mm.then_inc(pv_done, 1)

                def turn_heads(u):
                    pe.wait_ge(o_copied, u + 1)
                    pe.wait_ge(rows_ready, turned_so_far[0])
                    if u >= 1:
                        pe.wait_ge(normalised, u)
                    heads_turned[0] = u + 1
                    for qt in range(2):
                        mm = pe.transpose(ps[:, 7, TOK + qt * P:TOK + (qt + 1) * P], heads_out[:, qt * P:(qt + 1) * P],
                                          ident[:, :])
                    mm.then_inc(o_turned, 1)

                pe.wait_ge(q_loaded, 144)
                if not cross:
                    pe.wait_ge(k_copies[0], 32)
                for c in range(lead):
                    phase_a(c)
                    if c >= chunks and c % chunks == min(1, chunks - 1):
                        turn_maxima(c // chunks - 1)
                for n in range(steps + 2):
                    u, t = n // tiles, n % tiles
                    if n < steps:
                        scores_t(n)
                    if n > tiles and n % tiles == 2 % tiles:
                        turn_heads((n - 2) // tiles - 1)
                    if n < steps:
                        for c in range(first_chunk[n], first_chunk[n + 1]):
                            phase_a(c)
                        for v in maxima_turned(n):
                            turn_maxima(v)
                    if n >= 2:
                        weighted(n - 2)
                turn_heads(units - 1)
                pe.wait_ge(normalised, units)
                for i in range(2 * PAIR):
                    mm = pe.transpose(ps[:, 0, i * P:(i + 1) * P], attn_tok[:, i // 2, i % 2, :], ident[:, :])
                mm.then_inc(all_turned, 1)

            @block.vector
            def _(dve):
                def maxima_of(n):
                    u, c = n // chunks, n % chunks
                    bank = 2 * (n % 2)
                    dve.wait_ge(a_ready, n + 1)
                    if cross:
                        src = ps[:, bank:bank + 2, :].rearrange("p a b -> p (a b)")[:, 0:HALF - c % 2]
                        dst = maxima[:, u % 2, c:c + 1]
                    elif kind == "self":
                        src = ps[:, bank:bank + 2, :].rearrange("p a (b k) -> p (a b) k", b=2)
                        dst = maxima[:, u % 2, 4 * c:4 * c + 4]
                    else:
                        src = ps[:, bank, :].rearrange("p (r k) -> p r k", r=8)
                        dst = maxima[:, u % 2, 0:8]
                    dve.tensor_reduce(dst, src, AX.X, ALU.max).then_inc(max_done, 1)
                    if c == chunks - 1:
                        split_maxima(u)

                def split_maxima(u):
                    dve.wait_ge(max_done, (u + 1) * chunks)
                    m, k, parts = maxima[:, u % 2, 0:8], u * smalls, neg_parts[:, u % 2, :, :, :]
                    if cross:
                        m = max8[:, :]
                        dve.tensor_reduce(m, maxima[:, u % 2, :].rearrange("p (r h) -> p r h", h=2), AX.X, ALU.max) \
                            .then_inc(small, 1)
                        k += 1
                        dve.wait_ge(small, k)
                    if u >= 2:
                        dve.wait_ge(neg_turned, u - 1)
                    m = m.rearrange("p (j t) -> p t j", t=2)
                    rest = neg_f[:, :].rearrange("p (t j) -> p t j", t=2)
                    dve.tensor_scalar(parts[:, :, 0, :], m, -1.0, None, ALU.mult).then_inc(small, 1)
                    dve.wait_ge(small, k + 1)
                    dve.scalar_tensor_tensor(rest, m, -1.0, parts[:, :, 0, :], ALU.mult, ALU.subtract) \
                        .then_inc(small, 1)
                    dve.wait_ge(small, k + 2)
                    dve.tensor_copy(parts[:, :, 1, :], rest).then_inc(small, 1)
                    dve.wait_ge(small, k + 3)
                    dve.tensor_tensor(parts[:, :, 2, :], rest, parts[:, :, 1, :], ALU.subtract).then_inc(neg_ready, 1)

                def heads_to_tokens(u):
                    b, g = u // GROUPS, u % GROUPS
                    dve.wait_ge(o_turned, u + 1)
                    got = ps[:, 7, TOK:2 * TOK].rearrange("p (t j c) -> p t j c", t=2, j=GROUP)
                    dve.reciprocal(sums_inv[:, :, :], got[:, :, :, HD]).then_inc(inverted, 1)
                    dve.wait_ge(inverted, u + 1)
                    dst = attn_tok[:, b, :, 32 * g:32 * g + 32].rearrange("p t (j d) -> p t j d", j=GROUP)
                    inv = sums_inv[:, :, :].unsqueeze(3).to_broadcast([P, 2, GROUP, HD])
                    dve.tensor_tensor(dst, got[:, :, :, 0:HD], inv, ALU.mult).then_inc(normalised, 1)

                if kind == "window":
                    for i in range(4):
                        dve.memset(probs[i][:, :, 0:P], 0.0).then_inc(cleared, 1)
                for c in range(lead):
                    maxima_of(c)
                for n in range(steps + 2):
                    if n > tiles and n % tiles == 2 % tiles:
                        heads_to_tokens((n - 2) // tiles - 1)
                    if n < steps:
                        for c in range(first_chunk[n], first_chunk[n + 1]):
                            maxima_of(c)
                heads_to_tokens(units - 1)

            @block.scalar
            def _(act):
                def rows_of_maxima(u):
                    act.wait_ge(neg_turned, u + 1)
                    if u >= 2:
                        act.wait_ge(neg_loaded[u % 2], 32 * (u // 2))
                    act.copy(neg_rows[u % 2][:, :], ps[0:24, 7, 0:P // 2].bitcast(BF16)).then_inc(rows_ready, 1)

                def copy_heads(u):
                    act.wait_ge(pv_done, (u + 1) * tiles)
                    if u >= 1:
                        act.wait_ge(o_turned, u)
                    act.copy(heads_out[:, :], ps[:, 6, 0:TOK]).then_inc(o_copied, 1)

                if kind == "window":
                    act.wait_ge(cleared, 4)
                for u in maxima_turned(-1):
                    rows_of_maxima(u)
                for n in range(steps):
                    u, t = n // tiles, n % tiles
                    rows = keys_of(t)
                    if n >= 4:
                        act.wait_ge(pv_done, n - 3)
                    for hp in range(2):
                        act.wait_ge(st_ready, 2 * n + hp + 1)
                        if kind == "window":
                            for h in range(2):
                                half = slice(h * WIN, (h + 1) * WIN)
                                src = ps[half, 4 + hp, 0:2 * WIN].rearrange("p (j q) -> p j q", j=2)
                                e = act.activation(probs[n % 4][half, 2 * hp:2 * hp + 2, half], src,
                                                   ACT.Exp, scale=SCALE)
                        else:
                            src = ps[0:rows, 4 + hp, :].rearrange("p (j q) -> p j q", j=2)
                            e = act.activation(probs[n % 4][0:rows, 2 * hp:2 * hp + 2, :], src,
                                               ACT.Exp, scale=SCALE)
                        e.then_inc(exp_done, 1)
                    for v in maxima_turned(n):
                        rows_of_maxima(v)
                    if t == 1 and u >= 1:
                        copy_heads(u - 1)
                copy_heads(units - 1)
                act.wait_ge(all_turned, 1)
                b_ap = 0.0 if v_bias is None else v_bias
                act.activation(attn[:, :], ps[:, 0, :], ACT.Identity, bias=b_ap).then_inc(o_copied, 1)

    def top_attention(v_bias):
        s, other = semaphores()
        (s_ready, top8, offset_done, taken8, top16, taken16, e_done, rest_done, weight_done, t_ready, t_copied,
         pv_done, o_copied, o_turned, inv_done, normalised, all_turned) = [s.take() for _ in range(17)]
        units = PAIR * GROUPS
        total = units * 8

        def turned_at(t):
            return ps[:, (4, 5, 7, 4)[t // 4], (t % 4) * P:(t % 4 + 1) * P]

        turned_heads = ps[:, 4, TOK:2 * TOK]
        heads_tok = tmp_a[:, 0:TOK]
        scores = ps[:, 0:4, :].rearrange("p a b -> p (a b)")[:, 0:CTX]

        with nc.Block() as block:
            @block.sync
            def _(sp):
                sp.sem_clear(other)
                for u in range(units):
                    if u >= 3:
                        sp.wait_ge(s_ready, 8 * (u - 2))
                        load_key_parts(sp, u, 3)
                    copy_key_parts(sp, u, 3)

            @block.tensor
            def _(pe):
                def score_tile(i):
                    u, r = i // 8, i % 8
                    b, g, slot, j, qt = u // GROUPS, u % GROUPS, u % 3, r // 2, r % 2
                    if r == 0:
                        pe.wait_ge(k_copies[slot], 32 * (u // 3 + 1))
                    if i >= 1:
                        pe.wait_ge(e_done, i)
                    for col in range(0, CTX, 512):
                        width = min(512, CTX - col)
                        mm = pe.matmul(ps[:, col // 512, 0:width],
                                       q_stack[0:SCORE_ROWS, 4 * g + j, b * TOK + qt * P:b * TOK + (qt + 1) * P],
                                       k_stack[slot][0:SCORE_ROWS, j, col:col + width], start=True, stop=True)
                    mm.then_inc(s_ready, 1)

                def turn_weights(i):
                    pe.wait_ge(weight_done, i + 1)
                    if i >= 1:
                        pe.wait_ge(t_copied, 3 * i)
                    for t in range(12):
                        mm = pe.transpose(turned_at(t), weight_e[i % 2][:, t * P:(t + 1) * P], ident[:, :])
                        if t in (7, 11):
                            mm.then_inc(t_ready, 1)

                def turn_last(i):
                    pe.wait_ge(t_copied, 3 * i + 1)
                    rows = tile_rows(12)
                    mm = pe.transpose(turned_at(12)[0:rows, :], weight_e[i % 2][:, 12 * P:12 * P + rows], ident[:, :])
                    if i % 8 == 2 and i > 8:
                        mm = turn_heads(i // 8 - 1)
                    mm.then_inc(t_ready, 1)

                def weighted(i):
                    u, r = i // 8, i % 8
                    b, g, j, qt = u // GROUPS, u % GROUPS, r // 2, r % 2
                    pe.wait_ge(t_copied, 3 * (i + 1))
                    if r == 0 and u >= 1:
                        pe.wait_ge(o_copied, u)
                    for t in range(CTX_TILES):
                        rows = tile_rows(t)
                        h = 4 * g + j
                        mm = pe.matmul(ps[32 * j:32 * j + 32, 6, qt * P:(qt + 1) * P],
                                       values[0:rows, b * CTX_TILES + t, h * VH:h * VH + 32],
                                       probs_t[i % 2][0:rows, t, :], start=(t == 0), stop=(t == CTX_TILES - 1))
                    mm.then_inc(pv_done, 1)

                def turn_heads(u):
                    pe.wait_ge(o_copied, u + 1)
                    for qt in range(2):
                        mm = pe.transpose(turned_heads[:, qt * P:(qt + 1) * P], heads_out[:, qt * P:(qt + 1) * P],
                                          ident[:, :])
                    return mm

                pe.wait_ge(q_loaded, 144)
                for i in range(total + 3):
                    if i < total:
                        score_tile(i)
                    if 2 <= i < total + 2:
                        turn_weights(i - 2)
                    if i >= 3:
                        weighted(i - 3)
                    if 2 <= i < total + 2:
                        turn_last(i - 2)
                turn_heads(units - 1).then_inc(t_ready, 1)
                pe.wait_ge(normalised, units)
                for i in range(2 * PAIR):
                    mm = pe.transpose(ps[:, 7, i * P:(i + 1) * P], attn_tok[:, i // 2, i % 2, :], ident[:, :])
                mm.then_inc(all_turned, 1)

            @block.vector
            def _(dve):
                def heads_to_tokens(u):
                    b, g = u // GROUPS, u % GROUPS
                    dve.wait_ge(o_turned, u + 1)
                    got = heads_tok.rearrange("p (t j c) -> p t j c", t=2, j=GROUP)
                    dve.reciprocal(sums_inv[:, :, :], got[:, :, :, HD]).then_inc(inv_done, 1)
                    dve.wait_ge(inv_done, u + 1)
                    dst = attn_tok[:, b, :, 32 * g:32 * g + 32].rearrange("p t (j d) -> p t j d", j=GROUP)
                    inv = sums_inv[:, :, :].unsqueeze(3).to_broadcast([P, 2, GROUP, HD])
                    dve.tensor_tensor(dst, got[:, :, :, 0:HD], inv, ALU.mult).then_inc(normalised, 1)

                for i in range(total):
                    top, left = best[:, i % 2, :], untaken[i % 2]
                    dve.wait_ge(s_ready, i + 1)
                    if i >= 2:
                        dve.wait_ge(e_done, i - 1)
                        dve.wait_ge(rest_done, i - 1)
                    dve.max(top[:, 0:8], scores).then_inc(top8, 1)
                    if i >= 2:
                        dve.wait_ge(weight_done, i - 1)
                    dve.wait_ge(top8, i + 1)
                    dve.match_replace(left, top[:, 0:8], scores, LOW).then_inc(taken8, 1)
                    dve.tensor_scalar(top[:, TOPK:TOPK + 1], top[:, 0:1], -SCALE, None, ALU.mult) \
                        .then_inc(offset_done, 1)
                    dve.wait_ge(taken8, i + 1)
                    dve.max(top[:, 8:16], left).then_inc(top16, 1)
                    dve.wait_ge(top16, i + 1)
                    dve.match_replace(left, top[:, 8:16], left, LOW).then_inc(taken16, 1)
                    if i % 8 == 5 and i > 12:
                        heads_to_tokens(i // 8 - 1)
                heads_to_tokens(units - 1)

            @block.scalar
            def _(act):
                def copy_turned(i):
                    rows, slot = tile_rows(12), probs_t[i % 2]
                    act.wait_ge(t_ready, 3 * i + 1)
                    if i >= 2:
                        act.wait_ge(pv_done, i - 1)
                    act.copy(slot[:, 0:8, :], ps[:, 4:6, :].rearrange("p a (t q) -> p (a t) q", t=4)) \
                        .then_inc(t_copied, 1)
                    act.wait_ge(t_ready, 3 * i + 2)
                    act.copy(slot[:, 8:12, :], ps[:, 7, :].rearrange("p (t q) -> p t q", t=4)).then_inc(t_copied, 1)
                    act.wait_ge(t_ready, 3 * i + 3)
                    if i % 8 == 2 and i > 8:
                        copy_turned_heads(i // 8 - 1)
                    act.copy(slot[0:rows, 12, :], turned_at(12)[0:rows, :]).then_inc(t_copied, 1)

                def copy_turned_heads(u):
                    if u >= 1:
                        act.wait_ge(normalised, u)
                    act.copy(heads_tok, turned_heads).then_inc(o_turned, 1)

                def copy_heads(u):
                    act.wait_ge(pv_done, 8 * (u + 1))
                    if u >= 1:
                        act.wait_ge(o_turned, u)
                    act.copy(heads_out[:, :], ps[:, 6, 0:TOK]).then_inc(o_copied, 1)

                for i in range(total + 1):
                    if i < total:
                        top, left = best[:, i % 2, :], untaken[i % 2]
                        act.wait_ge(taken8, i + 1)
                        act.wait_ge(offset_done, i + 1)
                        if i >= 2:
                            act.wait_ge(t_ready, 3 * (i - 1))
                        act.activation(weight_e[i % 2], scores, ACT.Exp, bias=top[:, TOPK:TOPK + 1], scale=SCALE) \
                            .then_inc(e_done, 1)
                        act.wait_ge(taken16, i + 1)
                        act.activation(left, left, ACT.Exp, bias=top[:, TOPK:TOPK + 1], scale=SCALE) \
                            .then_inc(rest_done, 1)
                    if i >= 10 and i % 8 == 2 and i < total:
                        copy_heads(i // 8 - 1)
                    if i >= 1:
                        copy_turned(i - 1)
                copy_heads(units - 1)
                act.wait_ge(t_ready, 3 * total + 1)
                copy_turned_heads(units - 1)
                act.wait_ge(all_turned, 1)
                act.activation(attn[:, :], ps[:, 7, :], ACT.Identity, bias=v_bias).then_inc(o_copied, 1)

            @block.gpsimd
            def _(pool):
                for i in range(total):
                    pool.wait_ge(rest_done, i + 1)
                    pool.wait_ge(e_done, i + 1)
                    pool.tensor_tensor(weight_e[i % 2], weight_e[i % 2], untaken[i % 2], ALU.subtract) \
                        .then_inc(weight_done, 1)

    def project_prototypes():
        jobs = [([(w("0q"), normed[:, :])], tmp_a[:, :])]
        flat = ctx[:, :, :].rearrange("p b n -> p (b n)")
        k_flat = k0.rearrange("p b n -> p (b n)")
        for c in range(0, PAIR * CTX, 512):
            n = min(512, PAIR * CTX - c)
            jobs.append(([(w("0k"), flat[:, c:c + n])], k_flat[:, c:c + n]))
        for b in range(PAIR):
            for t in range(CTX_TILES):
                rows = tile_rows(t)
                jobs.append(([(ctx[:, b, t * P:t * P + rows], w("0v"))], v0[0:rows, b * CTX_TILES + t, :]))
        s, other = semaphores()
        product_ready, act_emptied, dve_emptied = s.take(), s.take(), s.take()
        with nc.Block() as block:
            @block.sync
            def _(sp):
                sp.sem_clear(other)

            @block.tensor
            def _(pe):
                for i, (terms, dst) in enumerate(jobs):
                    if i >= 4:
                        pe.wait_ge(act_emptied if i % 2 == 0 else dve_emptied, (i - 4) // 2 + 1)
                    lhs, rhs = terms[0]
                    pe.matmul(ps[0:dst.shape[0], i % 4, 0:dst.shape[1]], lhs, rhs, start=True, stop=True) \
                        .then_inc(product_ready, 1)

            @block.scalar
            def _(act):
                for i, (terms, dst) in enumerate(jobs):
                    if i % 2 == 0:
                        act.wait_ge(product_ready, i + 1)
                        act.copy(dst, ps[0:dst.shape[0], i % 4, 0:dst.shape[1]]).then_inc(act_emptied, 1)

            @block.vector
            def _(dve):
                for i, (terms, dst) in enumerate(jobs):
                    if i % 2 == 1:
                        dve.wait_ge(product_ready, i + 1)
                        dve.tensor_copy(dst, ps[0:dst.shape[0], i % 4, 0:dst.shape[1]]).then_inc(dve_emptied, 1)

    def prototype_attention():
        s, other = semaphores()
        (a_ready, max_done, neg_ready, neg_turned, row_ready, st_ready, exp_done, pv_done, batch_done, inverted,
         scaled) = [s.take() for _ in range(11)]
        scale0 = float(D) ** -0.5
        tiles = CTX_TILES
        with nc.Block() as block:
            @block.sync
            def _(sp):
                sp.sem_clear(other)

            @block.tensor
            def _(pe):
                for b in range(PAIR):
                    for r in range(4):
                        n = b * 4 + r
                        qt, half = r // 2, r % 2
                        bank = 2 * (n % 2)
                        if n >= 2:
                            pe.wait_ge(max_done, n - 1)
                        for col in range(0, HALF - half, 512):
                            width = min(512, HALF - half - col)
                            mm = pe.matmul(ps[:, bank + col // 512, 0:width],
                                           tmp_a[:, b * TOK + qt * P:b * TOK + (qt + 1) * P],
                                           k0[:, b, half * HALF + col:half * HALF + col + width], start=True, stop=True)
                        mm.then_inc(a_ready, 1)
                pe.wait_ge(neg_ready, 1)
                for i in range(4):
                    mm = pe.transpose(ps[0:1, 4, i * P:(i + 1) * P], max8[:, i:i + 1], ident[:, :])
                mm.then_inc(neg_turned, 1)
                pe.wait_ge(row_ready, 1)
                for n in range(PAIR * tiles + 1):
                    if n < PAIR * tiles:
                        b, t = n // tiles, n % tiles
                        rows = tile_rows(t)
                        if n >= 2:
                            pe.wait_ge(exp_done, n - 1)
                        st = ps[0:rows, n % 2, 0:TOK]
                        pe.matmul(st, k0[:, b, t * P:t * P + rows], tmp_a[:, b * TOK:(b + 1) * TOK],
                                  start=True, stop=False)
                        pe.matmul(st, ones[0:1, 0:rows], neg_row0[:, b * TOK:(b + 1) * TOK],
                                  start=False, stop=True).then_inc(st_ready, 1)
                    if n >= 1:
                        m = n - 1
                        b, t = m // tiles, m % tiles
                        rows = tile_rows(t)
                        pe.wait_ge(exp_done, n)
                        pe.matmul(ps[:, 4 + 2 * b, 0:TOK], v0[0:rows, m, :], probs0[m % 3][0:rows, :],
                                  start=(t == 0), stop=(t == tiles - 1))
                        pe.matmul(ps[:, 5 + 2 * b, 0:TOK], ones[0:rows, :], probs0[m % 3][0:rows, :],
                                  start=(t == 0), stop=(t == tiles - 1)).then_inc(pv_done, 1)

            @block.vector
            def _(dve):
                for n in range(PAIR * 4):
                    bank = 2 * (n % 2)
                    dve.wait_ge(a_ready, n + 1)
                    src = ps[:, bank:bank + 2, :].rearrange("p a b -> p (a b)")[:, 0:HALF - n % 2]
                    dve.tensor_reduce(maxima[:, 0, n:n + 1], src, AX.X, ALU.max).then_inc(max_done, 1)
                dve.wait_ge(max_done, 8)
                dve.tensor_reduce(neg_f[:, 0:4], maxima[:, 0, 0:8].rearrange("p (r h) -> p r h", h=2), AX.X, ALU.max) \
                    .then_inc(scaled, 1)
                dve.wait_ge(scaled, 1)
                dve.tensor_scalar(max8[:, 0:4], neg_f[:, 0:4], -1.0, None, ALU.mult).then_inc(neg_ready, 1)
                dve.wait_ge(neg_turned, 1)
                dve.tensor_copy(neg_row0, ps[0:1, 4, :]).then_inc(row_ready, 1)
                for b in range(PAIR):
                    cols = slice(b * TOK, (b + 1) * TOK)
                    dve.wait_ge(pv_done, (b + 1) * tiles)
                    dve.reciprocal(tmp_b[:, cols], ps[:, 5 + 2 * b, 0:TOK]).then_inc(inverted, 1)
                    dve.wait_ge(inverted, b + 1)
                    dve.tensor_tensor(attn[:, cols], ps[:, 4 + 2 * b, 0:TOK], tmp_b[:, cols], ALU.mult) \
                        .then_inc(scaled, 1)

            @block.scalar
            def _(act):
                for n in range(PAIR * tiles):
                    rows = tile_rows(n % tiles)
                    act.wait_ge(st_ready, n + 1)
                    if n >= 3:
                        act.wait_ge(pv_done, n - 2)
                    act.activation(probs0[n % 3][0:rows, :], ps[0:rows, n % 2, 0:TOK], ACT.Exp, scale=scale0) \
                        .then_inc(exp_done, 1)

    def route():
        s, other = semaphores()
        logits_ready, biased, step, exp_done = [s.take() for _ in range(4)]
        at = W.at["0router"][0]
        with nc.Block() as block:
            @block.sync
            def _(sp):
                sp.sem_clear(other)

            @block.tensor
            def _(pe):
                for e in range(3):
                    pe.matmul(ps[:, e, :], weights[:, at + e:at + e + 1].to_broadcast([P, P]), normed[:, :],
                              start=True, stop=False)
                    pe.matmul(ps[:, e, :], weights[:, at + 3 + e:at + 4 + e].to_broadcast([P, P]), attn[:, :],
                              start=False, stop=True).then_inc(logits_ready, 1)

            @block.vector
            def _(dve):
                for e in range(3):
                    dve.wait_ge(logits_ready, e + 1)
                    for b in range(PAIR):
                        cols = slice(b * TOK, (b + 1) * TOK)
                        dve.tensor_scalar(router_p[:, e, cols], ps[:, e, cols], modc("0router", b, e), None, ALU.add) \
                            .then_inc(biased, 1)
                dve.wait_ge(biased, 6)
                dve.tensor_tensor(tmp_a[:, :], router_p[:, 0, :], router_p[:, 1, :], ALU.max).then_inc(step, 1)
                dve.wait_ge(step, 1)
                dve.tensor_tensor(tmp_a[:, :], tmp_a[:, :], router_p[:, 2, :], ALU.max).then_inc(step, 1)
                dve.wait_ge(step, 2)
                for e in range(3):
                    dve.tensor_tensor(router_p[:, e, :], router_p[:, e, :], tmp_a[:, :], ALU.subtract).then_inc(step, 1)
                dve.wait_ge(exp_done, 3)
                dve.tensor_tensor(tmp_b[:, :], router_p[:, 0, :], router_p[:, 1, :], ALU.add).then_inc(step, 1)
                dve.wait_ge(step, 6)
                dve.tensor_tensor(tmp_b[:, :], tmp_b[:, :], router_p[:, 2, :], ALU.add).then_inc(step, 1)
                dve.wait_ge(step, 7)
                dve.reciprocal(tmp_a[:, :], tmp_b[:, :]).then_inc(step, 1)
                dve.wait_ge(step, 8)
                for e in range(3):
                    dve.tensor_tensor(router_p[:, e, :], router_p[:, e, :], tmp_a[:, :], ALU.mult).then_inc(step, 1)

            @block.scalar
            def _(act):
                for e in range(3):
                    act.wait_ge(step, 3 + e)
                    act.activation(router_p[:, e, :], router_p[:, e, :], ACT.Exp).then_inc(exp_done, 1)

    def hidden_of_experts():
        s, other = semaphores()
        product_ready, emptied = s.take(), s.take()
        with nc.Block() as block:
            @block.sync
            def _(sp):
                sp.sem_clear(other)

            @block.tensor
            def _(pe):
                for i in range(7):
                    if i >= 4:
                        pe.wait_ge(emptied, 2 * (i - 3))
                    for k, rhs in enumerate((normed[:, :], attn[:, :])):
                        lhs = w("0gate1", k) if i == 6 else w("0e1", (i // 2) * 4 + k * 2 + i % 2)
                        mm = pe.matmul(ps[:, i % 4, :], lhs, rhs, start=(k == 0), stop=(k == 1))
                    mm.then_inc(product_ready, 1)

            @block.scalar
            def _(act):
                for i in range(7):
                    act.wait_ge(product_ready, i + 1)
                    for b in range(PAIR):
                        cols = slice(b * TOK, (b + 1) * TOK)
                        col = modc("0gate1", b) if i == 6 else modc("0e1", b, i)
                        act.activation(hidden[:, i, cols], ps[:, i % 4, cols], ACT.Silu, bias=col).then_inc(emptied, 1)

    def mix_experts():
        s, other = semaphores()
        product_ready, gate_done, weighed, mixed, out_ready, gated, added = [s.take() for _ in range(7)]
        with nc.Block() as block:
            @block.sync
            def _(sp):
                sp.sem_clear(other)

            @block.tensor
            def _(pe):
                for e in range(3):
                    for k in range(2):
                        mm = pe.matmul(ps[:, e, :], w("0e2", 2 * e + k), hidden[:, 2 * e + k, :], start=(k == 0), stop=(k == 1))
                    mm.then_inc(product_ready, 1)
                pe.matmul(ps[:, 3, :], w("0gate2"), hidden[:, 6, :], start=True, stop=True).then_inc(product_ready, 1)
                pe.wait_ge(mixed, 2)
                pe.matmul(ps[:, 4, :], w("0out"), tmp_a[:, :], start=True, stop=True).then_inc(out_ready, 1)

            @block.scalar
            def _(act):
                act.wait_ge(product_ready, 4)
                act.activation(tmp_b[:, :], ps[:, 3, :], ACT.Sigmoid, bias=bias("0gate2")).then_inc(gate_done, 1)

            @block.vector
            def _(dve):
                for e in range(3):
                    dve.wait_ge(product_ready, e + 1)
                    dst = tmp_a[:, :] if e == 0 else router_p[:, e, :]
                    dve.scalar_tensor_tensor(dst, ps[:, e, :], bias("0e2", e), router_p[:, e, :], ALU.add, ALU.mult) \
                        .then_inc(weighed, 1)
                for e in (1, 2):
                    dve.wait_ge(weighed, e + 1)
                    if e == 2:
                        dve.wait_ge(mixed, 1)
                    dve.tensor_tensor(tmp_a[:, :], tmp_a[:, :], router_p[:, e, :], ALU.add).then_inc(mixed, 1)
                dve.wait_ge(out_ready, 1)
                dve.wait_ge(gate_done, 1)
                dve.scalar_tensor_tensor(tmp_b[:, :], ps[:, 4, :], bias("0out"), tmp_b[:, :], ALU.add, ALU.mult) \
                    .then_inc(gated, 1)
                dve.wait_ge(gated, 1)
                dve.tensor_tensor(x[:, :], x[:, :], tmp_b[:, :], ALU.add).then_inc(added, 1)

    def swiglu():
        s, other = semaphores()
        product_ready, silu_done, multiplied = s.take(), s.take(), s.take()
        with nc.Block() as block:
            @block.sync
            def _(sp):
                sp.sem_clear(other)

            @block.tensor
            def _(pe):
                for i in range(8):
                    chunk = i // 2 + 4 * (i % 2)
                    if i >= 4:
                        if i % 2 == 0:
                            pe.wait_ge(silu_done, i // 2 - 1)
                        else:
                            pe.wait_ge(multiplied, i // 2 - 1)
                    pe.matmul(ps[:, i % 4, :], w("3f1", chunk), normed[:, :], start=True, stop=True) \
                        .then_inc(product_ready, 1)

            @block.scalar
            def _(act):
                for c in range(4):
                    act.wait_ge(product_ready, 2 * c + 1)
                    act.activation(hidden[:, c, :], ps[:, (2 * c) % 4, :], ACT.Silu, bias=bias("3f1", c)) \
                        .then_inc(silu_done, 1)

            @block.vector
            def _(dve):
                for c in range(4):
                    dve.wait_ge(product_ready, 2 * c + 2)
                    dve.wait_ge(silu_done, c + 1)
                    dve.scalar_tensor_tensor(hidden[:, c, :], ps[:, (2 * c + 1) % 4, :], bias("3f1", 4 + c),
                                             hidden[:, c, :], ALU.add, ALU.mult).then_inc(multiplied, 1)

    ctx_flat = ctx[:, :, :].rearrange("p b n -> p (b n)")

    def self_jobs(src, layer, rope=False):
        jobs = []
        for n, dst in (("sq", q_parts[:, :, :]), ("sk", k_parts[:, :, 0:N])):
            if rope:
                for b in range(PAIR):
                    cols = slice(b * TOK, (b + 1) * TOK)
                    jobs.append((src[:, cols], w(f"{layer}{n}"), w(f"{layer}{n}r"), None,
                                 rope_tok[:, 0, :], rope_tok[:, 1, :], dst[:, :, cols]))
            else:
                jobs.append((src, w(f"{layer}{n}"), None, bias(f"{layer}{n}"), None, None, dst))
        values_ = [[(src[:, i * P:(i + 1) * P], i) for i in range(4)]]
        return jobs, values_

    def cross_jobs(src, layer, rope=False):
        if rope:
            jobs = [(src[:, b * TOK:(b + 1) * TOK], w(f"{layer}cq"), w(f"{layer}cqr"), None, rope_tok[:, 0, :],
                     rope_tok[:, 1, :], q_parts[:, :, b * TOK:(b + 1) * TOK]) for b in range(PAIR)]
        else:
            jobs = [(src, w(f"{layer}cq"), None, bias(f"{layer}cq"), None, None, q_parts[:, :, :])]
        for b in range(PAIR):
            for c in range(0, CTX, 512):
                n = min(512, CTX - c)
                dst = k_parts[:, :, b * CTX + c:b * CTX + c + n]
                if rope:
                    jobs.append((ctx[:, b, c:c + n], w(f"{layer}ck"), w(f"{layer}ckr"), None,
                                 rope_ctx[:, 0, c:c + n], rope_ctx[:, 1, c:c + n], dst))
                else:
                    jobs.append((ctx[:, b, c:c + n], w(f"{layer}ck"), None, bias(f"{layer}ck"), None, None, dst))
        groups = []
        for b in range(PAIR):
            for first in range(0, CTX_TILES, 4):
                groups.append([(ctx[:, b, t * P:t * P + tile_rows(t)], b * CTX_TILES + t)
                               for t in range(first, min(first + 4, CTX_TILES))])
        return jobs, groups

    eps5, eps6 = sb("eps5", [P, 1]), sb("eps6", [P, 1])
    eps_col = {1e-5: eps5[:, :], 1e-6: eps6[:, :]}

    nc.vector.memset(eps5[:, :], 1e-5)
    nc.vector.memset(eps6[:, :], 1e-6)
    load_constants()
    with nc.Fori(0, BATCHES // PAIR) as pair:
        first_turn = turn[0]
        load_pair(pair)
        layer_norm(1e-5, lambda b: (bias("0g"), bias("0b")))
        project_prototypes()
        prototype_attention()
        route()
        hidden_of_experts()
        mix_experts()
        if last_stage >= 1:
            layer_norm(1e-5, lambda b: (lnw[:, 0, b, 0:1], lnw[:, 0, b, 1:2]))
            project_heads(*self_jobs(normed[:, :], 1), w("1sv"), None)
            attention("self", bias("1sv"))
            add_to_x([(w("1so"), attn[:, :])], bias("1so"), after_attention=True)
        if last_stage >= 2:
            project_heads(*cross_jobs(x[:, :], 1), w("1cv"), 4)
            attention("cross", bias("1cv"))
            add_to_x([(w("1co"), attn[:, :])], bias("1co"), after_attention=True)
        if last_stage >= 3:
            layer_norm(1e-5, lambda b: (lnw[:, 1, b, 0:1], lnw[:, 1, b, 1:2]))
            dense([([(w("1f1", i), normed[:, :])], hidden[:, i, :], ACT.Gelu, bias("1f1", i)) for i in range(4)])
            add_to_x([(w("1f2", i), hidden[:, i, :]) for i in range(4)], bias("1f2"))
        if last_stage >= 4:
            layer_norm(1e-5, lambda b: (modc("2ln1", b, 0), modc("2ln1", b, 1)))
            project_heads(*self_jobs(normed[:, :], 2, rope=True), w("2sv"), None, rope=True)
            attention("self", None)
            add_to_x([(w("2so"), attn[:, :])], None, after_attention=True)
        if last_stage >= 5:
            layer_norm(1e-5, lambda b: (modc("2ln2", b, 0), modc("2ln2", b, 1)))
            project_heads(*cross_jobs(normed[:, :], 2, rope=True), w("2cv"), 4, rope=True, load_rope=True)
            attention("cross", None)
            add_to_x([(w("2co"), attn[:, :])], None, after_attention=True)
            layer_norm(1e-5, lambda b: (modc("2ln3", b, 0), modc("2ln3", b, 1)))
            dense([([(w("2f1", i), normed[:, :])], hidden[:, i, :], ACT.Gelu, bias("2f1", i)) for i in range(4)])
            add_to_x([(w("2f2", i), hidden[:, i, :]) for i in range(4)], bias("2f2"))
        if last_stage >= 6:
            layer_norm(1e-6, lambda b: (modc("3ada", b, 1), modc("3ada", b, 0)))
            project_heads(*self_jobs(normed[:, :], 3), w("3sv"), None)
            attention("window", bias("3sv"))
            add_to_x([(w("3so"), attn[:, :])], bias("3so"), lambda b: modc("3ada", b, 2), after_attention=True)
        if last_stage >= 7:
            layer_norm(1e-6, lambda b: (modc("3ada", b, 4), modc("3ada", b, 3)))
            project_heads(*cross_jobs(normed[:, :], 3), w("3cv"), 3)
            top_attention(bias("3cv"))
            add_to_x([(w("3co"), attn[:, :])], bias("3co"), lambda b: modc("3ada", b, 5), after_attention=True)
        if last_stage >= 8:
            layer_norm(1e-6, lambda b: (modc("3ada", b, 7), modc("3ada", b, 6)))
            swiglu()
            add_to_x([(w("3f2", i), hidden[:, i, :]) for i in range(4)], bias("3f2"), lambda b: modc("3ada", b, 8))
        store_pair(pair)
        even_out(first_turn)


def _rows(a, k):
    a = np.asarray(a)
    return a.reshape(k, D, -1).transpose(1, 0, 2).reshape(D, -1)


def heads(a, order, turned=False):
    d = (order[:, 1] + turned * (HD // 2)) % HD
    return a[..., order[:, 0] * HD + d]


def pack(i):
    g = {k: np.asarray(v) for k, v in i.items()}
    L0, L1, L2, L3 = (lambda n, k=k: g[f"L{k}_xcond_{n}"] for k in range(4))
    e1 = L0("e_w1")
    blocks = {
        "0q": L0("Wq"), "0k": L0("Wk"), "0v": L0("Wv"), "0out": L0("out_w"), "0gate2": L0("gate_w2"),
        "0gate1": _rows(L0("gate_w1")[:2 * D], 2),
        "0e1": np.concatenate([_rows(e1[e, :2 * D], 2) for e in range(3)], 1),
        "0e2": np.concatenate([_rows(L0("e_w2")[e], 2) for e in range(3)], 1),
        "0router": _rows(L0("router_W")[:2 * D], 2),
        "1sq": heads(L1("sa_qw"), BY_DIM), "1sk": heads(L1("sa_kw"), BY_DIM), "1sv": L1("sa_vw"), "1so": L1("sa_ow"),
        "1cq": heads(L1("ca_qw"), BY_DIM), "1ck": heads(L1("ca_kw"), BY_GROUP), "1cv": L1("ca_vw"), "1co": L1("ca_ow"),
        "1f1": L1("ffn_w1"), "1f2": _rows(L1("ffn_w2"), 4),
        "2sq": heads(L2("qkv_w")[:D].T, BY_DIM), "2sqr": heads(L2("qkv_w")[:D].T, BY_DIM, True),
        "2sk": heads(L2("qkv_w")[D:2 * D].T, BY_DIM), "2skr": heads(L2("qkv_w")[D:2 * D].T, BY_DIM, True),
        "2sv": L2("qkv_w")[2 * D:].T, "2so": L2("sa_out_w").T,
        "2cq": heads(L2("q_w").T, BY_DIM), "2cqr": heads(L2("q_w").T, BY_DIM, True),
        "2ck": heads(L2("k_w").T, BY_GROUP), "2ckr": heads(L2("k_w").T, BY_GROUP, True),
        "2cv": L2("v_w").T, "2co": L2("ca_out_w").T, "2f1": L2("ffn_w1").T, "2f2": _rows(L2("ffn_w2").T, 4),
        "3sq": heads(L3("w_qkv")[:, :D], BY_DIM), "3sk": heads(L3("w_qkv")[:, D:2 * D], BY_DIM), "3sv": L3("w_qkv")[:, 2 * D:],
        "3so": L3("w_so"), "3cq": heads(L3("w_q"), BY_DIM), "3ck": heads(L3("w_kv")[:, :D], BY_GROUP), "3cv": L3("w_kv")[:, D:],
        "3co": L3("w_co"), "3f1": L3("w_m1"), "3f2": _rows(L3("w_m2"), 4),
    }
    W, M, B = weight_plan(), modulation_plan(), bias_plan()
    weights = np.concatenate([blocks[n] for n in W.at], 1)
    cond_blocks = {
        "0gate1": L0("gate_w1")[2 * D:], "0e1": np.concatenate([e1[e, 2 * D:] for e in range(3)], 1),
        "1aff1": L1("aff1_w"), "1aff2": L1("aff2_w"), "2ln1": L2("ln1_w").T, "2ln2": L2("ln2_w").T,
        "2ln3": L2("ln3_w").T, "3ada": L3("w_ada"), "0router": L0("router_W")[2 * D:],
    }
    modw = np.concatenate([cond_blocks[n] for n in M.at], 1)

    def cols(v):
        return np.asarray(v).reshape(-1, D).T

    mod_bias = {
        "0gate1": cols(L0("gate_b1")), "0e1": cols(L0("e_b1")), "1aff1": cols(L1("aff1_b")), "1aff2": cols(L1("aff2_b")),
        "2ln1": cols(L2("ln1_b")), "2ln2": cols(L2("ln2_b")), "2ln3": cols(L2("ln3_b")), "3ada": cols(L3("b_ada")),
        "0router": np.broadcast_to(L0("router_b"), (D, 3)),
    }
    qkv_b, kv_b = L3("b_qkv"), L3("b_kv")
    bias_blocks = {
        "mod": np.concatenate([mod_bias[n] for n in M.at], 1),
        "0g": cols(L0("ln_gamma")), "0b": cols(L0("ln_beta")), "0gate2": cols(L0("gate_b2")), "0out": cols(L0("out_b")),
        "0e2": cols(L0("e_b2")), "1g1": cols(L1("ln1_g")), "1b1": cols(L1("ln1_b")), "1g2": cols(L1("ln2_g")),
        "1b2": cols(L1("ln2_b")), "1sq": cols(heads(L1("sa_qb"), BY_DIM)), "1sk": cols(heads(L1("sa_kb"), BY_DIM)),
        "1sv": cols(L1("sa_vb")), "1so": cols(L1("sa_ob")), "1cq": cols(heads(L1("ca_qb"), BY_DIM)),
        "1ck": cols(heads(L1("ca_kb"), BY_GROUP)), "1cv": cols(L1("ca_vb")), "1co": cols(L1("ca_ob")), "1f1": cols(L1("ffn_b1")),
        "1f2": cols(L1("ffn_b2")), "2f1": cols(L2("ffn_b1")), "2f2": cols(L2("ffn_b2")),
        "3sq": cols(heads(qkv_b[:D], BY_DIM)), "3sk": cols(heads(qkv_b[D:2 * D], BY_DIM)), "3sv": cols(qkv_b[2 * D:]),
        "3so": cols(L3("b_so")), "3cq": cols(heads(L3("b_q"), BY_DIM)), "3ck": cols(heads(kv_b[:D], BY_GROUP)), "3cv": cols(kv_b[D:]),
        "3co": cols(L3("b_co")), "3f1": cols(L3("b_m1")), "3f2": cols(L3("b_m2")),
    }
    biases = np.concatenate([bias_blocks[n] for n in B.at], 1)

    half = HD // 2
    inv_freq = (np.float32(1.0) / np.float32(10000.0) ** (np.arange(half, dtype=np.float32) / np.float32(half)))

    def tables(order, positions):
        d = order[:, 1]
        ang = positions.astype(np.float32)[None, :] * inv_freq.astype(np.float32)[d % half][:, None]
        sign = np.where(d < half, -1.0, 1.0)[:, None]
        return np.concatenate([np.cos(ang.astype(np.float64)), np.sin(ang.astype(np.float64)) * sign], 1) \
            .astype(np.float32)

    rope = tables(BY_GROUP, np.arange(CTX))
    const = np.concatenate([np.eye(P, dtype=np.float32), tables(BY_DIM, np.roll(np.arange(TOK), -SHIFT))], 1)

    pairs = BATCHES // PAIR
    x = np.roll(g["x"], -SHIFT, axis=1).reshape(pairs, N, D).transpose(0, 2, 1)
    ctx = g["ctx_1024"].reshape(pairs, PAIR * CTX, D).transpose(0, 2, 1)
    return {"x": x, "ctx": ctx, "cond": g["cond_1024"].T, "weights": weights, "modw": modw, "biases": biases,
            "const": const, "rope": rope}


def kernel(**inputs):
    import concourse.bacc as bacc
    from concourse.bass_utils import run_bass_kernel_spmd

    nc = bacc.Bacc("TRN2", target_bir_lowering=False, num_devices=1)
    arrays = {f"in_{k}": np.ascontiguousarray(v) for k, v in pack(inputs).items()}
    args = [nc.dram_tensor(k, v.shape, F32, kind="ExternalInput").ap() for k, v in arrays.items()]
    out = nc.dram_tensor("out_0", (BATCHES // PAIR, D, N), F32, kind="ExternalOutput").ap()
    build_program(nc, *args, out)
    r = run_bass_kernel_spmd(nc, [arrays], core_ids=[0])
    got = np.asarray(r.results[0]["out_0"])
    return np.roll(got.transpose(0, 2, 1).reshape(BATCHES, TOK, D), SHIFT, axis=1)
```

```python
import numpy as np

import concourse.bass as bass
from concourse import mybir

F32 = mybir.dt.float32
BF16 = mybir.dt.bfloat16
ALU = mybir.AluOpType
ACT = mybir.ActivationFunctionType
AX = mybir.AxisListType

P = 128
D = 128
HEADS, HD = 16, 8
GROUP = 4
GROUPS = HEADS // GROUP
BATCHES, TOK, CTX = 4, 256, 1601
PAIR = 2
N = PAIR * TOK
CTX_TILES = -(-CTX // P)
SHIFT, WIN = 32, 64
TOPK = 16
SPLIT_ROWS = 9 * HD
SCORE_ROWS = 96
MAX_ROWS = 99
VH = HD + 1
VROW = HEADS * VH + 24
SCALE = float(np.float32(1.0) / np.sqrt(np.float32(HD)))
LOW = -3.0e38
TWO_ONES = float(np.array([0x3F803F80], np.uint32).view(np.float32)[0])

BY_DIM = np.array([(h, d) for d in range(HD) for h in range(HEADS)])
BY_GROUP = np.array([(GROUP * g + j, d) for g in range(GROUPS) for d in range(HD) for j in range(GROUP)])


class Columns:

    def __init__(self):
        self.at, self.n = {}, 0

    def add(self, name, width):
        self.at[name] = (self.n, width)
        self.n += width


def weight_plan():
    w = Columns()
    for name, width in [
        ("0q", D), ("0kT", D), ("0v", D), ("0out", D), ("0gate2", D), ("0gate1", 2 * D), ("0e1", 3 * 2 * 2 * D),
        ("0e2", 3 * 2 * D), ("0router", 2 * 3),
        ("1sq", D), ("1sk", D), ("1sv", D), ("1so", D), ("1cq", D), ("1ck", D), ("1cv", D), ("1co", D),
        ("1f1", 4 * D), ("1f2", 4 * D),
        ("2sq", D), ("2sqr", D), ("2sk", D), ("2skr", D), ("2sv", D), ("2so", D),
        ("2cq", D), ("2cqr", D), ("2ck", D), ("2ckr", D), ("2cv", D), ("2co", D), ("2f1", 4 * D), ("2f2", 4 * D),
        ("3sq", D), ("3sk", D), ("3sv", D), ("3so", D), ("3cq", D), ("3ck", D), ("3cv", D), ("3co", D),
        ("3f1", 8 * D), ("3f2", 4 * D),
    ]:
        w.add(name, width)
    return w


def modulation_plan():
    m = Columns()
    for name, chunks in [("0gate1", 1), ("0e1", 6), ("1aff1", 2), ("1aff2", 2), ("2ln1", 2), ("2ln2", 2),
                         ("2ln3", 2), ("3ada", 9)]:
        m.add(name, chunks)
    m.add("0router", 3)
    return m


def bias_plan():
    b = Columns()
    b.add("mod", modulation_plan().n)
    for name, n in [("0g", 1), ("0b", 1), ("0gate2", 1), ("0out", 1), ("0e2", 3),
                    ("1g1", 1), ("1b1", 1), ("1g2", 1), ("1b2", 1), ("1sq", 1), ("1sk", 1), ("1sv", 1), ("1so", 1),
                    ("1cq", 1), ("1ck", 1), ("1cv", 1), ("1co", 1), ("1f1", 4), ("1f2", 1), ("2f1", 4), ("2f2", 1),
                    ("3sq", 1), ("3sk", 1), ("3sv", 1), ("3so", 1), ("3cq", 1), ("3ck", 1), ("3cv", 1), ("3co", 1),
                    ("3f1", 8), ("3f2", 1)]:
        b.add(name, n)
    return b


class SemaphoreSet:

    def __init__(self, nc, name, n):
        self.sems = [nc.alloc_semaphore(f"{name}{i}") for i in range(n)]
        self.range = range(self.sems[0].num, self.sems[0].num + n)
        self.used = 0

    def take(self, n=1):
        got = self.sems[self.used:self.used + n]
        self.used += n
        return got[0] if n == 1 else got


def build_program(nc, x_in, ctx_in, cond_in, weights_in, modw_in, bias_in, const_in, rope_in, out, last_stage=99):
    W, M, B = weight_plan(), modulation_plan(), bias_plan()

    def sb(name, shape, dt=F32):
        return nc.alloc_sbuf_tensor(name, shape, dt)

    weights = sb("weights", [P, W.n])
    biases = sb("biases", [P, B.n])
    ident = sb("ident", [P, P])
    ident16 = sb("ident16", [P, P], BF16)
    mean_w = sb("mean_w", [P, P])
    ones16 = sb("ones16", [3, P], BF16)
    rope_tok = sb("rope_tok", [P, 2, TOK])
    mod_all = sb("mod_all", [P, BATCHES, M.n])
    x = sb("x", [P, N])
    normed = sb("normed", [P, N])
    tmp_a = sb("tmp_a", [P, N])
    scratch = sb("scratch", [P, 2 * N + 3 * N // 2])
    tmp_b, attn = scratch[:, 0:N], scratch[:, N:2 * N]
    q_parts = scratch[:, 2 * N:].bitcast(BF16).rearrange("p (i n) -> p i n", i=3)
    ctx = sb("ctx", [P, PAIR, CTX])
    mod = sb("mod", [P, PAIR, M.n])
    lnw = sb("lnw", [P, 2, PAIR, 2])
    k_parts = sb("k_parts", [P, 3, PAIR * CTX], BF16)
    q_stack = sb("q_stack", [P, HEADS, N], BF16)
    k_room = sb("k_room", [P, 3 * GROUP * CTX], BF16)
    values = sb("values", [P, PAIR * CTX_TILES, VROW])
    attn_tok = sb("attn_tok", [P, PAIR, 2, D])
    heads_out = sb("heads_out", [P, TOK])
    maxima = sb("maxima", [P, 2, 16])
    max8 = sb("max8", [P, 8])
    neg_f = sb("neg_f", [P, 8])
    neg_parts = sb("neg_parts", [P, 2, 2, 3, GROUP], BF16)
    neg_rows = [sb(f"neg_rows{i}", [24, P], BF16) for i in range(2)]
    sums_inv = sb("sums_inv", [P, 2, GROUP])
    deviation = sb("deviation", [P, PAIR, TOK // P])
    shared = sb("shared", [P, 9920])
    slots = [k_room[:, i * GROUP * CTX:(i + 1) * GROUP * CTX] for i in range(3)]
    slots.append(shared[:, 9920 - GROUP * CTX // 2:9920].bitcast(BF16))
    k_stack = [v.rearrange("p (j n) -> p j n", j=GROUP) for v in slots]
    k_tokens = k_room[:, 0:HEADS * N].rearrange("p (h n) -> p h n", h=HEADS)

    def part(first, shape):
        size = int(np.prod(shape))
        v = shared[:, first:first + size]
        if len(shape) == 2:
            v = v.rearrange("p (a b) -> p a b", a=shape[0])
        if len(shape) == 3:
            v = v.rearrange("p (a b c) -> p a b c", a=shape[0], b=shape[1])
        return v

    modw = shared[:, 0:M.at["0router"][0] * D + 3]
    condT = shared[:, 29 * D:29 * D + BATCHES]
    condS = shared[:, 29 * D + BATCHES:29 * D + 2 * BATCHES]
    split_f = part(0, [2, 512])
    split_t = part(1024, [2, 512])
    split_r = part(2048, [2, 512])
    rope_ctx = part(3072, [2, CTX])
    probs = [part(1024 * i, [GROUP, TOK]) for i in range(4)]
    hidden = part(0, [7, N])
    router_p = part(7 * N, [3, N])
    v0 = part(0, [PAIR * CTX_TILES, D + 1])
    probs0 = [part(PAIR * CTX_TILES * (D + 1) + TOK * i, [TOK]) for i in range(3)]
    neg_row0 = shared[0:3, 7424:7424 + N // 2].bitcast(BF16)
    untaken = [part(CTX * i, [CTX]) for i in range(2)]
    weight_e = [part(CTX * (2 + i), [CTX]) for i in range(2)]
    probs_t = [part(4 * CTX + CTX_TILES * P * i, [CTX_TILES, P]) for i in range(2)]
    best = sb("best", [P, 2, TOPK + 1])
    largest_count = sb("largest_count", [1, PAIR * GROUPS + 1], mybir.dt.int32)

    ps = nc.alloc_psum_tensor("ps", [P, 8, 512], F32)

    def words(v):
        return v.bitcast(F32)

    def w(name, i=0, n=1):
        at, width = W.at[name]
        return weights[:, at + i * D:at + (i + n) * D]

    def bias(name, i=0):
        at = B.at[name][0] + i
        return biases[:, at:at + 1]

    def modc(name, b, i=0):
        at = M.at[name][0] + i
        return mod[:, b, at:at + 1]

    sets = [SemaphoreSet(nc, "even", 28), SemaphoreSet(nc, "odd", 28)]
    turn = [0]
    carried = SemaphoreSet(nc, "carried", 10)
    q_loaded, ctx_loaded = carried.take(2)
    weights_loaded = nc.alloc_semaphore("weights_loaded")
    k_terms, k_copies = carried.take(4), carried.take(4)

    def semaphores():
        s, other = sets[turn[0] % 2], sets[1 - turn[0] % 2]
        turn[0] += 1
        s.used = 0
        return s, other.range

    def tile_rows(t):
        return min(P, CTX - t * P)

    def load_constants():
        s, other = semaphores()
        loaded, cond_loaded, silu_done, mod_ready, biased = [s.take() for _ in range(5)]
        with nc.Block() as block:
            @block.sync
            def _(sp):
                sp.sem_clear(other)
                sp.dma_start(modw, modw_in).then_inc(cond_loaded, 16)
                sp.dma_start(condT, cond_in).then_inc(cond_loaded, 16)
                sp.dma_start(biases[:, :], bias_in).then_inc(cond_loaded, 16)
                sp.dma_start(ident[:, :], const_in[:, 0:P]).then_inc(loaded, 16)
                sp.dma_start(rope_tok[:, :, :], const_in[:, P:P + 2 * TOK].rearrange("p (a b) -> p a b", a=2)) \
                    .then_inc(loaded, 16)
                sp.dma_start(weights[:, :], weights_in).then_inc(weights_loaded, 16)
                sp.wait_ge(loaded, 32)

            @block.gpsimd
            def _(pool):
                pool.memset(words(q_stack[64:96, :, :].rearrange("p h n -> p (h n)")), 0.0)
                pool.memset(words(k_room[64:96, :]), 0.0)

            @block.vector
            def _(dve):
                dve.memset(mean_w[:, :], 1.0 / D)
                dve.memset(words(k_room[96:128, :]), TWO_ONES)
                dve.memset(values[:, :, :], 1.0)
                dve.memset(ones16[:, :], 1.0)
                dve.wait_ge(loaded, 32)
                dve.tensor_copy(ident16[:, :], ident[:, :])
                dve.wait_ge(mod_ready, 1)
                dve.wait_ge(cond_loaded, 48)
                m_view = ps[:, 0, 0:M.n * BATCHES].rearrange("p (c b) -> p b c", b=BATCHES)
                b_view = biases[:, 0:M.n].unsqueeze(1).to_broadcast([P, BATCHES, M.n])
                dve.tensor_tensor(mod_all[:, :, :], m_view, b_view, ALU.add).then_inc(biased, 1)

            @block.scalar
            def _(act):
                act.wait_ge(cond_loaded, 48)
                act.activation(condS, condT, ACT.Silu).then_inc(silu_done, 1)

            @block.tensor
            def _(pe):
                pe.wait_ge(cond_loaded, 48)
                pe.wait_ge(silu_done, 1)
                for c in range(M.n):
                    router = c >= M.at["0router"][0]
                    ada = M.at["3ada"][0] <= c < M.at["3ada"][0] + 9
                    if router:
                        e = M.at["0router"][0] * D + c - M.at["0router"][0]
                        lhs = modw[:, e:e + 1].to_broadcast([P, P])
                    else:
                        lhs = modw[:, c * D:(c + 1) * D]
                    mm = pe.matmul(ps[:, 0, c * BATCHES:(c + 1) * BATCHES], lhs, condS if ada else condT,
                                   start=True, stop=True)
                mm.then_inc(mod_ready, 1)

    def even_out(first_turn):
        if (turn[0] - first_turn) % 2:
            s, other = semaphores()
            with nc.Block() as block:
                @block.sync
                def _(sp):
                    sp.sem_clear(other)

    def store_pair(pair):
        s, other = semaphores()
        stored = s.take()
        with nc.Block() as block:
            @block.sync
            def _(sp):
                sp.sem_clear(other)
                sp.dma_start(out[bass.ds(pair, 1), :, :].rearrange("a p n -> (a p) n"), x[:, :]).then_inc(stored, 16)
                sp.wait_ge(stored, 16)

    class Norm:

        def __init__(self, s, eps, affine):
            self.eps, self.affine = eps, affine
            (self.mean_ready, self.centred, self.squared, self.var_ready, self.root_done, self.inverted, self.spread,
             self.scaled, self.done, self.table_loaded) = [s.take() for _ in range(10)]
            self.mean = [ps[:, b, 0:TOK] for b in range(PAIR)]
            self.factor = [ps[:, 4 + b, 0:TOK] for b in range(PAIR)]
            self.cols = [slice(b * TOK, (b + 1) * TOK) for b in range(PAIR)]
            self.tiles = TOK // P

        def tensor(self, pe):
            for b in range(PAIR):
                pe.matmul(self.mean[b], mean_w[:, :], x[:, self.cols[b]], start=True, stop=True) \
                    .then_inc(self.mean_ready, 1)
            for b in range(PAIR):
                pe.wait_ge(self.squared, b + 1)
                for i in range(self.tiles):
                    at = b * TOK + i * P
                    mm = pe.matmul(ps[:, 2 + b, i:i + 1], tmp_b[:, at:at + P], mean_w[:, 0:1], start=True, stop=True)
                mm.then_inc(self.var_ready, 1)
            for b in range(PAIR):
                pe.wait_ge(self.inverted, b + 1)
                for i in range(self.tiles):
                    mm = pe.matmul(self.factor[b][:, i * P:(i + 1) * P],
                                   deviation[:, b, i:i + 1].to_broadcast([P, P]), ident[:, :], start=True, stop=True)
                mm.then_inc(self.spread, 1)

        def scalar(self, act):
            act.activation(max8[:, 0:1], eps_col[self.eps], ACT.Sqrt).then_inc(self.table_loaded, 1)
            for b in range(PAIR):
                act.wait_ge(self.centred, b + 1)
                act.activation(tmp_b[:, self.cols[b]], tmp_a[:, self.cols[b]], ACT.Square).then_inc(self.squared, 1)
            for b in range(PAIR):
                act.wait_ge(self.var_ready, b + 1)
                act.activation(deviation[:, b, :], ps[:, 2 + b, 0:self.tiles], ACT.Sqrt, bias=eps_col[self.eps]) \
                    .then_inc(self.root_done, 1)

        def vector(self, dve):
            cols = self.cols
            for b in range(PAIR):
                dve.wait_ge(self.mean_ready, b + 1)
                dve.tensor_tensor(tmp_a[:, cols[b]], x[:, cols[b]], self.mean[b], ALU.subtract) \
                    .then_inc(self.centred, 1)
            for b in range(PAIR):
                dve.wait_ge(self.root_done, b + 1)
                dve.reciprocal(deviation[:, b, :], deviation[:, b, :]).then_inc(self.inverted, 1)
            dve.wait_ge(self.centred, PAIR)
            for b in range(PAIR):
                scale, shift = self.affine(b)
                dve.wait_ge(self.spread, b + 1)
                dve.scalar_tensor_tensor(tmp_a[:, cols[b]], tmp_a[:, cols[b]], scale, self.factor[b], ALU.mult, ALU.mult) \
                    .then_inc(self.scaled, 1)
            for b in range(PAIR):
                scale, shift = self.affine(b)
                dve.wait_ge(self.scaled, b + 1)
                dve.tensor_scalar(normed[:, cols[b]], tmp_a[:, cols[b]], shift, None, ALU.add).then_inc(self.done, 1)

    def load_pair(pair, norm_next):
        s, other = semaphores()
        loaded, copied, made = s.take(), s.take(), s.take()
        norm = Norm(s, *norm_next)
        with nc.Block() as block:
            @block.sync
            def _(sp):
                sp.sem_clear(other)
                sp.dma_start(x[:, :], x_in[bass.ds(pair, 1), :, :].rearrange("a p n -> (a p) n")).then_inc(loaded, 16)
                sp.dma_start(ctx[:, :, :].rearrange("p b n -> p (b n)"),
                             ctx_in[bass.ds(pair, 1), :, :].rearrange("a p n -> (a p) n")).then_inc(ctx_loaded, 16)
                sp.wait_ge(loaded, 16)

            @block.tensor
            def _(pe):
                pe.wait_ge(loaded, 16)
                norm.tensor(pe)

            @block.scalar
            def _(act):
                norm.scalar(act)

            @block.vector
            def _(dve):
                src = mod_all[:, :, :].rearrange("p b m -> p (b m)")
                dve.tensor_copy(mod[:, :, :].rearrange("p b m -> p (b m)"),
                                src[:, bass.ds(pair * (PAIR * M.n), PAIR * M.n)]).then_inc(copied, 1)
                dve.wait_ge(copied, 1)
                for i, name in enumerate(("1aff1", "1aff2")):
                    for b in range(PAIR):
                        dve.tensor_scalar(lnw[:, i, b, 0:1], modc(name, b, 0), bias(f"1g{i + 1}"), None, ALU.mult)
                        dve.scalar_tensor_tensor(lnw[:, i, b, 1:2], modc(name, b, 0), bias(f"1b{i + 1}"),
                                                 modc(name, b, 1), ALU.mult, ALU.add)
                at2 = M.at["2ln1"][0]
                g2 = mod[:, :, at2:at2 + 6:2]
                dve.tensor_scalar(g2, g2, 1.0, None, ALU.add)
                at3 = M.at["3ada"][0]
                g3 = mod[:, :, at3 + 1:at3 + 9:3]
                dve.tensor_scalar(g3, g3, 1.0, None, ALU.add).then_inc(made, 1)
                dve.wait_ge(loaded, 16)
                norm.vector(dve)

    def add_to_x(terms, b_col, gate=None, after_attention=False, norm_next=None):
        s, other = semaphores()
        product_ready, gated, added = s.take(), s.take(), s.take()
        norm = Norm(s, *norm_next) if norm_next else None
        with nc.Block() as block:
            @block.sync
            def _(sp):
                sp.sem_clear(other)
                if after_attention:
                    sp.sem_clear(carried.range)

            @block.tensor
            def _(pe):
                for k, (lhs, rhs) in enumerate(terms):
                    mm = pe.matmul(ps[:, 6, :], lhs, rhs, start=(k == 0), stop=(k == len(terms) - 1))
                mm.then_inc(product_ready, 1)
                if norm:
                    pe.wait_ge(added, 1)
                    norm.tensor(pe)

            @block.scalar
            def _(act):
                if norm:
                    norm.scalar(act)

            @block.vector
            def _(dve):
                dve.wait_ge(product_ready, 1)
                vector_add(dve, b_col, gate, gated, added)
                if norm:
                    norm.vector(dve)

    def vector_add(dve, b_col, gate, gated, added):
        if gate is None:
            if b_col is None:
                dve.tensor_tensor(x[:, :], ps[:, 6, :], x[:, :], ALU.add).then_inc(added, 1)
            else:
                dve.scalar_tensor_tensor(x[:, :], ps[:, 6, :], b_col, x[:, :], ALU.add, ALU.add).then_inc(added, 1)
            return
        for b in range(PAIR):
            cols = slice(b * TOK, (b + 1) * TOK)
            dve.tensor_scalar(tmp_a[:, cols], ps[:, 6, cols], b_col, gate(b), ALU.add, ALU.mult).then_inc(gated, 1)
        dve.wait_ge(gated, PAIR)
        dve.tensor_tensor(x[:, :], tmp_a[:, :], x[:, :], ALU.add).then_inc(added, 1)

    def feed_forward(layer, gate=None, norm_next=None):
        s, other = semaphores()
        wide_ready, chunk_done, multiplied, product_ready, gated, added = [s.take() for _ in range(6)]
        norm = Norm(s, *norm_next) if norm_next else None
        doubled = layer == 3
        hidden_ready = multiplied if doubled else chunk_done
        with nc.Block() as block:
            @block.sync
            def _(sp):
                sp.sem_clear(other)

            @block.tensor
            def _(pe):
                for c in range(4):
                    if doubled:
                        if c >= 2:
                            pe.wait_ge(multiplied, c - 1)
                        for half in range(2):
                            pe.matmul(ps[:, 2 * (c % 2) + half, :], w("3f1", c + 4 * half), normed[:, :],
                                      start=True, stop=True).then_inc(wide_ready, 1)
                    else:
                        pe.matmul(ps[:, c, :], w(f"{layer}f1", c), normed[:, :], start=True, stop=True) \
                            .then_inc(wide_ready, 1)
                for c in range(4):
                    pe.wait_ge(hidden_ready, c + 1)
                    mm = pe.matmul(ps[:, 6, :], w(f"{layer}f2", c), hidden[:, c, :], start=(c == 0), stop=(c == 3))
                mm.then_inc(product_ready, 1)
                if norm:
                    pe.wait_ge(added, 1)
                    norm.tensor(pe)

            @block.scalar
            def _(act):
                for c in range(4):
                    if doubled:
                        act.wait_ge(wide_ready, 2 * c + 1)
                        act.activation(hidden[:, c, :], ps[:, 2 * (c % 2), :], ACT.Silu, bias=bias("3f1", c)) \
                            .then_inc(chunk_done, 1)
                    else:
                        act.wait_ge(wide_ready, c + 1)
                        act.activation(hidden[:, c, :], ps[:, c, :], ACT.Gelu, bias=bias(f"{layer}f1", c)) \
                            .then_inc(chunk_done, 1)
                if norm:
                    norm.scalar(act)

            @block.vector
            def _(dve):
                if doubled:
                    for c in range(4):
                        dve.wait_ge(wide_ready, 2 * c + 2)
                        dve.wait_ge(chunk_done, c + 1)
                        dve.scalar_tensor_tensor(hidden[:, c, :], ps[:, 2 * (c % 2) + 1, :], bias("3f1", 4 + c),
                                                 hidden[:, c, :], ALU.add, ALU.mult).then_inc(multiplied, 1)
                dve.wait_ge(product_ready, 1)
                vector_add(dve, bias(f"{layer}f2"), gate, gated, added)
                if norm:
                    norm.vector(dve)

    def load_queries(sp):
        for j in range(3):
            for i in range(3):
                sp.dma_start(q_stack[24 * j + 8 * i:24 * j + 8 * i + 8, :, :], q_parts[:, j, :]).then_inc(q_loaded, 16)

    def load_key_parts(sp, u, ring):
        b, g, slot = u // GROUPS, u % GROUPS, u % ring
        for i in range(3):
            sp.dma_start(k_stack[slot][8 * i:8 * i + 8, :, :],
                         k_parts[32 * g:32 * g + 32, i, b * CTX:(b + 1) * CTX]).then_inc(k_terms[slot], 16)

    def copy_key_parts(sp, u, ring):
        copy_rows(sp, u % ring, k_stack[u % ring], u // ring + 1)

    def copy_rows(sp, slot, stack, times):
        sp.wait_ge(k_terms[slot], 48 * times)
        for j in (1, 2):
            sp.dma_start(stack[24 * j:24 * j + 24, :, :], stack[0:24, :, :]).then_inc(k_copies[slot], 16)

    def project_heads(split_jobs, value_jobs, w_v, slots_filled, rope=False, load_rope=False):
        s, other = semaphores()
        (proj_ready, exact_done, hi_done, rest_done, mid_done, lo_done, turned, rotated, v_ready, v_done,
         rope_loaded, filled) = [s.take() for _ in range(12)]
        q_jobs = PAIR if rope else 1
        with nc.Block() as block:
            @block.sync
            def _(sp):
                sp.sem_clear(other)
                if load_rope:
                    sp.dma_start(rope_ctx, rope_in.rearrange("p (a b) -> p a b", a=2)).then_inc(rope_loaded, 16)
                sp.wait_ge(lo_done, q_jobs)
                load_queries(sp)
                if slots_filled is None:
                    sp.wait_ge(lo_done, 2 * q_jobs)
                    for i in range(3):
                        sp.dma_start(k_tokens[8 * i:8 * i + 8, :, :], k_parts[:, i, 0:N]).then_inc(k_terms[0], 16)
                else:
                    sp.wait_ge(lo_done, q_jobs + 4)
                    for u in range(slots_filled):
                        load_key_parts(sp, u, slots_filled)
                        if u == 1:
                            copy_key_parts(sp, 0, slots_filled)
                if load_rope:
                    sp.wait_ge(rope_loaded, 16)

            @block.gpsimd
            def _(pool):
                if slots_filled == 4:
                    pool.memset(words(slots[3][64:96, :]), 0.0).then_inc(filled, 1)
                    pool.memset(words(slots[3][96:128, :]), TWO_ONES).then_inc(filled, 1)

            @block.tensor
            def _(pe):
                v_next = 0

                def value_group(i):
                    if i >= 2:
                        pe.wait_ge(v_done, i - 1)
                    for k, (src, tile) in enumerate(value_jobs[i]):
                        mm = pe.matmul(ps[0:src.shape[1], 4 + i % 2, k * D:(k + 1) * D], src, w_v, start=True, stop=True)
                    mm.then_inc(v_ready, 1)

                for c, (src, wk, wr, b, cos, sin, dst) in enumerate(split_jobs):
                    n = src.shape[1]
                    if c >= 2:
                        if rope:
                            pe.wait_ge(turned, 2 * (c - 1))
                        else:
                            pe.wait_ge(exact_done, 2 * (c - 1))
                    mm = pe.matmul(ps[:, c % 2, 0:n], wk, src, start=True, stop=True)
                    if rope:
                        mm = pe.matmul(ps[:, 2 + c % 2, 0:n], wr, src, start=True, stop=True)
                    mm.then_inc(proj_ready, 1)
                    if v_next < len(value_jobs):
                        value_group(v_next)
                        v_next += 1
                while v_next < len(value_jobs):
                    value_group(v_next)
                    v_next += 1

            @block.scalar
            def _(act):
                v_next = 0

                def value_group(i):
                    act.wait_ge(v_ready, i + 1)
                    jobs = value_jobs[i]
                    rows, tile = jobs[0][0].shape[1], jobs[0][1]
                    dst = values[0:rows, tile:tile + len(jobs), 0:HEADS * VH] \
                        .rearrange("p t (h c) -> p t h c", c=VH)[:, :, :, 0:HD]
                    src = ps[0:rows, 4 + i % 2, 0:len(jobs) * D].rearrange("p (t h d) -> p t h d", t=len(jobs), d=HD)
                    for k in range(len(jobs)):
                        mm = act.copy(dst[:, k], src[:, k])
                    mm.then_inc(v_done, 1)

                for c, (src, wk, wr, b, cos, sin, dst) in enumerate(split_jobs):
                    n = src.shape[1]
                    if rope:
                        act.wait_ge(rotated, c + 1)
                        act.copy(dst[:, 0, :], split_f[:, c % 2, 0:n]).then_inc(hi_done, 1)
                    else:
                        act.wait_ge(proj_ready, c + 1)
                        if c >= 2:
                            act.wait_ge(rest_done, c - 1)
                        act.activation(split_f[:, c % 2, 0:n], ps[:, c % 2, 0:n], ACT.Identity, bias=b) \
                            .then_inc(exact_done, 1)
                        act.activation(dst[:, 0, :], ps[:, c % 2, 0:n], ACT.Identity, bias=b).then_inc(exact_done, 1)
                    if v_next < len(value_jobs):
                        value_group(v_next)
                        v_next += 1
                while v_next < len(value_jobs):
                    value_group(v_next)
                    v_next += 1

            @block.vector
            def _(dve):
                if load_rope:
                    dve.wait_ge(rope_loaded, 16)

                def rotate(c):
                    src, wk, wr, b, cos, sin, dst = split_jobs[c]
                    n = src.shape[1]
                    exact, turn_ = split_f[:, c % 2, 0:n], split_t[:, c % 2, 0:n]
                    dve.wait_ge(proj_ready, c + 1)
                    dve.tensor_tensor(exact, ps[:, c % 2, 0:n], cos, ALU.mult).then_inc(turned, 1)
                    dve.tensor_tensor(turn_, ps[:, 2 + c % 2, 0:n], sin, ALU.mult).then_inc(turned, 1)
                    dve.wait_ge(turned, 2 * (c + 1))
                    dve.tensor_tensor(exact, exact, turn_, ALU.add).then_inc(rotated, 1)

                def split(c):
                    src, dst = split_jobs[c][0], split_jobs[c][-1]
                    n = src.shape[1]
                    exact, rest = split_f[:, c % 2, 0:n], split_r[:, c % 2, 0:n]
                    if rope:
                        dve.wait_ge(hi_done, c + 1)
                    else:
                        dve.wait_ge(exact_done, 2 * (c + 1))
                    dve.tensor_tensor(rest, exact, dst[:, 0, :], ALU.subtract).then_inc(rest_done, 1)
                    dve.wait_ge(rest_done, c + 1)
                    dve.tensor_copy(dst[:, 1, :], rest).then_inc(mid_done, 1)
                    dve.wait_ge(mid_done, c + 1)
                    dve.tensor_tensor(dst[:, 2, :], rest, dst[:, 1, :], ALU.subtract).then_inc(lo_done, 1)

                if rope:
                    rotate(0)
                for c in range(len(split_jobs)):
                    if rope and c + 1 < len(split_jobs):
                        rotate(c + 1)
                    split(c)

    HALF = (CTX + 1) // 2

    def attention(kind, v_bias):
        s, other = semaphores()
        cross = kind == "cross"
        tiles = CTX_TILES if cross else 2
        units = PAIR * GROUPS
        steps = units * tiles
        neg_loaded = s.take(2)
        (st_ready, exp_done, pv_done, a_ready, max_done, small, neg_ready, neg_turned, rows_ready,
         o_copied, o_turned, normalised, all_turned, inverted, cleared) = [s.take() for _ in range(15)]
        chunks = {"cross": 16, "self": 2, "window": 1}[kind]
        smalls = 4 if cross else 3
        keys_of = tile_rows if cross else (lambda t: P)
        lead = {"cross": 21, "self": 6, "window": 4}[kind]
        all_chunks = units * chunks
        first_chunk = [min(all_chunks, lead + round(chunks * n / tiles)) for n in range(steps + 1)]

        spare_from = min(n for n in range(steps + 1) if first_chunk[n] == all_chunks)

        def score_bank(n):
            return 0 if n >= spare_from and n % 2 else 4

        def earlier_user(n):
            for m in range(n - 1, -1, -1):
                if score_bank(m) == score_bank(n):
                    return m
            return -1 if score_bank(n) == 0 else None

        def maxima_turned(n):
            first, last = (0, lead) if n < 0 else (first_chunk[n], first_chunk[n + 1])
            got = [c // chunks - 1 for c in range(first, last) if c % chunks == min(1, chunks - 1) and c >= chunks]
            if n >= 1 and last == all_chunks and first < all_chunks:
                got.append(units - 1)
            return got

        def key(rows, u, j, at, n):
            b, g = u // GROUPS, u % GROUPS
            if cross:
                return k_stack[u % 4][0:rows, j, at:at + n]
            return k_tokens[0:rows, 4 * g + j, b * TOK + at:b * TOK + at + n]

        def query(rows, u, j, at, n):
            b, g = u // GROUPS, u % GROUPS
            return q_stack[0:rows, 4 * g + j, b * TOK + at:b * TOK + at + n]

        with nc.Block() as block:
            @block.sync
            def _(sp):
                sp.sem_clear(other)

                def rows_out(u):
                    b, g = u // GROUPS, u % GROUPS
                    sp.wait_ge(rows_ready, u + 1)
                    for qt in range(2):
                        sp.dma_start(q_stack[96:99, 4 * g:4 * g + 4, b * TOK + qt * P:b * TOK + (qt + 1) * P],
                                     neg_rows[u % 2][12 * qt:12 * qt + 12, :]).then_inc(neg_loaded[u % 2], 16)

                if cross:
                    for u in range(1, 4):
                        copy_key_parts(sp, u, 4)
                else:
                    copy_rows(sp, 0, k_tokens, 1)
                for u in range(units):
                    rows_out(u)
                    if cross and 1 <= u < units - 3:
                        sp.wait_ge(st_ready, 2 * tiles * u)
                        load_key_parts(sp, u + 3, 4)
                        copy_key_parts(sp, u + 3, 4)

            @block.tensor
            def _(pe):
                turned_so_far, heads_turned = [0], [0]

                def phase_a(n):
                    u, c = n // chunks, n % chunks
                    if cross and c == 0:
                        pe.wait_ge(k_copies[u % 4], 32 * (u // 4 + 1))
                    if n >= 2:
                        pe.wait_ge(max_done, n - 1)
                    bank = 2 * (n % 2)
                    if cross:
                        r, half = c // 2, c % 2
                        j, qt = r // 2, r % 2
                        for col in range(0, HALF - half, 512):
                            width = min(512, HALF - half - col)
                            mm = pe.matmul(ps[:, bank + col // 512, 0:width], query(SCORE_ROWS, u, j, qt * P, P),
                                           key(SCORE_ROWS, u, j, half * HALF + col, width), start=True, stop=True)
                    elif kind == "self":
                        for i in range(4):
                            j, qt = (4 * c + i) // 2, i % 2
                            mm = pe.matmul(ps[:, bank + i // 2, (i % 2) * TOK:(i % 2 + 1) * TOK],
                                           query(SCORE_ROWS, u, j, qt * P, P), key(SCORE_ROWS, u, j, 0, TOK),
                                           start=True, stop=True)
                    else:
                        for r in range(8):
                            j, qt = r // 2, r % 2
                            for h in range(2):
                                at = qt * P + h * WIN
                                mm = pe.matmul(ps[h * WIN:(h + 1) * WIN, bank, r * WIN:(r + 1) * WIN],
                                               query(SCORE_ROWS, u, j, at, WIN), key(SCORE_ROWS, u, j, at, WIN),
                                               start=True, stop=True)
                    mm.then_inc(a_ready, 1)

                def turn_maxima(u):
                    pe.wait_ge(neg_ready, u + 1)
                    if u >= 1:
                        pe.wait_ge(rows_ready, u)
                    if heads_turned[0]:
                        pe.wait_ge(normalised, heads_turned[0])
                    turned_so_far[0] = u + 1
                    pe.transpose(ps[0:24, 7, 0:P // 2].bitcast(BF16),
                                 neg_parts[:, u % 2, :, :, :].rearrange("p a b c -> p (a b c)"),
                                 ident16[:, :]).then_inc(neg_turned, 1)

                def scores_t(n):
                    u, t = n // tiles, n % tiles
                    if t == 0:
                        pe.wait_ge(neg_loaded[u % 2], 32 * (u // 2 + 1))
                    rows = keys_of(t)
                    for hp in range(2):
                        before = earlier_user(n)
                        if before == -1:
                            pe.wait_ge(max_done, all_chunks)
                        elif before is not None:
                            pe.wait_ge(exp_done, 2 * before + 1 + hp)
                        for i in range(2):
                            j = 2 * hp + i
                            if kind == "window":
                                for h in range(2):
                                    at = t * P + h * WIN
                                    mm = pe.matmul(ps[h * WIN:(h + 1) * WIN, score_bank(n) + hp, i * WIN:(i + 1) * WIN],
                                                   key(MAX_ROWS, u, j, at, WIN), query(MAX_ROWS, u, j, at, WIN),
                                                   start=True, stop=True)
                            else:
                                mm = pe.matmul(ps[0:rows, score_bank(n) + hp, i * TOK:(i + 1) * TOK],
                                               key(MAX_ROWS, u, j, t * P, rows), query(MAX_ROWS, u, j, 0, TOK),
                                               start=True, stop=True)
                        mm.then_inc(st_ready, 1)

                def weighted(n):
                    u, t = n // tiles, n % tiles
                    b, g = u // GROUPS, u % GROUPS
                    rows = keys_of(t)
                    pe.wait_ge(exp_done, 2 * (n + 1))
                    if t == 0 and u >= 1:
                        pe.wait_ge(o_copied, u)
                    for j in range(4):
                        lhs = values[0:rows, b * tiles + t, (4 * g + j) * VH:(4 * g + j) * VH + 32]
                        if kind == "window":
                            mm = pe.matmul(ps[32 * j:32 * j + 32, 6, t * P:(t + 1) * P], lhs,
                                           probs[n % 4][:, j, 0:P], start=True, stop=True)
                        else:
                            mm = pe.matmul(ps[32 * j:32 * j + 32, 6, 0:TOK], lhs, probs[n % 4][0:rows, j, :],
                                           start=(t == 0), stop=(t == tiles - 1))
                    mm.then_inc(pv_done, 1)

                def turn_heads(u):
                    pe.wait_ge(o_copied, u + 1)
                    pe.wait_ge(rows_ready, turned_so_far[0])
                    if u >= 1:
                        pe.wait_ge(normalised, u)
                    heads_turned[0] = u + 1
                    for qt in range(2):
                        mm = pe.transpose(ps[:, 7, TOK + qt * P:TOK + (qt + 1) * P], heads_out[:, qt * P:(qt + 1) * P],
                                          ident[:, :])
                    mm.then_inc(o_turned, 1)

                pe.wait_ge(q_loaded, 144)
                if not cross:
                    pe.wait_ge(k_copies[0], 32)
                for c in range(lead):
                    phase_a(c)
                    if c >= chunks and c % chunks == min(1, chunks - 1):
                        turn_maxima(c // chunks - 1)
                for n in range(steps + 2):
                    u, t = n // tiles, n % tiles
                    if n < steps:
                        scores_t(n)
                    if n > tiles and n % tiles == 2 % tiles:
                        turn_heads((n - 2) // tiles - 1)
                    if n < steps:
                        for c in range(first_chunk[n], first_chunk[n + 1]):
                            phase_a(c)
                        for v in maxima_turned(n):
                            turn_maxima(v)
                    if n >= 2:
                        weighted(n - 2)
                turn_heads(units - 1)
                pe.wait_ge(normalised, units)
                for i in range(2 * PAIR):
                    mm = pe.transpose(ps[:, 0, i * P:(i + 1) * P], attn_tok[:, i // 2, i % 2, :], ident[:, :])
                mm.then_inc(all_turned, 1)

            @block.vector
            def _(dve):
                def maxima_of(n):
                    u, c = n // chunks, n % chunks
                    bank = 2 * (n % 2)
                    dve.wait_ge(a_ready, n + 1)
                    if cross:
                        src = ps[:, bank:bank + 2, :].rearrange("p a b -> p (a b)")[:, 0:HALF - c % 2]
                        dst = maxima[:, u % 2, c:c + 1]
                    elif kind == "self":
                        src = ps[:, bank:bank + 2, :].rearrange("p a (b k) -> p (a b) k", b=2)
                        dst = maxima[:, u % 2, 4 * c:4 * c + 4]
                    else:
                        src = ps[:, bank, :].rearrange("p (r k) -> p r k", r=8)
                        dst = maxima[:, u % 2, 0:8]
                    dve.tensor_reduce(dst, src, AX.X, ALU.max).then_inc(max_done, 1)
                    if c == chunks - 1:
                        split_maxima(u)

                def split_maxima(u):
                    dve.wait_ge(max_done, (u + 1) * chunks)
                    m, k, parts = maxima[:, u % 2, 0:8], u * smalls, neg_parts[:, u % 2, :, :, :]
                    if cross:
                        m = max8[:, :]
                        dve.tensor_reduce(m, maxima[:, u % 2, :].rearrange("p (r h) -> p r h", h=2), AX.X, ALU.max) \
                            .then_inc(small, 1)
                        k += 1
                        dve.wait_ge(small, k)
                    if u >= 2:
                        dve.wait_ge(neg_turned, u - 1)
                    m = m.rearrange("p (j t) -> p t j", t=2)
                    rest = neg_f[:, :].rearrange("p (t j) -> p t j", t=2)
                    dve.tensor_scalar(parts[:, :, 0, :], m, -1.0, None, ALU.mult).then_inc(small, 1)
                    dve.wait_ge(small, k + 1)
                    dve.scalar_tensor_tensor(rest, m, -1.0, parts[:, :, 0, :], ALU.mult, ALU.subtract) \
                        .then_inc(small, 1)
                    dve.wait_ge(small, k + 2)
                    dve.tensor_copy(parts[:, :, 1, :], rest).then_inc(small, 1)
                    dve.wait_ge(small, k + 3)
                    dve.tensor_tensor(parts[:, :, 2, :], rest, parts[:, :, 1, :], ALU.subtract).then_inc(neg_ready, 1)

                def heads_to_tokens(u):
                    b, g = u // GROUPS, u % GROUPS
                    dve.wait_ge(o_turned, u + 1)
                    got = ps[:, 7, TOK:2 * TOK].rearrange("p (t j c) -> p t j c", t=2, j=GROUP)
                    dve.reciprocal(sums_inv[:, :, :], got[:, :, :, HD]).then_inc(inverted, 1)
                    dve.wait_ge(inverted, u + 1)
                    dst = attn_tok[:, b, :, 32 * g:32 * g + 32].rearrange("p t (j d) -> p t j d", j=GROUP)
                    inv = sums_inv[:, :, :].unsqueeze(3).to_broadcast([P, 2, GROUP, HD])
                    dve.tensor_tensor(dst, got[:, :, :, 0:HD], inv, ALU.mult).then_inc(normalised, 1)

                if kind == "window":
                    for i in range(4):
                        dve.memset(probs[i][:, :, 0:P], 0.0).then_inc(cleared, 1)
                for c in range(lead):
                    maxima_of(c)
                for n in range(steps + 2):
                    if n > tiles and n % tiles == 2 % tiles:
                        heads_to_tokens((n - 2) // tiles - 1)
                    if n < steps:
                        for c in range(first_chunk[n], first_chunk[n + 1]):
                            maxima_of(c)
                heads_to_tokens(units - 1)

            @block.scalar
            def _(act):
                def rows_of_maxima(u):
                    act.wait_ge(neg_turned, u + 1)
                    if u >= 2:
                        act.wait_ge(neg_loaded[u % 2], 32 * (u // 2))
                    act.copy(neg_rows[u % 2][:, :], ps[0:24, 7, 0:P // 2].bitcast(BF16)).then_inc(rows_ready, 1)

                def copy_heads(u):
                    act.wait_ge(pv_done, (u + 1) * tiles)
                    if u >= 1:
                        act.wait_ge(o_turned, u)
                    act.copy(heads_out[:, :], ps[:, 6, 0:TOK]).then_inc(o_copied, 1)

                if kind == "window":
                    act.wait_ge(cleared, 4)
                for u in maxima_turned(-1):
                    rows_of_maxima(u)
                for n in range(steps):
                    u, t = n // tiles, n % tiles
                    rows = keys_of(t)
                    if n >= 4:
                        act.wait_ge(pv_done, n - 3)
                    for hp in range(2):
                        act.wait_ge(st_ready, 2 * n + hp + 1)
                        if kind == "window":
                            for h in range(2):
                                half = slice(h * WIN, (h + 1) * WIN)
                                src = ps[half, score_bank(n) + hp, 0:2 * WIN].rearrange("p (j q) -> p j q", j=2)
                                e = act.activation(probs[n % 4][half, 2 * hp:2 * hp + 2, half], src,
                                                   ACT.Exp, scale=SCALE)
                        else:
                            src = ps[0:rows, score_bank(n) + hp, :].rearrange("p (j q) -> p j q", j=2)
                            e = act.activation(probs[n % 4][0:rows, 2 * hp:2 * hp + 2, :], src,
                                               ACT.Exp, scale=SCALE)
                        e.then_inc(exp_done, 1)
                    for v in maxima_turned(n):
                        rows_of_maxima(v)
                    if t == 1 and u >= 1:
                        copy_heads(u - 1)
                copy_heads(units - 1)
                act.wait_ge(all_turned, 1)
                b_ap = 0.0 if v_bias is None else v_bias
                act.activation(attn[:, :], ps[:, 0, :], ACT.Identity, bias=b_ap).then_inc(o_copied, 1)

    def top_attention(v_bias):
        s, other = semaphores()
        (s_ready, maxed, small, offset_done, copied, e_done, masked, weight_done, t_ready, t_copied,
         pv_done, o_copied, o_turned, inv_done, normalised, all_turned, most_done, most_turned,
         last_done) = [s.take() for _ in range(19)]
        units = PAIR * GROUPS
        total = units * 8
        parts = 16

        def turned_at(t):
            return ps[:, (4, 5, 7, 4)[t // 4], (t % 4) * P:(t % 4 + 1) * P]

        turned_heads = ps[:, 4, TOK:2 * TOK]
        heads_tok = tmp_a[:, 0:TOK]
        scores = ps[:, 0:4, :].rearrange("p a b -> p (a b)")[:, 0:CTX]
        kept = [ctx[:, 0, :], ctx[:, 1, :], part(0, [CTX]), scratch[:, 0:CTX]]
        weight = [part(CTX * (1 + i), [CTX]) for i in range(3)]
        candidates = [normed[:, 8 * parts * i:8 * parts * (i + 1)] for i in range(2)]
        counts = normed[:, 16 * parts:16 * parts + total]
        most = normed[:, 16 * parts + total:16 * parts + total + units]

        with nc.Block() as block:
            @block.sync
            def _(sp):
                sp.sem_clear(other)
                for u in range(units):
                    if u >= 3:
                        sp.wait_ge(s_ready, 8 * (u - 2))
                        load_key_parts(sp, u, 3)
                    if u >= 1:
                        copy_key_parts(sp, u, 3)

            @block.tensor
            def _(pe):
                def score_tile(i):
                    u, r = i // 8, i % 8
                    b, g, slot, j, qt = u // GROUPS, u % GROUPS, u % 3, r // 2, r % 2
                    if r == 0:
                        pe.wait_ge(k_copies[slot], 32 * (u // 3 + 1))
                    if i >= 1:
                        pe.wait_ge(copied, i)
                    for col in range(0, CTX, 512):
                        width = min(512, CTX - col)
                        mm = pe.matmul(ps[:, col // 512, 0:width],
                                       q_stack[0:SCORE_ROWS, 4 * g + j, b * TOK + qt * P:b * TOK + (qt + 1) * P],
                                       k_stack[slot][0:SCORE_ROWS, j, col:col + width], start=True, stop=True)
                    mm.then_inc(s_ready, 1)

                def turn_weights(i):
                    if i < total - 1:
                        pe.wait_ge(weight_done, i + 1)
                    else:
                        pe.wait_ge(last_done, 1)
                    if i >= 1:
                        pe.wait_ge(t_copied, 3 * i)
                    for t in range(12):
                        mm = pe.transpose(turned_at(t), weight[i % 3][:, t * P:(t + 1) * P], ident[:, :])
                        if t in (7, 11):
                            mm.then_inc(t_ready, 1)

                def turn_last(i):
                    pe.wait_ge(t_copied, 3 * i + 1)
                    rows = tile_rows(12)
                    mm = pe.transpose(turned_at(12)[0:rows, :], weight[i % 3][:, 12 * P:12 * P + rows], ident[:, :])
                    if i % 8 == 1 and i > 8:
                        mm = turn_heads(i // 8 - 1)
                    mm.then_inc(t_ready, 1)

                def weighted(i):
                    u, r = i // 8, i % 8
                    b, g, j, qt = u // GROUPS, u % GROUPS, r // 2, r % 2
                    pe.wait_ge(t_copied, 3 * (i + 1))
                    if r == 0 and u >= 1:
                        pe.wait_ge(o_copied, u)
                    for t in range(CTX_TILES):
                        rows = tile_rows(t)
                        h = 4 * g + j
                        mm = pe.matmul(ps[32 * j:32 * j + 32, 6, qt * P:(qt + 1) * P],
                                       values[0:rows, b * CTX_TILES + t, h * VH:h * VH + 32],
                                       probs_t[i % 2][0:rows, t, :], start=(t == 0), stop=(t == CTX_TILES - 1))
                    mm.then_inc(pv_done, 1)

                def turn_heads(u):
                    pe.wait_ge(o_copied, u + 1)
                    for qt in range(2):
                        mm = pe.transpose(turned_heads[:, qt * P:(qt + 1) * P], heads_out[:, qt * P:(qt + 1) * P],
                                          ident[:, :])
                    return mm

                pe.wait_ge(q_loaded, 144)
                score_tile(0)
                for i in range(total + 4):
                    if 3 <= i < total + 3:
                        turn_weights(i - 3)
                    if i >= 4:
                        weighted(i - 4)
                    if i + 1 < total:
                        score_tile(i + 1)
                    if 3 <= i < total + 3:
                        turn_last(i - 3)
                pe.wait_ge(most_done, 1)
                for u in range(units):
                    mm = pe.matmul(ps[0:1, u // 4, (u % 4) * P:(u % 4 + 1) * P], most[:, u:u + 1], ident[:, :],
                                   start=True, stop=True)
                mm.then_inc(most_turned, 1)
                turn_heads(units - 1).then_inc(t_ready, 1)
                pe.wait_ge(normalised, units)
                for i in range(2 * PAIR):
                    mm = pe.transpose(ps[:, 7, i * P:(i + 1) * P], attn_tok[:, i // 2, i % 2, :], ident[:, :])
                mm.then_inc(all_turned, 1)

            @block.vector
            def _(dve):
                def choose(i):
                    dve.wait_ge(copied, i + 1)
                    for c in range(parts):
                        m = dve.max(candidates[i % 2][:, 8 * c:8 * c + 8], kept[i % 4][:, c::parts])
                    m.then_inc(maxed, 1)

                def bound(i):
                    top, few = best[:, i % 2, :], candidates[i % 2]
                    dve.wait_ge(maxed, i + 1)
                    dve.max(top[:, 0:8], few).then_inc(small, 1)
                    dve.wait_ge(small, 3 * i + 1)
                    dve.match_replace(few, top[:, 0:8], few, LOW).then_inc(small, 1)
                    dve.tensor_scalar(top[:, TOPK:TOPK + 1], top[:, 0:1], -SCALE, None, ALU.mult) \
                        .then_inc(offset_done, 1)
                    dve.wait_ge(small, 3 * i + 2)
                    dve.max(top[:, 8:16], few).then_inc(small, 1)

                def mask(i):
                    dve.wait_ge(e_done, i + 1)
                    dve.wait_ge(small, 3 * i + 3)
                    dve.tensor_scalar(kept[i % 4], kept[i % 4], best[:, i % 2, TOPK - 1:TOPK], 0.0, ALU.is_ge, ALU.add,
                                      accum_out=counts[:, i:i + 1]).then_inc(masked, 1)

                def heads_to_tokens(u):
                    b, g = u // GROUPS, u % GROUPS
                    dve.wait_ge(o_turned, u + 1)
                    got = heads_tok.rearrange("p (t j c) -> p t j c", t=2, j=GROUP)
                    dve.reciprocal(sums_inv[:, :, :], got[:, :, :, HD]).then_inc(inv_done, 1)
                    dve.wait_ge(inv_done, u + 1)
                    dst = attn_tok[:, b, :, 32 * g:32 * g + 32].rearrange("p t (j d) -> p t j d", j=GROUP)
                    inv = sums_inv[:, :, :].unsqueeze(3).to_broadcast([P, 2, GROUP, HD])
                    dve.tensor_tensor(dst, got[:, :, :, 0:HD], inv, ALU.mult).then_inc(normalised, 1)

                for i in range(total + 1):
                    if i < total:
                        choose(i)
                    if i >= 1:
                        mask(i - 1)
                    if i < total:
                        bound(i)
                    if i % 8 == 5 and i > 12:
                        heads_to_tokens(i // 8 - 1)
                dve.wait_ge(masked, total)
                last = total - 1
                dve.tensor_tensor(weight[last % 3], weight[last % 3], kept[last % 4], ALU.mult).then_inc(last_done, 1)
                dve.tensor_reduce(most, counts.rearrange("p (u t) -> p u t", u=units), AX.X, ALU.max).then_inc(most_done, 1)
                dve.wait_ge(most_turned, 1)
                turned = ps[0:1, 0:2, :].rearrange("p a (u t) -> p (a u) t", u=4)
                dve.tensor_reduce(largest_count[:, 0:units], turned, AX.X, ALU.max).then_inc(most_done, 1)
                dve.wait_ge(most_done, 2)
                dve.tensor_reduce(largest_count[:, units:], largest_count[:, 0:units], AX.X, ALU.max).then_inc(most_done, 1)
                heads_to_tokens(units - 1)

            @block.scalar
            def _(act):
                def copy_turned(i):
                    rows, slot = tile_rows(12), probs_t[i % 2]
                    act.wait_ge(t_ready, 3 * i + 1)
                    if i >= 2:
                        act.wait_ge(pv_done, i - 1)
                    act.copy(slot[:, 0:8, :], ps[:, 4:6, :].rearrange("p a (t q) -> p (a t) q", t=4)) \
                        .then_inc(t_copied, 1)
                    act.wait_ge(t_ready, 3 * i + 2)
                    act.copy(slot[:, 8:12, :], ps[:, 7, :].rearrange("p (t q) -> p t q", t=4)).then_inc(t_copied, 1)
                    act.wait_ge(t_ready, 3 * i + 3)
                    if i % 8 == 1 and i > 8:
                        copy_turned_heads(i // 8 - 1)
                    act.copy(slot[0:rows, 12, :], turned_at(12)[0:rows, :]).then_inc(t_copied, 1)

                def copy_turned_heads(u):
                    if u >= 1:
                        act.wait_ge(normalised, u)
                    act.copy(heads_tok, turned_heads).then_inc(o_turned, 1)

                def copy_heads(u):
                    act.wait_ge(pv_done, 8 * (u + 1))
                    if u >= 1:
                        act.wait_ge(o_turned, u)
                    act.copy(heads_out[:, :], ps[:, 6, 0:TOK]).then_inc(o_copied, 1)

                def keep(i):
                    act.wait_ge(s_ready, i + 1)
                    if i >= 4:
                        act.wait_ge(weight_done, i - 3)
                    act.copy(kept[i % 4], scores).then_inc(copied, 1)

                keep(0)
                for i in range(total + 2):
                    if i + 1 < total:
                        keep(i + 1)
                    if i >= 11 and i % 8 == 3 and i < total:
                        copy_heads(i // 8 - 1)
                    if i < total:
                        act.wait_ge(offset_done, i + 1)
                        act.wait_ge(copied, i + 1)
                        if i >= 3:
                            act.wait_ge(t_ready, 3 * (i - 2))
                        act.activation(weight[i % 3], kept[i % 4], ACT.Exp, bias=best[:, i % 2, TOPK:TOPK + 1],
                                       scale=SCALE).then_inc(e_done, 1)
                    if i >= 2:
                        copy_turned(i - 2)
                copy_heads(units - 1)
                act.wait_ge(t_ready, 3 * total + 1)
                copy_turned_heads(units - 1)
                act.wait_ge(all_turned, 1)
                act.activation(attn[:, :], ps[:, 7, :], ACT.Identity, bias=v_bias).then_inc(o_copied, 1)

            @block.gpsimd
            def _(pool):
                for i in range(total - 1):
                    pool.wait_ge(masked, i + 1)
                    pool.wait_ge(e_done, i + 1)
                    pool.tensor_tensor(weight[i % 3], weight[i % 3], kept[i % 4], ALU.mult).then_inc(weight_done, 1)

    def exact_top_attention(u, any_reached, v_bias):
        s, other = semaphores()
        terms, copies = s.take(), s.take()
        (s_ready, top8, offset_done, taken8, top16, taken16, e_done, rest_done, weight_done, t_ready, t_copied,
         pv_done, o_copied, o_turned, inv_done, normalised, all_turned) = [s.take() for _ in range(17)]
        b, g, total = u // GROUPS, u % GROUPS, 8

        def unit_reached(engine):
            return engine.value_load(largest_count[:, u:u + 1], min_val=0, max_val=CTX)

        def turned_at(t):
            return ps[:, (4, 5, 7, 4)[t // 4], (t % 4) * P:(t % 4 + 1) * P]

        turned_heads = ps[:, 4, TOK:2 * TOK]
        scores = ps[:, 0:4, :].rearrange("p a b -> p (a b)")[:, 0:CTX]

        def load(sp):
            for i in range(3):
                sp.dma_start(k_stack[0][8 * i:8 * i + 8, :, :],
                             k_parts[32 * g:32 * g + 32, i, b * CTX:(b + 1) * CTX]).then_inc(terms, 16)
            sp.wait_ge(terms, 48)
            for j in (1, 2):
                sp.dma_start(k_stack[0][24 * j:24 * j + 24, :, :], k_stack[0][0:24, :, :]).then_inc(copies, 16)

        def products(pe):
            pe.wait_ge(copies, 32)
            for i in range(total + 3):
                if i < total:
                    j, qt = i // 2, i % 2
                    if i >= 1:
                        pe.wait_ge(e_done, i)
                    for col in range(0, CTX, 512):
                        width = min(512, CTX - col)
                        mm = pe.matmul(ps[:, col // 512, 0:width],
                                       q_stack[0:SCORE_ROWS, 4 * g + j, b * TOK + qt * P:b * TOK + (qt + 1) * P],
                                       k_stack[0][0:SCORE_ROWS, j, col:col + width], start=True, stop=True)
                    mm.then_inc(s_ready, 1)
                if 2 <= i < total + 2:
                    pe.wait_ge(weight_done, i - 1)
                    if i >= 3:
                        pe.wait_ge(t_copied, 3 * (i - 2))
                    for t in range(12):
                        mm = pe.transpose(turned_at(t), weight_e[i % 2][:, t * P:(t + 1) * P], ident[:, :])
                        if t in (7, 11):
                            mm.then_inc(t_ready, 1)
                if i >= 3:
                    j, qt = (i - 3) // 2, (i - 3) % 2
                    pe.wait_ge(t_copied, 3 * (i - 2))
                    for t in range(CTX_TILES):
                        rows, head = tile_rows(t), 4 * g + j
                        mm = pe.matmul(ps[32 * j:32 * j + 32, 6, qt * P:(qt + 1) * P],
                                       values[0:rows, b * CTX_TILES + t, head * VH:head * VH + 32],
                                       probs_t[(i - 3) % 2][0:rows, t, :], start=(t == 0), stop=(t == CTX_TILES - 1))
                    mm.then_inc(pv_done, 1)
                if 2 <= i < total + 2:
                    pe.wait_ge(t_copied, 3 * (i - 2) + 1)
                    rows = tile_rows(12)
                    pe.transpose(turned_at(12)[0:rows, :], weight_e[i % 2][:, 12 * P:12 * P + rows], ident[:, :]) \
                        .then_inc(t_ready, 1)
            pe.wait_ge(o_copied, 1)
            for qt in range(2):
                mm = pe.transpose(turned_heads[:, qt * P:(qt + 1) * P], heads_out[:, qt * P:(qt + 1) * P], ident[:, :])
            mm.then_inc(o_turned, 1)
            pe.wait_ge(normalised, 1)
            for i in range(2 * PAIR):
                mm = pe.transpose(ps[:, 7, i * P:(i + 1) * P], attn_tok[:, i // 2, i % 2, :], ident[:, :])
            mm.then_inc(all_turned, 1)

        def sixteen_best(dve):
            for i in range(total):
                top, left = best[:, i % 2, :], untaken[i % 2]
                dve.wait_ge(s_ready, i + 1)
                if i >= 2:
                    dve.wait_ge(e_done, i - 1)
                    dve.wait_ge(rest_done, i - 1)
                dve.max(top[:, 0:8], scores).then_inc(top8, 1)
                if i >= 2:
                    dve.wait_ge(weight_done, i - 1)
                dve.wait_ge(top8, i + 1)
                dve.match_replace(left, top[:, 0:8], scores, LOW).then_inc(taken8, 1)
                dve.tensor_scalar(top[:, TOPK:TOPK + 1], top[:, 0:1], -SCALE, None, ALU.mult).then_inc(offset_done, 1)
                dve.wait_ge(taken8, i + 1)
                dve.max(top[:, 8:16], left).then_inc(top16, 1)
                dve.wait_ge(top16, i + 1)
                dve.match_replace(left, top[:, 8:16], left, LOW).then_inc(taken16, 1)
            dve.wait_ge(o_turned, 1)
            got = turned_heads.rearrange("p (t j c) -> p t j c", t=2, j=GROUP)
            dve.reciprocal(sums_inv[:, :, :], got[:, :, :, HD]).then_inc(inv_done, 1)
            dve.wait_ge(inv_done, 1)
            dst = attn_tok[:, b, :, 32 * g:32 * g + 32].rearrange("p t (j d) -> p t j d", j=GROUP)
            inv = sums_inv[:, :, :].unsqueeze(3).to_broadcast([P, 2, GROUP, HD])
            dve.tensor_tensor(dst, got[:, :, :, 0:HD], inv, ALU.mult).then_inc(normalised, 1)

        def exponentials(act):
            for i in range(total + 1):
                if i < total:
                    top, left = best[:, i % 2, :], untaken[i % 2]
                    act.wait_ge(taken8, i + 1)
                    act.wait_ge(offset_done, i + 1)
                    if i >= 2:
                        act.wait_ge(t_ready, 3 * (i - 1))
                    act.activation(weight_e[i % 2], scores, ACT.Exp, bias=top[:, TOPK:TOPK + 1], scale=SCALE) \
                        .then_inc(e_done, 1)
                    act.wait_ge(taken16, i + 1)
                    act.activation(left, left, ACT.Exp, bias=top[:, TOPK:TOPK + 1], scale=SCALE).then_inc(rest_done, 1)
                if i >= 1:
                    rows, slot = tile_rows(12), probs_t[(i - 1) % 2]
                    act.wait_ge(t_ready, 3 * i - 2)
                    if i >= 3:
                        act.wait_ge(pv_done, i - 2)
                    act.copy(slot[:, 0:8, :], ps[:, 4:6, :].rearrange("p a (t q) -> p (a t) q", t=4)) \
                        .then_inc(t_copied, 1)
                    act.wait_ge(t_ready, 3 * i - 1)
                    act.copy(slot[:, 8:12, :], ps[:, 7, :].rearrange("p (t q) -> p t q", t=4)).then_inc(t_copied, 1)
                    act.wait_ge(t_ready, 3 * i)
                    act.copy(slot[0:rows, 12, :], turned_at(12)[0:rows, :]).then_inc(t_copied, 1)
            act.wait_ge(pv_done, total)
            act.copy(heads_out[:, :], ps[:, 6, 0:TOK]).then_inc(o_copied, 1)
            act.wait_ge(all_turned, 1)
            act.activation(attn[:, :], ps[:, 7, :], ACT.Identity, bias=v_bias).then_inc(o_copied, 1)

        def differences(pool):
            for i in range(total):
                pool.wait_ge(rest_done, i + 1)
                pool.wait_ge(e_done, i + 1)
                pool.tensor_tensor(weight_e[i % 2], weight_e[i % 2], untaken[i % 2], ALU.subtract) \
                    .then_inc(weight_done, 1)

        with nc.Block() as block:
            @block.sync
            def _(sp):
                sp.sem_clear(other)
                with sp.If(any_reached > TOPK):
                    with sp.If(unit_reached(sp) > TOPK):
                        load(sp)

            @block.tensor
            def _(pe):
                with pe.If(any_reached > TOPK):
                    with pe.If(unit_reached(pe) > TOPK):
                        products(pe)

            @block.vector
            def _(dve):
                with dve.If(any_reached > TOPK):
                    with dve.If(unit_reached(dve) > TOPK):
                        sixteen_best(dve)

            @block.scalar
            def _(act):
                with act.If(any_reached > TOPK):
                    with act.If(unit_reached(act) > TOPK):
                        exponentials(act)

            @block.gpsimd
            def _(pool):
                with pool.If(any_reached > TOPK):
                    with pool.If(unit_reached(pool) > TOPK):
                        differences(pool)

    def project_prototypes():
        q_job, qk_job = 0, 5
        jobs = [([(ctx[:, b, t * P:t * P + tile_rows(t)], w("0v"))], v0[0:tile_rows(t), b * CTX_TILES + t, 0:D])
                for b in range(PAIR) for t in range(CTX_TILES)]
        jobs.insert(q_job, ([(w("0q"), normed[:, :])], tmp_a[:, :]))
        jobs.insert(qk_job, ([(w("0kT"), tmp_a[:, :])], tmp_b[:, :]))
        s, other = semaphores()
        product_ready, act_emptied, dve_emptied = s.take(), s.take(), s.take()
        with nc.Block() as block:
            @block.sync
            def _(sp):
                sp.sem_clear(other)

            @block.tensor
            def _(pe):
                pe.wait_ge(weights_loaded, 16)
                pe.wait_ge(ctx_loaded, 16)
                for i, (terms, dst) in enumerate(jobs):
                    if i >= 4:
                        pe.wait_ge(act_emptied if i % 2 == 0 else dve_emptied, (i - 4) // 2 + 1)
                    if i == qk_job:
                        pe.wait_ge(act_emptied, q_job // 2 + 1)
                    lhs, rhs = terms[0]
                    pe.matmul(ps[0:dst.shape[0], i % 4, 0:dst.shape[1]], lhs, rhs, start=True, stop=True) \
                        .then_inc(product_ready, 1)

            @block.scalar
            def _(act):
                for i, (terms, dst) in enumerate(jobs):
                    if i % 2 == 0:
                        act.wait_ge(product_ready, i + 1)
                        act.copy(dst, ps[0:dst.shape[0], i % 4, 0:dst.shape[1]]).then_inc(act_emptied, 1)

            @block.vector
            def _(dve):
                for i, (terms, dst) in enumerate(jobs):
                    if i % 2 == 1:
                        dve.wait_ge(product_ready, i + 1)
                        dve.tensor_copy(dst, ps[0:dst.shape[0], i % 4, 0:dst.shape[1]]).then_inc(dve_emptied, 1)

    def prototype_attention():
        s, other = semaphores()
        (a_ready, max_done, small, neg_ready, neg_turned, row_ready, st_ready, exp_done, pv_done, inverted,
         normalised, o_turned, ones_set, attn_done) = [s.take() for _ in range(14)]
        scale0 = float(D) ** -0.5
        tiles = CTX_TILES
        parts = neg_parts[:, 0, :, :, :].rearrange("p a b c -> p (a b c)")[:, 0:12].rearrange("p (i k) -> p i k", k=3)
        with nc.Block() as block:
            @block.sync
            def _(sp):
                sp.sem_clear(other)

            @block.tensor
            def _(pe):
                for b in range(PAIR):
                    for r in range(4):
                        n = b * 4 + r
                        qt, half = r // 2, r % 2
                        bank = 2 * (n % 2)
                        if n >= 2:
                            pe.wait_ge(max_done, n - 1)
                        for col in range(0, HALF - half, 512):
                            width = min(512, HALF - half - col)
                            mm = pe.matmul(ps[:, bank + col // 512, 0:width],
                                           tmp_b[:, b * TOK + qt * P:b * TOK + (qt + 1) * P],
                                           ctx[:, b, half * HALF + col:half * HALF + col + width], start=True, stop=True)
                        mm.then_inc(a_ready, 1)
                pe.wait_ge(neg_ready, 1)
                for i in range(4):
                    mm = pe.transpose(ps[0:3, 4, i * P // 2:(i + 1) * P // 2].bitcast(BF16), parts[:, i, :], ident16[:, :])
                mm.then_inc(neg_turned, 1)
                pe.wait_ge(row_ready, 1)
                pe.wait_ge(ones_set, 1)
                for n in range(PAIR * tiles + 1):
                    if n < PAIR * tiles:
                        b, t = n // tiles, n % tiles
                        rows = tile_rows(t)
                        if n >= 2:
                            pe.wait_ge(exp_done, n - 1)
                        st = ps[0:rows, n % 2, 0:TOK]
                        pe.matmul(st, ctx[:, b, t * P:t * P + rows], tmp_b[:, b * TOK:(b + 1) * TOK],
                                  start=True, stop=False)
                        pe.matmul(st, ones16[:, 0:rows], neg_row0[:, b * TOK:(b + 1) * TOK],
                                  start=False, stop=True).then_inc(st_ready, 1)
                    if n >= 1:
                        m = n - 1
                        b, t = m // tiles, m % tiles
                        rows = tile_rows(t)
                        pe.wait_ge(exp_done, n)
                        for qt in range(2):
                            mm = pe.matmul(ps[:, 4 + 2 * b + qt, 0:D + 1], probs0[m % 3][0:rows, qt * P:(qt + 1) * P],
                                           v0[0:rows, m, :], start=(t == 0), stop=(t == tiles - 1))
                        mm.then_inc(pv_done, 1)
                for b in range(PAIR):
                    pe.wait_ge(normalised, 2 * (b + 1))
                    for qt in range(2):
                        mm = pe.transpose(ps[:, 2 + b, qt * P:(qt + 1) * P], attn_tok[:, b, qt, :], ident[:, :])
                    mm.then_inc(o_turned, 1)

            @block.vector
            def _(dve):
                dve.memset(v0[:, :, D:D + 1], 1.0).then_inc(ones_set, 1)
                for n in range(PAIR * 4):
                    bank = 2 * (n % 2)
                    dve.wait_ge(a_ready, n + 1)
                    src = ps[:, bank:bank + 2, :].rearrange("p a b -> p (a b)")[:, 0:HALF - n % 2]
                    dve.tensor_reduce(maxima[:, 0, n:n + 1], src, AX.X, ALU.max).then_inc(max_done, 1)
                dve.wait_ge(max_done, 8)
                m, rest = max8[:, 0:4], neg_f[:, 0:4]
                dve.tensor_reduce(m, maxima[:, 0, 0:8].rearrange("p (r h) -> p r h", h=2), AX.X, ALU.max) \
                    .then_inc(small, 1)
                dve.wait_ge(small, 1)
                dve.tensor_scalar(parts[:, :, 0], m, -1.0, None, ALU.mult).then_inc(small, 1)
                dve.wait_ge(small, 2)
                dve.scalar_tensor_tensor(rest, m, -1.0, parts[:, :, 0], ALU.mult, ALU.subtract).then_inc(small, 1)
                dve.wait_ge(small, 3)
                dve.tensor_copy(parts[:, :, 1], rest).then_inc(small, 1)
                dve.wait_ge(small, 4)
                dve.tensor_tensor(parts[:, :, 2], rest, parts[:, :, 1], ALU.subtract).then_inc(neg_ready, 1)
                dve.wait_ge(neg_turned, 1)
                dve.tensor_copy(neg_row0, ps[0:3, 4, 0:N // 2].bitcast(BF16)).then_inc(row_ready, 1)
                for b in range(PAIR):
                    dve.wait_ge(pv_done, (b + 1) * tiles)
                    for qt in range(2):
                        i, got = 2 * b + qt, ps[:, 4 + 2 * b + qt, :]
                        dve.reciprocal(sums_inv[:, 0, i:i + 1], got[:, D:D + 1]).then_inc(inverted, 1)
                        dve.wait_ge(inverted, i + 1)
                        dve.tensor_scalar(attn_tok[:, b, qt, :], got[:, 0:D], sums_inv[:, 0, i:i + 1], None, ALU.mult) \
                            .then_inc(normalised, 1)

            @block.scalar
            def _(act):
                for n in range(PAIR * tiles):
                    rows = tile_rows(n % tiles)
                    act.wait_ge(st_ready, n + 1)
                    if n >= 3:
                        act.wait_ge(pv_done, n - 2)
                    act.activation(probs0[n % 3][0:rows, :], ps[0:rows, n % 2, 0:TOK], ACT.Exp, scale=scale0) \
                        .then_inc(exp_done, 1)
                for b in range(PAIR):
                    act.wait_ge(o_turned, b + 1)
                    act.copy(attn[:, b * TOK:(b + 1) * TOK], ps[:, 2 + b, 0:TOK]).then_inc(attn_done, 1)

    def route_and_expand():
        s, other = semaphores()
        logits_ready, biased, step, exp_done, product_ready, emptied = [s.take() for _ in range(6)]
        at = W.at["0router"][0]
        with nc.Block() as block:
            @block.sync
            def _(sp):
                sp.sem_clear(other)

            @block.tensor
            def _(pe):
                for e in range(3):
                    pe.matmul(ps[:, e, :], weights[:, at + e:at + e + 1].to_broadcast([P, P]), normed[:, :],
                              start=True, stop=False)
                    pe.matmul(ps[:, e, :], weights[:, at + 3 + e:at + 4 + e].to_broadcast([P, P]), attn[:, :],
                              start=False, stop=True).then_inc(logits_ready, 1)
                for i in range(7):
                    if i >= 4:
                        pe.wait_ge(emptied, 2 * (i - 3))
                    for k, rhs in enumerate((normed[:, :], attn[:, :])):
                        lhs = w("0gate1", k) if i == 6 else w("0e1", (i // 2) * 4 + k * 2 + i % 2)
                        mm = pe.matmul(ps[:, 3 + i % 4, :], lhs, rhs, start=(k == 0), stop=(k == 1))
                    mm.then_inc(product_ready, 1)

            @block.vector
            def _(dve):
                for e in range(3):
                    dve.wait_ge(logits_ready, e + 1)
                    for b in range(PAIR):
                        cols = slice(b * TOK, (b + 1) * TOK)
                        dve.tensor_scalar(router_p[:, e, cols], ps[:, e, cols], modc("0router", b, e), None, ALU.add) \
                            .then_inc(biased, 1)
                dve.wait_ge(biased, 6)
                dve.tensor_tensor(tmp_a[:, :], router_p[:, 0, :], router_p[:, 1, :], ALU.max).then_inc(step, 1)
                dve.wait_ge(step, 1)
                dve.tensor_tensor(tmp_a[:, :], tmp_a[:, :], router_p[:, 2, :], ALU.max).then_inc(step, 1)
                dve.wait_ge(step, 2)
                for e in range(3):
                    dve.tensor_tensor(router_p[:, e, :], router_p[:, e, :], tmp_a[:, :], ALU.subtract).then_inc(step, 1)
                dve.wait_ge(exp_done, 3)
                dve.tensor_tensor(tmp_b[:, :], router_p[:, 0, :], router_p[:, 1, :], ALU.add).then_inc(step, 1)
                dve.wait_ge(step, 6)
                dve.tensor_tensor(tmp_b[:, :], tmp_b[:, :], router_p[:, 2, :], ALU.add).then_inc(step, 1)
                dve.wait_ge(step, 7)
                dve.reciprocal(tmp_a[:, :], tmp_b[:, :]).then_inc(step, 1)
                dve.wait_ge(step, 8)
                for e in range(3):
                    dve.tensor_tensor(router_p[:, e, :], router_p[:, e, :], tmp_a[:, :], ALU.mult).then_inc(step, 1)

            @block.scalar
            def _(act):
                for i in range(7):
                    if i == 2:
                        for e in range(3):
                            act.wait_ge(step, 3 + e)
                            act.activation(router_p[:, e, :], router_p[:, e, :], ACT.Exp).then_inc(exp_done, 1)
                    act.wait_ge(product_ready, i + 1)
                    for b in range(PAIR):
                        cols = slice(b * TOK, (b + 1) * TOK)
                        col = modc("0gate1", b) if i == 6 else modc("0e1", b, i)
                        act.activation(hidden[:, i, cols], ps[:, 3 + i % 4, cols], ACT.Silu, bias=col) \
                            .then_inc(emptied, 1)

    def mix_experts(norm_next):
        s, other = semaphores()
        product_ready, gate_done, weighed, mixed, out_ready, gated, added = [s.take() for _ in range(7)]
        norm = Norm(s, *norm_next)
        with nc.Block() as block:
            @block.sync
            def _(sp):
                sp.sem_clear(other)

            @block.tensor
            def _(pe):
                for e in range(3):
                    for k in range(2):
                        mm = pe.matmul(ps[:, e, :], w("0e2", 2 * e + k), hidden[:, 2 * e + k, :], start=(k == 0), stop=(k == 1))
                    mm.then_inc(product_ready, 1)
                pe.matmul(ps[:, 3, :], w("0gate2"), hidden[:, 6, :], start=True, stop=True).then_inc(product_ready, 1)
                pe.wait_ge(mixed, 2)
                pe.matmul(ps[:, 4, :], w("0out"), tmp_a[:, :], start=True, stop=True).then_inc(out_ready, 1)
                pe.wait_ge(added, 1)
                norm.tensor(pe)

            @block.scalar
            def _(act):
                act.wait_ge(product_ready, 4)
                act.activation(tmp_b[:, :], ps[:, 3, :], ACT.Sigmoid, bias=bias("0gate2")).then_inc(gate_done, 1)
                norm.scalar(act)

            @block.vector
            def _(dve):
                for e in range(3):
                    dve.wait_ge(product_ready, e + 1)
                    dst = tmp_a[:, :] if e == 0 else router_p[:, e, :]
                    dve.scalar_tensor_tensor(dst, ps[:, e, :], bias("0e2", e), router_p[:, e, :], ALU.add, ALU.mult) \
                        .then_inc(weighed, 1)
                for e in (1, 2):
                    dve.wait_ge(weighed, e + 1)
                    if e == 2:
                        dve.wait_ge(mixed, 1)
                    dve.tensor_tensor(tmp_a[:, :], tmp_a[:, :], router_p[:, e, :], ALU.add).then_inc(mixed, 1)
                dve.wait_ge(out_ready, 1)
                dve.wait_ge(gate_done, 1)
                dve.scalar_tensor_tensor(tmp_b[:, :], ps[:, 4, :], bias("0out"), tmp_b[:, :], ALU.add, ALU.mult) \
                    .then_inc(gated, 1)
                dve.wait_ge(gated, 1)
                dve.tensor_tensor(x[:, :], x[:, :], tmp_b[:, :], ALU.add).then_inc(added, 1)
                norm.vector(dve)

    ctx_flat = ctx[:, :, :].rearrange("p b n -> p (b n)")

    def self_jobs(src, layer, rope=False):
        jobs = []
        for n, dst in (("sq", q_parts[:, :, :]), ("sk", k_parts[:, :, 0:N])):
            if rope:
                for b in range(PAIR):
                    cols = slice(b * TOK, (b + 1) * TOK)
                    jobs.append((src[:, cols], w(f"{layer}{n}"), w(f"{layer}{n}r"), None,
                                 rope_tok[:, 0, :], rope_tok[:, 1, :], dst[:, :, cols]))
            else:
                jobs.append((src, w(f"{layer}{n}"), None, bias(f"{layer}{n}"), None, None, dst))
        values_ = [[(src[:, i * P:(i + 1) * P], i) for i in range(4)]]
        return jobs, values_

    def cross_jobs(src, layer, rope=False):
        if rope:
            jobs = [(src[:, b * TOK:(b + 1) * TOK], w(f"{layer}cq"), w(f"{layer}cqr"), None, rope_tok[:, 0, :],
                     rope_tok[:, 1, :], q_parts[:, :, b * TOK:(b + 1) * TOK]) for b in range(PAIR)]
        else:
            jobs = [(src, w(f"{layer}cq"), None, bias(f"{layer}cq"), None, None, q_parts[:, :, :])]
        for b in range(PAIR):
            for c in range(0, CTX, 512):
                n = min(512, CTX - c)
                dst = k_parts[:, :, b * CTX + c:b * CTX + c + n]
                if rope:
                    jobs.append((ctx[:, b, c:c + n], w(f"{layer}ck"), w(f"{layer}ckr"), None,
                                 rope_ctx[:, 0, c:c + n], rope_ctx[:, 1, c:c + n], dst))
                else:
                    jobs.append((ctx[:, b, c:c + n], w(f"{layer}ck"), None, bias(f"{layer}ck"), None, None, dst))
        groups = []
        for b in range(PAIR):
            for first in range(0, CTX_TILES, 4):
                groups.append([(ctx[:, b, t * P:t * P + tile_rows(t)], b * CTX_TILES + t)
                               for t in range(first, min(first + 4, CTX_TILES))])
        return jobs, groups

    eps5, eps6 = sb("eps5", [P, 1]), sb("eps6", [P, 1])
    eps_col = {1e-5: eps5[:, :], 1e-6: eps6[:, :]}

    nc.vector.memset(eps5[:, :], 1e-5)
    nc.vector.memset(eps6[:, :], 1e-6)
    load_constants()
    with nc.Fori(0, BATCHES // PAIR) as pair:
        first_turn = turn[0]
        load_pair(pair, (1e-5, lambda b: (bias("0g"), bias("0b"))))
        project_prototypes()
        prototype_attention()
        route_and_expand()
        mix_experts((1e-5, lambda b: (lnw[:, 0, b, 0:1], lnw[:, 0, b, 1:2])))
        if last_stage >= 1:
            project_heads(*self_jobs(normed[:, :], 1), w("1sv"), None)
            attention("self", bias("1sv"))
            add_to_x([(w("1so"), attn[:, :])], bias("1so"), after_attention=True)
        if last_stage >= 2:
            project_heads(*cross_jobs(x[:, :], 1), w("1cv"), 4)
            attention("cross", bias("1cv"))
            add_to_x([(w("1co"), attn[:, :])], bias("1co"), after_attention=True,
                     norm_next=(1e-5, lambda b: (lnw[:, 1, b, 0:1], lnw[:, 1, b, 1:2])))
        if last_stage >= 3:
            feed_forward(1, norm_next=(1e-5, lambda b: (modc("2ln1", b, 0), modc("2ln1", b, 1))))
        if last_stage >= 4:
            project_heads(*self_jobs(normed[:, :], 2, rope=True), w("2sv"), None, rope=True)
            attention("self", None)
            add_to_x([(w("2so"), attn[:, :])], None, after_attention=True,
                     norm_next=(1e-5, lambda b: (modc("2ln2", b, 0), modc("2ln2", b, 1))))
        if last_stage >= 5:
            project_heads(*cross_jobs(normed[:, :], 2, rope=True), w("2cv"), 4, rope=True, load_rope=True)
            attention("cross", None)
            add_to_x([(w("2co"), attn[:, :])], None, after_attention=True,
                     norm_next=(1e-5, lambda b: (modc("2ln3", b, 0), modc("2ln3", b, 1))))
            feed_forward(2, norm_next=(1e-6, lambda b: (modc("3ada", b, 1), modc("3ada", b, 0))))
        if last_stage >= 6:
            project_heads(*self_jobs(normed[:, :], 3), w("3sv"), None)
            attention("window", bias("3sv"))
            add_to_x([(w("3so"), attn[:, :])], bias("3so"), lambda b: modc("3ada", b, 2), after_attention=True,
                     norm_next=(1e-6, lambda b: (modc("3ada", b, 4), modc("3ada", b, 3))))
        if last_stage >= 7:
            project_heads(*cross_jobs(normed[:, :], 3), w("3cv"), 3)
            top_attention(bias("3cv"))
            any_reached = nc.values_load(largest_count[:, PAIR * GROUPS:], min_val=0, max_val=CTX)
            for u in range(PAIR * GROUPS):
                exact_top_attention(u, any_reached, bias("3cv"))
            add_to_x([(w("3co"), attn[:, :])], bias("3co"), lambda b: modc("3ada", b, 5), after_attention=True,
                     norm_next=(1e-6, lambda b: (modc("3ada", b, 7), modc("3ada", b, 6))))
        if last_stage >= 8:
            feed_forward(3, lambda b: modc("3ada", b, 8))
        store_pair(pair)
        even_out(first_turn)


def _rows(a, k):
    a = np.asarray(a)
    return a.reshape(k, D, -1).transpose(1, 0, 2).reshape(D, -1)


def heads(a, order, turned=False):
    d = (order[:, 1] + turned * (HD // 2)) % HD
    return a[..., order[:, 0] * HD + d]


def pack(i):
    g = {k: np.asarray(v) for k, v in i.items()}
    L0, L1, L2, L3 = (lambda n, k=k: g[f"L{k}_xcond_{n}"] for k in range(4))
    e1 = L0("e_w1")
    blocks = {
        "0q": L0("Wq"), "0kT": L0("Wk").T, "0v": L0("Wv"), "0out": L0("out_w"), "0gate2": L0("gate_w2"),
        "0gate1": _rows(L0("gate_w1")[:2 * D], 2),
        "0e1": np.concatenate([_rows(e1[e, :2 * D], 2) for e in range(3)], 1),
        "0e2": np.concatenate([_rows(L0("e_w2")[e], 2) for e in range(3)], 1),
        "0router": _rows(L0("router_W")[:2 * D], 2),
        "1sq": heads(L1("sa_qw"), BY_DIM), "1sk": heads(L1("sa_kw"), BY_DIM), "1sv": L1("sa_vw"), "1so": L1("sa_ow"),
        "1cq": heads(L1("ca_qw"), BY_DIM), "1ck": heads(L1("ca_kw"), BY_GROUP), "1cv": L1("ca_vw"), "1co": L1("ca_ow"),
        "1f1": L1("ffn_w1"), "1f2": _rows(L1("ffn_w2"), 4),
        "2sq": heads(L2("qkv_w")[:D].T, BY_DIM), "2sqr": heads(L2("qkv_w")[:D].T, BY_DIM, True),
        "2sk": heads(L2("qkv_w")[D:2 * D].T, BY_DIM), "2skr": heads(L2("qkv_w")[D:2 * D].T, BY_DIM, True),
        "2sv": L2("qkv_w")[2 * D:].T, "2so": L2("sa_out_w").T,
        "2cq": heads(L2("q_w").T, BY_DIM), "2cqr": heads(L2("q_w").T, BY_DIM, True),
        "2ck": heads(L2("k_w").T, BY_GROUP), "2ckr": heads(L2("k_w").T, BY_GROUP, True),
        "2cv": L2("v_w").T, "2co": L2("ca_out_w").T, "2f1": L2("ffn_w1").T, "2f2": _rows(L2("ffn_w2").T, 4),
        "3sq": heads(L3("w_qkv")[:, :D], BY_DIM), "3sk": heads(L3("w_qkv")[:, D:2 * D], BY_DIM), "3sv": L3("w_qkv")[:, 2 * D:],
        "3so": L3("w_so"), "3cq": heads(L3("w_q"), BY_DIM), "3ck": heads(L3("w_kv")[:, :D], BY_GROUP), "3cv": L3("w_kv")[:, D:],
        "3co": L3("w_co"), "3f1": L3("w_m1"), "3f2": _rows(L3("w_m2"), 4),
    }
    W, M, B = weight_plan(), modulation_plan(), bias_plan()
    weights = np.concatenate([blocks[n] for n in W.at], 1)
    cond_blocks = {
        "0gate1": L0("gate_w1")[2 * D:], "0e1": np.concatenate([e1[e, 2 * D:] for e in range(3)], 1),
        "1aff1": L1("aff1_w"), "1aff2": L1("aff2_w"), "2ln1": L2("ln1_w").T, "2ln2": L2("ln2_w").T,
        "2ln3": L2("ln3_w").T, "3ada": L3("w_ada"), "0router": L0("router_W")[2 * D:],
    }
    modw = np.concatenate([cond_blocks[n] for n in M.at], 1)

    def cols(v):
        return np.asarray(v).reshape(-1, D).T

    mod_bias = {
        "0gate1": cols(L0("gate_b1")), "0e1": cols(L0("e_b1")), "1aff1": cols(L1("aff1_b")), "1aff2": cols(L1("aff2_b")),
        "2ln1": cols(L2("ln1_b")), "2ln2": cols(L2("ln2_b")), "2ln3": cols(L2("ln3_b")), "3ada": cols(L3("b_ada")),
        "0router": np.broadcast_to(L0("router_b"), (D, 3)),
    }
    qkv_b, kv_b = L3("b_qkv"), L3("b_kv")
    bias_blocks = {
        "mod": np.concatenate([mod_bias[n] for n in M.at], 1),
        "0g": cols(L0("ln_gamma")), "0b": cols(L0("ln_beta")), "0gate2": cols(L0("gate_b2")), "0out": cols(L0("out_b")),
        "0e2": cols(L0("e_b2")), "1g1": cols(L1("ln1_g")), "1b1": cols(L1("ln1_b")), "1g2": cols(L1("ln2_g")),
        "1b2": cols(L1("ln2_b")), "1sq": cols(heads(L1("sa_qb"), BY_DIM)), "1sk": cols(heads(L1("sa_kb"), BY_DIM)),
        "1sv": cols(L1("sa_vb")), "1so": cols(L1("sa_ob")), "1cq": cols(heads(L1("ca_qb"), BY_DIM)),
        "1ck": cols(heads(L1("ca_kb"), BY_GROUP)), "1cv": cols(L1("ca_vb")), "1co": cols(L1("ca_ob")), "1f1": cols(L1("ffn_b1")),
        "1f2": cols(L1("ffn_b2")), "2f1": cols(L2("ffn_b1")), "2f2": cols(L2("ffn_b2")),
        "3sq": cols(heads(qkv_b[:D], BY_DIM)), "3sk": cols(heads(qkv_b[D:2 * D], BY_DIM)), "3sv": cols(qkv_b[2 * D:]),
        "3so": cols(L3("b_so")), "3cq": cols(heads(L3("b_q"), BY_DIM)), "3ck": cols(heads(kv_b[:D], BY_GROUP)), "3cv": cols(kv_b[D:]),
        "3co": cols(L3("b_co")), "3f1": cols(L3("b_m1")), "3f2": cols(L3("b_m2")),
    }
    biases = np.concatenate([bias_blocks[n] for n in B.at], 1)

    half = HD // 2
    inv_freq = (np.float32(1.0) / np.float32(10000.0) ** (np.arange(half, dtype=np.float32) / np.float32(half)))

    def tables(order, positions):
        d = order[:, 1]
        ang = positions.astype(np.float32)[None, :] * inv_freq.astype(np.float32)[d % half][:, None]
        sign = np.where(d < half, -1.0, 1.0)[:, None]
        return np.concatenate([np.cos(ang.astype(np.float64)), np.sin(ang.astype(np.float64)) * sign], 1) \
            .astype(np.float32)

    rope = tables(BY_GROUP, np.arange(CTX))
    const = np.concatenate([np.eye(P, dtype=np.float32), tables(BY_DIM, np.roll(np.arange(TOK), -SHIFT))], 1)

    pairs = BATCHES // PAIR
    x = np.roll(g["x"], -SHIFT, axis=1).reshape(pairs, N, D).transpose(0, 2, 1)
    ctx = g["ctx_1024"].reshape(pairs, PAIR * CTX, D).transpose(0, 2, 1)
    return {"x": x, "ctx": ctx, "cond": g["cond_1024"].T, "weights": weights, "modw": modw, "biases": biases,
            "const": const, "rope": rope}


def kernel(**inputs):
    import concourse.bacc as bacc
    from concourse.bass_utils import run_bass_kernel_spmd

    nc = bacc.Bacc("TRN2", target_bir_lowering=False, num_devices=1)
    arrays = {f"in_{k}": np.ascontiguousarray(v) for k, v in pack(inputs).items()}
    args = [nc.dram_tensor(k, v.shape, F32, kind="ExternalInput").ap() for k, v in arrays.items()]
    out = nc.dram_tensor("out_0", (BATCHES // PAIR, D, N), F32, kind="ExternalOutput").ap()
    build_program(nc, *args, out)
    r = run_bass_kernel_spmd(nc, [arrays], core_ids=[0])
    got = np.asarray(r.results[0]["out_0"])
    return np.roll(got.transpose(0, 2, 1).reshape(BATCHES, TOK, D), SHIFT, axis=1)
```
